# Optimizing a Trainium2 kernel written in Bass

```python
import numpy as np
import jax
import jax.numpy as jnp

def _softmax(x, axis=-1):
    return jax.nn.softmax(x, axis=axis)

def _gelu(x):
    return jax.nn.gelu(x, approximate=True)

def _silu(x):
    return jax.nn.silu(x)

def _sigmoid(x):
    return jax.nn.sigmoid(x)

def _layernorm(x, axis=-1, eps=1e-05):
    m = jnp.mean(x, axis=axis, keepdims=True)
    v = jnp.var(x, axis=axis, keepdims=True)
    return (x - m) / jnp.sqrt(v + eps)

def _scatter_add(tgt, idx, src, axis=0):
    return tgt.at[idx].add(src)

def _segment_sum(src, seg, n):
    return jax.ops.segment_sum(src, seg, n)
kernel_name = 'mk_gnn_ffn_d2_gnn_r8_62f190'

def setup_inputs(seed: int=0):
    np.random.seed(seed)
    _w = jnp.asarray

    def _rec_inputs():
        import jax
        import jax.numpy as jnp
        _gk = jax.random.key(seed)
        x = -0.0003713 + 1 * jax.random.normal(jax.random.fold_in(_gk, 1), (6250, 256), jnp.float32)
        src = jax.random.randint(jax.random.fold_in(_gk, 2), (100000,), 0, 6250, jnp.int32)
        dst = jnp.minimum((6250 * jax.random.uniform(jax.random.fold_in(_gk, 3), (100000,)) ** 2.0).astype(jnp.int32), 49999)
        _o = jnp.argsort(dst, stable=True)
        src = src[_o]
        dst = dst[_o]
        edge_attr_256 = 9.41057e-06 + 1 * jax.random.normal(jax.random.fold_in(_gk, 11), (100000, 256), jnp.float32)
        return (x, src, dst, edge_attr_256)
    x, src, dst, edge_attr_256 = _rec_inputs()

    def _L0_gnn_setup():
        import jax, jax.numpy as jnp
        import numpy as np
        N, E, DIN, HID, HEADS = (6250, 200000, 256, 256, 4)
        C = HID // 2 // HEADS
        NEG_SLOPE = 0.2
        BN_EPS = 1e-05

        def _gat(x, W, a_src, a_dst, b, src, dst):
            xl = (x @ W).reshape(N, HEADS, C)
            al = jnp.einsum('nhc,hc->nh', xl, a_src)
            ar = jnp.einsum('nhc,hc->nh', xl, a_dst)
            e = jax.nn.leaky_relu(al[src] + ar[dst], NEG_SLOPE)
            m = jax.ops.segment_max(e, dst, num_segments=N)
            w = jnp.exp(e - m[dst])
            den = jax.ops.segment_sum(w, dst, num_segments=N)
            alpha = w / (den[dst] + 1e-16)
            msg = xl[src] * alpha[..., None]
            out = jax.ops.segment_sum(msg, dst, num_segments=N)
            return out.reshape(N, HEADS * C) + b
        key = jax.random.key(seed)
        ks = jax.random.split(key, 16)
        s = lambda k, shp: jax.random.normal(k, shp, jnp.float32) * 0.05
        return {'x': jax.random.normal(ks[0], (N, DIN), jnp.float32), 'edge_index': jax.random.randint(ks[1], (2, E), 0, N, jnp.int32), 'W_f': s(ks[2], (DIN, HEADS * C)), 'a_src_f': s(ks[3], (HEADS, C)), 'a_dst_f': s(ks[4], (HEADS, C)), 'b_f': jnp.zeros((HEADS * C,), jnp.float32), 'W_b': s(ks[5], (DIN, HEADS * C)), 'a_src_b': s(ks[6], (HEADS, C)), 'a_dst_b': s(ks[7], (HEADS, C)), 'b_b': jnp.zeros((HEADS * C,), jnp.float32), 'W_fuse': s(ks[8], (HID, HID)), 'b_fuse': jnp.zeros((HID,), jnp.float32), 'gamma': jnp.ones((HID,), jnp.float32), 'beta': jnp.zeros((HID,), jnp.float32), 'run_mean': jnp.zeros((HID,), jnp.float32), 'run_var': jnp.ones((HID,), jnp.float32)}
    _L0_gnn_all = _L0_gnn_setup()
    _L0_gnn_in = {k: v for k, v in _L0_gnn_all.items() if k in ('W_f', 'a_src_f', 'a_dst_f', 'b_f', 'W_b', 'a_src_b', 'a_dst_b', 'b_b', 'W_fuse', 'b_fuse', 'gamma', 'beta', 'run_mean', 'run_var')}
    del _L0_gnn_all

    def _L0_ffn_setup():
        import jax, jax.numpy as jnp
        import numpy as np
        B, S, D, E, H, K = (4, 512, 256, 8, 512, 2)
        key = jax.random.key(seed)
        ks = jax.random.split(key, 6)
        x = jax.random.normal(ks[0], (B, S, D), jnp.float32)
        Wg = jax.random.normal(ks[1], (D, E), jnp.float32) * 0.02
        bg = jnp.zeros((E,), jnp.float32)
        W1 = jax.random.normal(ks[2], (E, D, H), jnp.float32) * 0.02
        b1 = jnp.zeros((E, H), jnp.float32)
        W2 = jax.random.normal(ks[3], (E, H, D), jnp.float32) * 0.02
        b2 = jnp.zeros((E, D), jnp.float32)
        return {'x': x, 'Wg': Wg, 'bg': bg, 'W1': W1, 'b1': b1, 'W2': W2, 'b2': b2}
    _L0_ffn_all = _L0_ffn_setup()
    _L0_ffn_in = {k: v for k, v in _L0_ffn_all.items() if k in ('Wg', 'bg', 'W1', 'b1', 'W2', 'b2')}
    del _L0_ffn_all

    def _L1_gnn_setup():
        import jax, jax.numpy as jnp
        import numpy as np
        N, E, NIN, H, C = (6250, 100000, 256, 8, 32)
        HC = H * C
        key = jax.random.key(seed)
        ks = jax.random.split(key, 12)
        s = 0.05
        x = jax.random.normal(ks[0], (N, NIN), dtype=jnp.float32)
        edge_index = jax.random.randint(ks[1], (2, E), 0, N, dtype=jnp.int64)
        edge_attr = jax.random.normal(ks[2], (E, NIN), dtype=jnp.float32)
        Wq = jax.random.normal(ks[3], (NIN, HC), dtype=jnp.float32) * s
        bq = jax.random.normal(ks[4], (HC,), dtype=jnp.float32) * s
        Wk = jax.random.normal(ks[5], (NIN, HC), dtype=jnp.float32) * s
        bk = jax.random.normal(ks[6], (HC,), dtype=jnp.float32) * s
        Wv = jax.random.normal(ks[7], (NIN, HC), dtype=jnp.float32) * s
        bv = jax.random.normal(ks[8], (HC,), dtype=jnp.float32) * s
        We = jax.random.normal(ks[9], (NIN, HC), dtype=jnp.float32) * s
        Ws = jax.random.normal(ks[10], (NIN, HC), dtype=jnp.float32) * s
        bs = jax.random.normal(ks[11], (HC,), dtype=jnp.float32) * s
        return {'x': x, 'edge_index': edge_index, 'edge_attr': edge_attr, 'Wq': Wq, 'bq': bq, 'Wk': Wk, 'bk': bk, 'Wv': Wv, 'bv': bv, 'We': We, 'Ws': Ws, 'bs': bs}
    _L1_gnn_all = _L1_gnn_setup()
    _L1_gnn_in = {k: v for k, v in _L1_gnn_all.items() if k in ('Wq', 'bq', 'Wk', 'bk', 'Wv', 'bv', 'We', 'Ws', 'bs')}
    del _L1_gnn_all

    def _L1_ffn_setup():
        import jax, jax.numpy as jnp
        import numpy as np
        DIM = 256
        H = 8
        D = 64
        G = 64
        INNER = H * D
        SCALE = D ** (-0.5)
        key = jax.random.key(seed)
        ks = jax.random.split(key, 12)
        B, N = (4, 2048)
        x = jax.random.normal(ks[0], (B, N, DIM), dtype=jnp.float32)
        s = lambda fan_in: 1.0 / np.sqrt(fan_in)
        W_fx = jax.random.normal(ks[1], (DIM, INNER), dtype=jnp.float32) * s(DIM)
        b_fx = jnp.zeros((INNER,), dtype=jnp.float32)
        W_x = jax.random.normal(ks[2], (DIM, INNER), dtype=jnp.float32) * s(DIM)
        b_x = jnp.zeros((INNER,), dtype=jnp.float32)
        A = jax.random.normal(ks[3], (G, D), dtype=jnp.float32)
        Q, _ = jnp.linalg.qr(A.T)
        W_slice = Q[:, :G].astype(jnp.float32)
        b_slice = jnp.zeros((G,), dtype=jnp.float32)
        W_q = jax.random.normal(ks[4], (D, D), dtype=jnp.float32) * s(D)
        W_k = jax.random.normal(ks[5], (D, D), dtype=jnp.float32) * s(D)
        W_v = jax.random.normal(ks[6], (D, D), dtype=jnp.float32) * s(D)
        W_out = jax.random.normal(ks[7], (INNER, DIM), dtype=jnp.float32) * s(INNER)
        b_out = jnp.zeros((DIM,), dtype=jnp.float32)
        temperature = jnp.ones((1, H, 1, 1), dtype=jnp.float32) * 0.5
        return {'x': x, 'W_fx': W_fx, 'b_fx': b_fx, 'W_x': W_x, 'b_x': b_x, 'W_slice': W_slice, 'b_slice': b_slice, 'W_q': W_q, 'W_k': W_k, 'W_v': W_v, 'W_out': W_out, 'b_out': b_out, 'temperature': temperature}
    _L1_ffn_all = _L1_ffn_setup()
    _L1_ffn_in = {k: v for k, v in _L1_ffn_all.items() if k in ('W_fx', 'b_fx', 'W_x', 'b_x', 'W_slice', 'b_slice', 'W_q', 'W_k', 'W_v', 'W_out', 'b_out', 'temperature')}
    del _L1_ffn_all
    return {'x': x, 'src': src, 'dst': dst, 'edge_attr_256': edge_attr_256, 'L0_gnn_W_f': _L0_gnn_in['W_f'], 'L0_gnn_a_src_f': _L0_gnn_in['a_src_f'], 'L0_gnn_a_dst_f': _L0_gnn_in['a_dst_f'], 'L0_gnn_b_f': _L0_gnn_in['b_f'], 'L0_gnn_W_b': _L0_gnn_in['W_b'], 'L0_gnn_a_src_b': _L0_gnn_in['a_src_b'], 'L0_gnn_a_dst_b': _L0_gnn_in['a_dst_b'], 'L0_gnn_b_b': _L0_gnn_in['b_b'], 'L0_gnn_W_fuse': _L0_gnn_in['W_fuse'], 'L0_gnn_b_fuse': _L0_gnn_in['b_fuse'], 'L0_gnn_gamma': _L0_gnn_in['gamma'], 'L0_gnn_beta': _L0_gnn_in['beta'], 'L0_gnn_run_mean': _L0_gnn_in['run_mean'], 'L0_gnn_run_var': _L0_gnn_in['run_var'], 'L0_ffn_Wg': _L0_ffn_in['Wg'], 'L0_ffn_bg': _L0_ffn_in['bg'], 'L0_ffn_W1': _L0_ffn_in['W1'], 'L0_ffn_b1': _L0_ffn_in['b1'], 'L0_ffn_W2': _L0_ffn_in['W2'], 'L0_ffn_b2': _L0_ffn_in['b2'], 'L1_gnn_Wq': _L1_gnn_in['Wq'], 'L1_gnn_bq': _L1_gnn_in['bq'], 'L1_gnn_Wk': _L1_gnn_in['Wk'], 'L1_gnn_bk': _L1_gnn_in['bk'], 'L1_gnn_Wv': _L1_gnn_in['Wv'], 'L1_gnn_bv': _L1_gnn_in['bv'], 'L1_gnn_We': _L1_gnn_in['We'], 'L1_gnn_Ws': _L1_gnn_in['Ws'], 'L1_gnn_bs': _L1_gnn_in['bs'], 'L1_ffn_W_fx': _L1_ffn_in['W_fx'], 'L1_ffn_b_fx': _L1_ffn_in['b_fx'], 'L1_ffn_W_x': _L1_ffn_in['W_x'], 'L1_ffn_b_x': _L1_ffn_in['b_x'], 'L1_ffn_W_slice': _L1_ffn_in['W_slice'], 'L1_ffn_b_slice': _L1_ffn_in['b_slice'], 'L1_ffn_W_q': _L1_ffn_in['W_q'], 'L1_ffn_W_k': _L1_ffn_in['W_k'], 'L1_ffn_W_v': _L1_ffn_in['W_v'], 'L1_ffn_W_out': _L1_ffn_in['W_out'], 'L1_ffn_b_out': _L1_ffn_in['b_out'], 'L1_ffn_temperature': _L1_ffn_in['temperature']}

def reference(x, src, dst, edge_attr_256, L0_gnn_W_f, L0_gnn_a_src_f, L0_gnn_a_dst_f, L0_gnn_b_f, L0_gnn_W_b, L0_gnn_a_src_b, L0_gnn_a_dst_b, L0_gnn_b_b, L0_gnn_W_fuse, L0_gnn_b_fuse, L0_gnn_gamma, L0_gnn_beta, L0_gnn_run_mean, L0_gnn_run_var, L0_ffn_Wg, L0_ffn_bg, L0_ffn_W1, L0_ffn_b1, L0_ffn_W2, L0_ffn_b2, L1_gnn_Wq, L1_gnn_bq, L1_gnn_Wk, L1_gnn_bk, L1_gnn_Wv, L1_gnn_bv, L1_gnn_We, L1_gnn_Ws, L1_gnn_bs, L1_ffn_W_fx, L1_ffn_b_fx, L1_ffn_W_x, L1_ffn_b_x, L1_ffn_W_slice, L1_ffn_b_slice, L1_ffn_W_q, L1_ffn_W_k, L1_ffn_W_v, L1_ffn_W_out, L1_ffn_b_out, L1_ffn_temperature):
    import jax
    import jax.numpy as jnp

    def _L0_gnn_ref(x, edge_index, W_f, a_src_f, a_dst_f, b_f, W_b, a_src_b, a_dst_b, b_b, W_fuse, b_fuse, gamma, beta, run_mean, run_var):
        import jax, jax.numpy as jnp
        import numpy as np
        N, E, DIN, HID, HEADS = (6250, 200000, 256, 256, 4)
        C = HID // 2 // HEADS
        NEG_SLOPE = 0.2
        BN_EPS = 1e-05

        def _gat(x, W, a_src, a_dst, b, src, dst):
            xl = (x @ W).reshape(N, HEADS, C)
            al = jnp.einsum('nhc,hc->nh', xl, a_src)
            ar = jnp.einsum('nhc,hc->nh', xl, a_dst)
            e = jax.nn.leaky_relu(al[src] + ar[dst], NEG_SLOPE)
            m = jax.ops.segment_max(e, dst, num_segments=N)
            w = jnp.exp(e - m[dst])
            den = jax.ops.segment_sum(w, dst, num_segments=N)
            alpha = w / (den[dst] + 1e-16)
            msg = xl[src] * alpha[..., None]
            out = jax.ops.segment_sum(msg, dst, num_segments=N)
            return out.reshape(N, HEADS * C) + b
        loop = jnp.arange(N, dtype=edge_index.dtype)
        src = jnp.concatenate([edge_index[0], loop])
        dst = jnp.concatenate([edge_index[1], loop])
        fwd = _gat(x, W_f, a_src_f, a_dst_f, b_f, src, dst)
        bwd = _gat(x, W_b, a_src_b, a_dst_b, b_b, dst, src)
        h = jnp.concatenate([fwd, bwd], axis=1) @ W_fuse + b_fuse
        h = (h - run_mean) * jax.lax.rsqrt(run_var + BN_EPS) * gamma + beta
        return jax.nn.relu(h)

    def _L0_ffn_ref(x, Wg, bg, W1, b1, W2, b2):
        import jax, jax.numpy as jnp
        import numpy as np
        B, S, D, E, H, K = (4, 512, 256, 8, 512, 2)
        Bv, Sv, Dv = x.shape
        gate_scores = x @ Wg + bg
        _, idx = jax.lax.top_k(gate_scores, K)
        mask = jax.nn.one_hot(idx, E, dtype=x.dtype).sum(axis=-2)
        xf = x.reshape(-1, Dv)
        mf = mask.reshape(-1, E)
        h = jax.nn.gelu(jnp.einsum('td,edh->teh', xf, W1) + b1[None], approximate=False)
        y = jnp.einsum('teh,ehd->ted', h, W2) + b2[None]
        out = jnp.einsum('ted,te->td', y, mf)
        return out.reshape(Bv, Sv, Dv)

    def _L1_gnn_ref(x, edge_index, edge_attr, Wq, bq, Wk, bk, Wv, bv, We, Ws, bs):
        import jax, jax.numpy as jnp
        import numpy as np
        N, E, NIN, H, C = (6250, 100000, 256, 8, 32)
        HC = H * C
        src, dst = (edge_index[0], edge_index[1])
        n = x.shape[0]
        q = (x @ Wq + bq).reshape(n, H, C)
        k = (x @ Wk + bk).reshape(n, H, C)
        v = (x @ Wv + bv).reshape(n, H, C)
        e = (edge_attr @ We).reshape(-1, H, C)
        k_j = k[src] + e
        v_j = v[src] + e
        q_i = q[dst]
        alpha = jnp.sum(q_i * k_j, axis=-1) / jnp.sqrt(jnp.float32(C))
        amax = jax.ops.segment_max(alpha, dst, num_segments=n)
        ex = jnp.exp(alpha - amax[dst])
        denom = jax.ops.segment_sum(ex, dst, num_segments=n)
        alpha = ex / denom[dst]
        out = jax.ops.segment_sum(v_j * alpha[:, :, None], dst, num_segments=n)
        out = out.reshape(n, HC)
        out = out + x @ Ws + bs
        return out

    def _L1_ffn_ref(x, W_fx, b_fx, W_x, b_x, W_slice, b_slice, W_q, W_k, W_v, W_out, b_out, temperature):
        import jax, jax.numpy as jnp
        import numpy as np
        DIM = 256
        H = 8
        D = 64
        G = 64
        INNER = H * D
        SCALE = D ** (-0.5)
        B, N, _ = x.shape
        fx_mid = (x @ W_fx + b_fx).reshape(B, N, H, D).transpose(0, 2, 1, 3)
        x_mid = (x @ W_x + b_x).reshape(B, N, H, D).transpose(0, 2, 1, 3)
        temp = jnp.clip(temperature, 0.1, 5.0)
        slice_weights = jax.nn.softmax((x_mid @ W_slice + b_slice) / temp, axis=-1)
        slice_norm = slice_weights.sum(axis=2)
        slice_token = jnp.einsum('bhnc,bhng->bhgc', fx_mid, slice_weights)
        slice_token = slice_token / (slice_norm[..., None] + 1e-05)
        q = slice_token @ W_q
        k = slice_token @ W_k
        v = slice_token @ W_v
        attn = jax.nn.softmax(jnp.einsum('bhgc,bhkc->bhgk', q, k) * SCALE, axis=-1)
        out_slice = jnp.einsum('bhgk,bhkc->bhgc', attn, v)
        out_x = jnp.einsum('bhgc,bhng->bhnc', out_slice, slice_weights)
        out_x = out_x.transpose(0, 2, 1, 3).reshape(B, N, INNER)
        return out_x @ W_out + b_out
    edge_index = jnp.stack([src, dst])
    x = x + _L0_gnn_ref(_layernorm(x, axis=-1), edge_index, L0_gnn_W_f, L0_gnn_a_src_f, L0_gnn_a_dst_f, L0_gnn_b_f, L0_gnn_W_b, L0_gnn_a_src_b, L0_gnn_a_dst_b, L0_gnn_b_b, L0_gnn_W_fuse, L0_gnn_b_fuse, L0_gnn_gamma, L0_gnn_beta, L0_gnn_run_mean, L0_gnn_run_var)
    x = x + _L0_ffn_ref(_layernorm(x, axis=-1)[None], L0_ffn_Wg, L0_ffn_bg, L0_ffn_W1, L0_ffn_b1, L0_ffn_W2, L0_ffn_b2)[0]
    x = x + _L1_gnn_ref(_layernorm(x, axis=-1), edge_index, edge_attr_256, L1_gnn_Wq, L1_gnn_bq, L1_gnn_Wk, L1_gnn_bk, L1_gnn_Wv, L1_gnn_bv, L1_gnn_We, L1_gnn_Ws, L1_gnn_bs)
    x = x + _L1_ffn_ref(_layernorm(x, axis=-1)[None], L1_ffn_W_fx, L1_ffn_b_fx, L1_ffn_W_x, L1_ffn_b_x, L1_ffn_W_slice, L1_ffn_b_slice, L1_ffn_W_q, L1_ffn_W_k, L1_ffn_W_v, L1_ffn_W_out, L1_ffn_b_out, L1_ffn_temperature)[0]
    return x

_drawn_inputs = setup_inputs


def setup_inputs(seed=0):
    import zlib

    import numpy as np

    out = dict(_drawn_inputs(seed))
    spreads = {'L0_gnn_b_f': (0.0, 0.1),
     'L0_gnn_b_b': (0.0, 0.1),
     'L0_gnn_b_fuse': (0.0, 0.1),
     'L0_gnn_gamma': (1.0, 0.2),
     'L0_gnn_beta': (0.0, 0.1),
     'L0_gnn_run_mean': (0.0, 0.1),
     'L0_gnn_run_var': (1.0, 0.2),
     'L0_ffn_bg': (0.0, 0.1),
     'L0_ffn_b1': (0.0, 0.1),
     'L0_ffn_b2': (0.0, 0.1),
     'L1_ffn_b_fx': (0.0, 0.1),
     'L1_ffn_b_x': (0.0, 0.8),
     'L1_ffn_b_slice': (0.0, 2.0),
     'L1_ffn_b_out': (0.0, 0.1),
     'L1_ffn_temperature': (0.5, 0.6)}
    factors = {'L0_gnn_a_dst_f': 3.6,
     'L0_gnn_a_dst_b': 3.899,
     'L1_gnn_bq': 3.866,
     'L1_gnn_bk': 64.0,
     'L1_ffn_W_x': 8.0,
     'L1_ffn_W_slice': 8.0,
     'L1_ffn_W_q': 8.0,
     'L1_ffn_W_k': 8.0}
    for name, (base, spread) in spreads.items():
        noise = np.random.default_rng([zlib.crc32(name.encode()), seed]).standard_normal(out[name].shape)
        drawn = base * np.exp(spread * noise) if base else spread * noise
        out[name] = jnp.asarray(drawn.astype(out[name].dtype))
    for name, factor in factors.items():
        out[name] = (out[name] * factor).astype(out[name].dtype)
    return out
```

```python
import concourse.bass as bass
from concourse import mybir
from contextlib import ExitStack

FP32 = mybir.dt.float32
BF16 = mybir.dt.bfloat16
I32 = mybir.dt.int32
ALU = mybir.AluOpType
ACT = mybir.ActivationFunctionType
AX = mybir.AxisListType

P = 128
N, D = 6250, 256
E = 100000
NI = -(-N // P)
NG, GT = 7, 7
assert NG * GT == NI
B = 8
T = 784
EP = P * T
NBLK = T // B
LO = 64
KEYS = P * LO
H, C = 8, 32
DEN, MX = H * C, H * C + H
SW = H * C + 2 * H
TW = 136
BIG = 1.0e30
LN_EPS = BN_EPS = 1e-5
EXP = 8
HID = 512


class Chip:

    def semaphores(self, phase, prefix):
        made = []

        def semaphore(name):
            made.append(self.nc.alloc_semaphore(prefix + name))
            return made[-1]

        def clear():
            self.nc.clear_and_free_semaphores(made)
            self.nc.all_engine_barrier()

        phase.callback(clear)
        return semaphore

    def alone(self, eng):
        eng.sem_inc(self.placed, 1)


def row_bcast(v, lo, n):
    return v[lo:lo + n].rearrange("(a n) -> a n", a=1).to_broadcast([P, n])


def layernorm_stats(c, v, w, x_of, n, sqrt_in, sqrt_out, turn):
    for j in range(n):
        c.nc.vector.bn_stats(w["stats"][:, j, :], x_of(j))
    v.drain()
    for j in range(n):
        c.nc.vector.bn_aggr(w["mv"][:, j, :], w["stats"][:, j, :])
    v.drain()
    c.nc.vector.tensor_scalar(w["rstd"][:, 0:n], w["mv"][:, 0:n, 1], LN_EPS, None, ALU.add).then_inc(sqrt_in, 1)
    v.wait_ge(sqrt_out, turn)
    c.nc.vector.reciprocal(w["rstd"][:, 0:n], w["rstd"][:, 0:n])
    v.drain()


def constants(c):
    nc = c.nc
    with ExitStack() as s:
        made = s.enter_context(nc.semaphore("const_made"))
        got = s.enter_context(nc.semaphore("x_loaded"))
        zero = s.enter_context(nc.semaphore("pad_zeroed"))
        block = s.enter_context(nc.Block())

        @block.gpsimd
        def _(pool):
            nc.gpsimd.memset(c.ident[:], 0.0)
            nc.gpsimd.memset(c.tri[:], 1.0)
            nc.gpsimd.memset(c.triT[:], 1.0)
            pool.drain()
            nc.gpsimd.affine_select(out=c.ident[:], in_=c.ident[:], compare_op=ALU.not_equal, fill=1.0,
                                    base=0, pattern=[[-1, P]], channel_multiplier=1)
            nc.gpsimd.affine_select(out=c.tri[:], in_=c.tri[:], compare_op=ALU.is_gt, fill=0.0,
                                    base=0, pattern=[[-1, P]], channel_multiplier=1)
            nc.gpsimd.affine_select(out=c.triT[:], in_=c.triT[:], compare_op=ALU.is_gt, fill=0.0,
                                    base=0, pattern=[[1, P]], channel_multiplier=-1)
            nc.gpsimd.iota(c.cols[:], [[1, P]], base=0, channel_multiplier=0,
                           allow_small_or_imprecise_dtypes=True)
            pool.drain()
            nc.gpsimd.memset(c.one[:], 1.0)
            nc.gpsimd.memset(c.zrow[:], 0.0).then_inc(made, 1)


        @block.vector
        def _(v):
            nc.vector.memset(c.x[96:128, :], 0.0).then_inc(zero, 1)
            v.wait_ge(made, 1)
            nc.vector.tensor_copy(c.identb[:], c.ident[:])
            nc.vector.tensor_copy(c.colsb[:], c.cols[:])
            v.drain()

        @block.sync
        def _(sp):
            x = c.A["x"]
            full = (P - 1) * NI
            sp.wait_ge(zero, 1)
            sp.dma_start(c.x[0:P - 1, :], x[0:full, :].rearrange("(p i) d -> p (i d)", i=NI)).then_inc(got, 16)
            sp.dma_start(c.x[P - 1:P, 0:(N - full) * D],
                         x[full:N, :].rearrange("(p i) d -> p (i d)", p=1)).then_inc(got, 16)
            sp.wait_ge(got, 32)


def layer0_tables(c):
    nc, A = c.nc, c.A
    with ExitStack() as s:
        sb = lambda n, shape, dt=FP32: s.enter_context(nc.sbuf_tensor(n, shape, dt))
        sem = lambda n: s.enter_context(nc.semaphore(n))
        pb = lambda n: s.enter_context(nc.psum_tensor(n, [P, 512], FP32))
        W = sb("t_W", [P, 2, 2 * TW])
        av = sb("t_av", [P, 4, 4])
        WT = sb("t_WT", [P, 2, 2, P])
        w = {"stats": sb("t_st", [P, GT, 6]), "mv": sb("t_mv", [P, GT, 2]), "rstd": sb("t_rs", [P, GT])}
        xln = sb("t_xln", [P, GT, D])
        xT = sb("t_xT", [P, 2, GT * P])
        row = sb("t_row", [P, 2, GT, TW])
        psT = [pb("t_psT0"), pb("t_psT1")]
        psO = [pb("t_psO0"), pb("t_psO1")]
        loaded, zeroed, wt, wtc, wa, ready = (sem("t_" + n) for n in ("ld", "z", "wt", "wtc", "wa", "rdy"))
        vin, root, xr, tr, tc, mm, oc, st = (sem("t_" + n) for n in ("vin", "root", "xr", "tr", "tc", "mm", "oc", "st"))
        block = s.enter_context(nc.Block())
        names = [("L0_gnn_a_src_f", 0), ("L0_gnn_a_dst_f", 1), ("L0_gnn_a_src_b", 2), ("L0_gnn_a_dst_b", 3)]

        @block.sync
        def _(sp):
            for d, name in enumerate(("L0_gnn_W_f", "L0_gnn_W_b")):
                sp.dma_start(W[:, :, d * TW:d * TW + P], A[name].rearrange("(k p) c -> p k c", p=P)).then_inc(loaded, 16)
            sp.wait_ge(zeroed, 1)
            for name, at in names:
                for h in range(4):
                    sp.dma_start(av[h * 32:(h + 1) * 32, at, h:h + 1],
                                 A[name][h:h + 1, :].rearrange("a c -> c a")).then_inc(loaded, 16)
            with sp.Fori(0, NG) as g:
                sp.wait_ge(oc, (g + 1) * GT)
                sp.wait_ge(loaded, 16 * 18)
                for d, tab in enumerate((c.t1, c.t2)):
                    sp.dma_start(tab.rearrange("(p i) w -> p (i w)", i=NI)[:, bass.ds(g * (GT * TW), GT * TW)],
                                 row[:, d, :, :]).then_inc(st, 16)
            sp.wait_ge(st, 32 * NG)

        @block.vector
        def _(v):
            nc.vector.memset(av[:], 0.0).then_inc(zeroed, 1)
            with v.Fori(0, NG) as g:
                layernorm_stats(c, v, w, lambda j: c.x[:, bass.ds((g * GT + j) * D, D)], GT, vin, root, g + 1)
                for j in range(GT):
                    nc.vector.tensor_scalar(xln[:, j, :], c.x[:, bass.ds((g * GT + j) * D, D)], w["mv"][:, j, 0:1],
                                            w["rstd"][:, j:j + 1], ALU.subtract, ALU.mult).then_inc(xr, 1)
                v.wait_ge(tr, (g + 1) * GT)

        @block.scalar
        def _(act):
            for d in range(2):
                act.wait_ge(wt, d + 1)
                nc.scalar.activation(WT[:, d, :, :], psT[d][:, 0:2 * P], ACT.Copy).then_inc(wtc, 1)
            act.wait_ge(wa, 1)
            for k in range(2):
                for d in range(2):
                    for q in range(2):
                        o = (k * 4 + d * 2 + q) * 4
                        last = nc.scalar.activation(W[:, k, d * TW + P + 4 * q:d * TW + P + 4 * q + 4],
                                                    psO[0][:, o:o + 4], ACT.Copy)
            last.then_inc(ready, 1)
            with act.Fori(0, NG) as g:
                act.wait_ge(vin, g + 1)
                nc.scalar.activation(w["rstd"][:], w["rstd"][:], ACT.Sqrt).then_inc(root, 1)
                for j in range(GT):
                    act.wait_ge(tr, g * GT + j + 1)
                    nc.scalar.activation(xT[:, :, j * P:(j + 1) * P],
                                         psT[j % 2][:, 0:2 * P].rearrange("p (k n) -> p k n", k=2),
                                         ACT.Copy).then_inc(tc, 1)
                for j in range(GT):
                    act.wait_ge(mm, g * GT + j + 1)
                    nc.scalar.activation(row[:, :, j, :], psO[j % 2][:, 0:2 * TW].rearrange("p (d w) -> p d w", d=2),
                                         ACT.Copy).then_inc(oc, 1)
                act.wait_ge(st, (g + 1) * 32)

        @block.tensor
        def _(pe):
            pe.wait_ge(loaded, 16 * 18)
            for d in range(2):
                for k in range(2):
                    last = nc.tensor.transpose(psT[d][:, k * P:(k + 1) * P], W[:, k, d * TW:d * TW + P], c.ident[:])
                last.then_inc(wt, 1)
            pe.wait_ge(wtc, 2)
            for k in range(2):
                for d in range(2):
                    for q in range(2):
                        o = (k * 4 + d * 2 + q) * 4
                        last = nc.tensor.matmul(psO[0][:, o:o + 4], WT[:, d, k, :], av[:, 2 * d + q, :],
                                                start=True, stop=True)
            last.then_inc(wa, 1)
            pe.wait_ge(ready, 1)
            with pe.Fori(0, NG) as g:
                for j in range(GT):
                    pe.wait_ge(xr, g * GT + j + 1)
                    if j >= 2:
                        pe.wait_ge(tc, g * GT + j - 1)
                    for k in range(2):
                        last = nc.tensor.transpose(psT[j % 2][:, k * P:(k + 1) * P], xln[:, j, k * P:(k + 1) * P], c.ident[:])
                    last.then_inc(tr, 1)
                for j in range(GT):
                    pe.wait_ge(tc, g * GT + j + 1)
                    if j >= 2:
                        pe.wait_ge(oc, g * GT + j - 1)
                    for k in range(2):
                        last = nc.tensor.matmul(psO[j % 2][:, 0:2 * TW], xT[:, k, j * P:(j + 1) * P], W[:, k, :],
                                                start=(k == 0), stop=(k == 1))
                    last.then_inc(mm, 1)
                pe.wait_ge(oc, (g + 1) * GT)


def sort_edges(c):
    nc, A = c.nc, c.A
    U = 2
    with ExitStack() as s:
        sb = lambda n, shape, dt=FP32: s.enter_context(nc.sbuf_tensor(n, shape, dt))
        sem = c.semaphores(s, "s_")
        pb = lambda n, shape=(P, 512), dt=FP32: s.enter_context(nc.psum_tensor(n, list(shape), dt))
        key = sb("s_key", [P, 2, T], I32)
        dig = sb("s_dig", [P, 2, 2, T], I32)
        eid = sb("s_eid", [P, T], I32)
        oh = sb("s_oh", [P, U, 2, B, P], BF16)
        ol = sb("s_ol", [P, U, 2, B, LO], BF16)
        keyf = sb("s_kf", [P, U, 2, B])
        oht = sb("s_oht", [P, 4, P])
        tab = sb("s_tab", [P, 4, LO])
        junk = sb("s_junk", [P, P])
        junk1, junk2 = sb("s_junk1", [P, 2 * B, P], BF16), sb("s_junk2", [P, 2 * B, LO], BF16)
        rank = sb("s_rank", [P, U, 2, 2, B])
        posf = sb("s_posf", [P, 2, B])
        pos = sb("s_pos", [P, U, 2, B], I32)
        rec = sb("s_rec", [P, U, B, 4], I32)
        hist, base, tmp = sb("s_hist", [P, 2, LO]), sb("s_base", [P, 2, LO]), sb("s_tmp", [P, LO])
        tot, offs = sb("s_tot", [P, 2]), sb("s_offs", [P, 2])
        nid = sb("s_nid", [P, LO])
        ends = sb("s_ends", [P, 2, 2, LO], I32)
        psT = [pb(f"s_psT{k}", (P, 1024), BF16) for k in range(2)]
        psK = [pb(f"s_psK{k}") for k in range(2)]
        psH = [pb(f"s_psH{k}") for k in range(2)]
        psR = [pb(f"s_psR{k}") for k in range(2)]
        kz, kld, made1, used1, hd, hc, off, offc, bd = (sem(n) for n in ("kz", "kld", "m1", "u1", "hd", "hc", "off", "offc", "bd"))
        made2, tp, tpc, kr, eqd, tbc, lk, lkd, hu, pd, sct0, sct1, rz, wr = (sem(n) for n in (
            "m2", "tp", "tpc", "kr", "eqd", "tbc", "lk", "lkd", "hu", "pd", "sct0", "sct1", "rz", "wr"))
        sct = [sct0, sct1]
        recs_free, ids = sem("recs_free"), sem("ids")
        block = s.enter_context(nc.Block())
        full = (P - 1) * T

        def one_hots(v, t0, u):
            for k in range(2):
                nc.vector.tensor_tensor(oh[:, u, k, :, :], c.colsb[:, :].unsqueeze(1).to_broadcast([P, B, P]),
                                        dig[:, k, 0, bass.ds(t0, B)].unsqueeze(2).to_broadcast([P, B, P]), ALU.is_equal)
                last = nc.vector.tensor_tensor(ol[:, u, k, :, :], c.colsb[:, 0:LO].unsqueeze(1).to_broadcast([P, B, LO]),
                                               dig[:, k, 1, bass.ds(t0, B)].unsqueeze(2).to_broadcast([P, B, LO]), ALU.is_equal)
            return last

        @block.sync
        def _(sp):
            sp.wait_ge(kz, 1)
            for k, name in enumerate(("dst", "src")):
                a = A[name]
                sp.dma_start(key[0:P - 1, k, :], a[0:full].rearrange("(p t) -> p t", t=T)).then_inc(kld, 16)
                sp.dma_start(key[P - 1:P, k, 0:E - full], a[full:E].rearrange("(p t) -> p t", p=1)).then_inc(kld, 16)
            for a in (c.st_f, c.st_b):
                sp.dma_start(a[0:EP, :].rearrange("(p t) w -> p (t w)", p=P), c.zrow[:]).then_inc(rz, 16)
            sp.wait_ge(rz, 32)
            sp.wait_ge(bd, 1)
            for k in range(2):
                for q in range(2):
                    sp.dma_start(c.ends[k][q].rearrange("(p l) -> p l", l=LO), ends[:, k, q, :]).then_inc(wr, 16)
            sp.wait_ge(wr, 64)
            sp.sem_inc(recs_free, U)
            with sp.Fori(0, NBLK // U) as i:
                for u in range(U):
                    sp.wait_ge(sct[u], (i + 1) * (16 * 2 * B))
                    sp.sem_inc(recs_free, 1)

        @block.vector
        def _(v):
            nc.vector.memset(key[:], N).then_inc(kz, 1)
            v.wait_ge(kld, 64)
            nc.vector.tensor_scalar(dig[:, :, 0, :], key[:], 6, None, ALU.logical_shift_right)
            nc.vector.tensor_scalar(dig[:, :, 1, :], key[:], LO - 1, None, ALU.bitwise_and)
            v.drain()
            v.sem_inc(used1, U)
            with v.Fori(0, NBLK // U) as i:
                for u in range(U):
                    v.wait_ge(used1, i * U + u + 1)
                    one_hots(v, (i * U + u) * B, u).then_inc(made1, 1)
            v.wait_ge(ids, 1)
            v.wait_ge(hd, 1)
            for k in range(2):
                nc.vector.tensor_copy(hist[:, k, :], psH[k][:, 0:LO])
            v.drain()
            for k in range(2):
                nc.vector.tensor_reduce(tot[:, k:k + 1], hist[:, k, :], AX.X, ALU.add)
            v.drain()
            nc.vector.tensor_copy(junk[:, 0:2], tot[:]).then_inc(hc, 1)
            v.wait_ge(off, 1)
            nc.vector.tensor_copy(offs[:], psR[0][:, 0:2])
            v.drain()
            nc.vector.memset(tmp[:], 0.0)
            v.drain()
            for k in range(2):
                nc.vector.tensor_tensor_scan(base[:, k, :], hist[:, k, :], tmp[:], offs[:, k:k + 1], ALU.add, ALU.add)
            v.drain()
            for k in range(2):
                nc.vector.tensor_scalar(tmp[:], hist[:, k, :], 0.5, None, ALU.is_ge)
                nc.vector.tensor_scalar(junk[:, 0:LO], base[:, k, :], -1.0 - EP, None, ALU.add)
                nc.vector.tensor_tensor(base[:, k, :], base[:, k, :], hist[:, k, :], ALU.subtract)
                v.drain()
                nc.vector.tensor_tensor(junk[:, 0:LO], junk[:, 0:LO], tmp[:], ALU.mult)
                nc.vector.tensor_tensor(junk[:, LO:2 * LO], base[:, k, :], nid[:], ALU.subtract)
                v.drain()
                nc.vector.tensor_scalar(ends[:, k, 1, :], junk[:, 0:LO], float(EP), None, ALU.add)
                nc.vector.tensor_tensor(junk[:, LO:2 * LO], junk[:, LO:2 * LO], tmp[:], ALU.mult)
                v.drain()
                nc.vector.tensor_tensor(ends[:, k, 0, :], junk[:, LO:2 * LO], nid[:], ALU.add)
                v.drain()
            nc.vector.tensor_copy(tmp[:], base[:, 0, :]).then_inc(bd, 1)
            with v.Fori(0, NBLK // U) as i:
                for u in range(U):
                    blk = i * U + u
                    v.wait_ge(hu, (blk + 1) * 2 * B)
                    nc.vector.tensor_copy(keyf[:, u, :, :], key[:, :, bass.ds(blk * B, B)])
                    one_hots(v, blk * B, u).then_inc(made2, 1)
                    v.drain()
                    for j in range(B):
                        for k in range(2):
                            n = 2 * j + k
                            v.wait_ge(kr, blk * 2 * B + n + 1)
                            nc.vector.scalar_tensor_tensor(out=junk1[:, n, :], in0=psK[k][:, 0:P], scalar=keyf[:, u, k, j:j + 1],
                                                           in1=c.tri[:], op0=ALU.is_equal, op1=ALU.mult,
                                                           accum_out=rank[:, u, k, 0, j:j + 1]).then_inc(eqd, 1)
                            v.wait_ge(lk, blk * 2 * B + n + 1)
                            nc.vector.scalar_tensor_tensor(out=junk2[:, n, :], in0=psR[k][:, 0:LO], scalar=1.0,
                                                           in1=ol[:, u, k, j, :], op0=ALU.mult, op1=ALU.mult,
                                                           accum_out=rank[:, u, k, 1, j:j + 1]).then_inc(lkd, 1)
                    v.drain()
                    nc.vector.tensor_tensor(posf[:], rank[:, u, :, 0, :], rank[:, u, :, 1, :], ALU.add)
                    v.drain()
                    v.wait_ge(recs_free, blk + 1)
                    nc.vector.tensor_copy(pos[:, u, :, :], posf[:])
                    nc.vector.tensor_copy(rec[:, u, :, 0:2], key[:, :, bass.ds(blk * B, B)].rearrange("p k t -> p t k"))
                    nc.vector.tensor_copy(rec[:, u, :, 2], eid[:, bass.ds(blk * B, B)]).then_inc(pd, 1)

        @block.scalar
        def _(act):
            act.wait_ge(bd, 1)
            with act.Fori(0, NBLK // U) as i:
                for u in range(U):
                    blk = i * U + u
                    for j in range(B):
                        for k in range(2):
                            n = 2 * j + k
                            r = n % 4
                            act.wait_ge(tp, blk * 2 * B + n + 1)
                            nc.scalar.activation(oht[:, r, :], psT[k][:, 0:P], ACT.Copy).then_inc(tpc, 1)
                            act.wait_ge(hu, (blk + U) * 2 * B + n - 1)
                            nc.scalar.activation(tab[:, r, :], psH[k][:, 0:LO], ACT.Copy).then_inc(tbc, 1)

        @block.tensor
        def _(pe):
            for k in range(2):
                nc.tensor.matmul(psH[k][:, 0:LO], c.zrow[:, 0:P], c.zrow[:, 0:LO], start=True, stop=False)
            with pe.Fori(0, NBLK // U) as i:
                for u in range(U):
                    pe.wait_ge(made1, i * U + u + 1)
                    for k in range(2):
                        for j in range(B):
                            last = nc.tensor.matmul(psH[k][:, 0:LO], oh[:, u, k, j, :], ol[:, u, k, j, :], start=False, stop=False)
                    last.then_inc(used1, 1)
            for k in range(2):
                last = nc.tensor.matmul(psH[k][:, 0:LO], c.zrow[:, 0:P], c.zrow[:, 0:LO], start=False, stop=True)
            last.then_inc(hd, 1)
            pe.wait_ge(hc, 1)
            nc.tensor.matmul(psR[0][:, 0:2], c.triT[:], tot[:], start=True, stop=True).then_inc(off, 1)
            pe.wait_ge(bd, 1)
            for k in range(2):
                last = nc.tensor.matmul(psH[k][:, 0:LO], c.ident[:], base[:, k, :], start=True, stop=True)
            last.then_inc(hu, 2 * U * B)
            pe.sem_inc(eqd, 2)
            pe.sem_inc(lkd, 2)
            pe.sem_inc(tpc, 2)
            with pe.Fori(0, NBLK // U) as i:
                for u in range(U):
                    blk = i * U + u
                    pe.wait_ge(made2, blk + 1)
                    for j in range(B):
                        for k in range(2):
                            n = 2 * j + k
                            r = n % 4
                            pe.wait_ge(tpc, blk * 2 * B + n + 1)
                            nc.tensor.transpose(psT[k][:, 0:P], oh[:, u, k, j, :], c.identb[:]).then_inc(tp, 1)
                            pe.wait_ge(eqd, blk * 2 * B + n + 1)
                            nc.tensor.matmul(psK[k][:, 0:P], keyf[:, u, k, j:j + 1].to_broadcast([P, P]), c.ident[:],
                                             start=True, stop=True).then_inc(kr, 1)
                            pe.wait_ge(tbc, blk * 2 * B + n + 1)
                            pe.wait_ge(lkd, blk * 2 * B + n + 1)
                            nc.tensor.matmul(psR[k][:, 0:LO], oht[:, r, :], tab[:, r, :], start=True, stop=True).then_inc(lk, 1)
                            last = nc.tensor.matmul(psH[k][:, 0:LO], oh[:, u, k, j, :], ol[:, u, k, j, :],
                                                    start=False, stop=True, skip_group_check=True)
                            last.then_inc(hu, 1)

        @block.gpsimd
        def _(pool):
            nc.gpsimd.iota(eid[:], [[1, T]], base=0, channel_multiplier=T)
            nc.gpsimd.iota(nid[:], [[1, LO]], base=EP, channel_multiplier=LO, allow_small_or_imprecise_dtypes=True)
            nc.gpsimd.memset(rec[:], 0)
            pool.drain()
            nc.gpsimd.tensor_scalar(eid[:], eid[:], E - 1, None, ALU.min).then_inc(ids, 1)
            pool.drain()
            pool.wait_ge(kz, 1)
            with pool.Fori(0, NBLK // U) as i:
                for u in range(U):
                    pool.wait_ge(pd, i * U + u + 1)
                    c.alone(pool)
                    for j in range(B):
                        for k, a in enumerate((c.rec_d, c.rec_s)):
                            pool.indirect_dma_start(a, bass.IndirectOffsetOnAxis(ap=pos[:, u, k, j:j + 1], axis=0),
                                                    rec[:, u, j, :], None).then_inc(sct[u], 16)
            for u in range(U):
                pool.wait_ge(sct[u], 16 * 2 * B * (NBLK // U))

def targets_logits(c):
    nc = c.nc
    with ExitStack() as s:
        sb = lambda n, shape, dt=FP32: s.enter_context(nc.sbuf_tensor(n, shape, dt))
        sem = c.semaphores(s, "a_")
        startn = sb("a_start", [P, 2, NI], I32)
        logit = sb("a_logit", [P, 2, NI, 4])
        idx = sb("a_idx", [P, 2, GT], I32)
        rows = sb("a_rows", [P, 2, GT, 4])
        val = sb("a_val", [P, 2, T, 4])
        first = sb("a_first", [P, 2, TW])
        ld, rl, sc, fg, vl, chunk = (sem(n) for n in ("ld", "rl", "sc", "fg", "vl", "chunk"))
        block = s.enter_context(nc.Block())

        @block.sync
        def _(sp):
            for d, (tab, rec) in enumerate(((c.t1, c.rec_d), (c.t2, c.rec_s))):
                sp.dma_start(c.rec[:, d, :, :], rec.rearrange("(p t) w -> p t w", p=P)).then_inc(rl, 16)
                sp.dma_start(startn[:, d, :], c.ends[d][0][0:NI * P].rearrange("(p i) -> p i", i=NI)).then_inc(ld, 16)
                sp.dma_start(logit[:, d, :, :], tab.rearrange("(p i) w -> p i w", i=NI)[:, :, 132:136]).then_inc(ld, 16)
            sp.wait_ge(sc, NG * 2 * GT * 16)
            for d, st in enumerate((c.st_f, c.st_b)):
                sp.dma_start(val[:, d, :, :], st[0:EP, :].rearrange("(p t) w -> p t w", p=P)).then_inc(vl, 16)
            sp.wait_ge(vl, 32)

        @block.gpsimd
        def _(pool):
            pool.wait_ge(ld, 64)
            pool.wait_ge(rl, 32)
            with pool.Fori(0, NG) as g:
                nc.gpsimd.tensor_copy(idx[:], startn[:, :, bass.ds(g * GT, GT)])
                nc.gpsimd.tensor_copy(rows[:], logit[:, :, bass.ds(g * GT, GT), :])
                pool.drain()
                for j in range(GT):
                    for d, st in enumerate((c.st_f, c.st_b)):
                        pool.indirect_dma_start(st, bass.IndirectOffsetOnAxis(ap=idx[:, d, j:j + 1], axis=0),
                                                rows[:, d, j, :], None).then_inc(sc, 16)
                pool.wait_ge(sc, (g + 1) * (2 * GT * 16))
                c.alone(pool)
            for d, (tab, col) in enumerate(((c.t1, 0), (c.t2, 1))):
                pool.indirect_dma_start(first[:, d, :], None, tab,
                                        bass.IndirectOffsetOnAxis(ap=c.rec[:, d, 0, col:col + 1], axis=0)).then_inc(fg, 16)
            pool.wait_ge(fg, 32)

        @block.vector
        def _(v):
            v.wait_ge(rl, 32)
            for d in range(2):
                k = c.rec[:, d, :, d]
                nc.vector.memset(c.sep[:, d, 0:1], 0.0)
                nc.vector.tensor_tensor(c.sep[:, d, 1:T], k[:, 1:T], k[:, 0:T - 1], ALU.is_equal)
            v.wait_ge(fg, 32)
            v.wait_ge(vl, 32)
            nc.vector.tensor_copy(val[:, :, 0, :], first[:, :, 132:136])
            v.drain()
            for d in range(2):
                for h in range(4):
                    nc.vector.tensor_tensor_scan(c.ar[:, :, 4 * d + h], c.sep[:, d, :], val[:, d, :, h], 0.0,
                                                 ALU.mult, ALU.add)
            v.drain()
            nc.vector.tensor_scalar(c.sep[:], c.sep[:], 1.0, BIG, ALU.subtract, ALU.mult)
            v.drain()


def edge_pass(c, layer):
    nc, A = c.nc, c.A
    U = 2
    B1 = B + 1
    state = c.state[layer]
    with ExitStack() as s:
        sb = lambda n, shape, dt=FP32: s.enter_context(nc.sbuf_tensor(f"e{layer}_{n}", shape, dt))
        sem = c.semaphores(s, f"e{layer}_")
        pb = lambda n: s.enter_context(nc.psum_tensor(f"e{layer}_{n}", [P, 512], FP32))
        idx = sb("idx", [P, U, 2, B, 4], I32)
        if layer == 0:
            g1, g2 = sb("g1", [P, U, B, TW]), sb("g2", [P, U, B, TW])
        else:
            kv, q, ea = sb("kv", [P, U, B, 512]), sb("q", [P, U, B, D]), sb("ea", [P, U, B, D])
            ke = sb("ke", [P, B, D])
            eaT = sb("eaT", [P, 4, 2, 2, P])
            we = sb("we", [P, 2, D])
            psT = [pb(f"psT{n}") for n in range(4)]
            psE = [pb(f"psE{n}") for n in range(4)]
        sepb = sb("sepb", [P, H, B1])
        at = sb("at", [P, H, B1])
        mt = sb("mt", [P, H, B1])
        ex = sb("ex", [P, 2, H, B])
        cw = sb("cw", [P, 2, H, B1])
        den = sb("den", [P, H, B1])
        wv = sb("wv", [P, B, D])
        st = sb("st", [P, U, B, SW])
        ld, gat0, gat1, eg0, eg1, used, exd, cwd, dnd, std, act_st, so0, so1, free, dump, tp, tcp, ep, ed = (
            sem(n) for n in ("ld", "gat0", "gat1", "eg0", "eg1", "used", "exd", "cwd", "dnd", "std", "acts", "so0",
                             "so1", "free", "dump", "tp", "tcp", "ep", "ed"))
        gat, eg, so = [gat0, gat1], [eg0, eg1], [so0, so1]
        block = s.enter_context(nc.Block())
        ngat = 2 * B * 16

        @block.sync
        def _(sp):
            if layer == 1:
                sp.dma_start(we[:], A["L1_gnn_We"].rearrange("(k p) n -> p k n", p=P)).then_inc(ld, 16)
            sp.wait_ge(dump, 1)
            sp.dma_start(state[EP:EP + 1, :], st[0:1, 1, B - 1, :]).then_inc(so[1], 16)
            sp.wait_ge(so[1], 16)
            sp.sem_inc(free, 1)
            with sp.Fori(0, NBLK // U) as i:
                for u in range(U):
                    blk = i * U + u
                    sp.wait_ge(std, blk + 1)
                    sp.wait_ge(act_st, blk + 1)
                    sp.dma_start(state[0:EP, :].rearrange("(p t) w -> p (t w)", p=P)[:, bass.ds(blk * (B * SW), B * SW)],
                                 st[:, u, :, :]).then_inc(so[u], 16)
                    sp.wait_ge(so[1 - u], (i + 1) * 16)
                    sp.sem_inc(free, 1)
            sp.wait_ge(so[1], (NBLK // U + 1) * 16)

        @block.gpsimd
        def _(pool):
            pool.sem_inc(used, U)
            with pool.Fori(0, NBLK // U) as i:
                for u in range(U):
                    blk = i * U + u
                    pool.wait_ge(used, blk + 1)
                    c.alone(pool)
                    nd = 2 if layer == 0 else 1
                    for d in range(nd):
                        nc.gpsimd.tensor_copy(idx[:, u, d, :, :], c.rec[:, d, bass.ds(blk * B, B), :])
                    pool.drain()
                    at_ = lambda d, j, w: bass.IndirectOffsetOnAxis(ap=idx[:, u, d, j, w:w + 1], axis=0)
                    if layer == 1:
                        for j in range(B):
                            pool.indirect_dma_start(ea[:, u, j, :], None, A["edge_attr_256"], at_(0, j, 2)).then_inc(eg[u], 16)
                    for j in range(B):
                        if layer == 0:
                            pool.indirect_dma_start(g1[:, u, j, :], None, c.t1, at_(0, j, 1)).then_inc(gat[u], 16)
                            pool.indirect_dma_start(g2[:, u, j, :], None, c.t2, at_(1, j, 0)).then_inc(gat[u], 16)
                        else:
                            pool.indirect_dma_start(q[:, u, j, :], None, c.q, at_(0, j, 0)).then_inc(gat[u], 16)
                            pool.indirect_dma_start(kv[:, u, j, :], None, c.kv, at_(0, j, 1)).then_inc(gat[u], 16)

        @block.vector
        def _(v):
            tt, copy = nc.vector.tensor_tensor, nc.vector.tensor_copy
            nc.vector.memset(st[:, :, :, 0:MX], 0.0)
            nc.vector.memset(st[:, :, :, MX:SW], -BIG)
            nc.vector.memset(sepb[:], -BIG)
            nc.vector.memset(at[:], -BIG)
            nc.vector.memset(cw[:], 0.0)
            v.drain()
            nc.vector.memset(den[:], 0.0).then_inc(dump, 1)
            if layer == 1:
                v.sem_inc(ed, 4)
            with v.Fori(0, NBLK // U) as i:
                for u in range(U):
                    blk = i * U + u
                    for d in range(2):
                        k = d if layer == 0 else 0
                        copy(sepb[:, 4 * d:4 * d + 4, 1:B1],
                             c.sep[:, k, bass.ds(blk * B, B)].unsqueeze(1).to_broadcast([P, 4, B]))
                    if layer == 0:
                        v.wait_ge(gat[u], (i + 1) * ngat)
                        for d, g in enumerate((g1, g2)):
                            tt(at[:, 4 * d:4 * d + 4, 1:B1].rearrange("p h b -> p b h"), g[:, u, :, P:P + 4],
                               c.ar[:, bass.ds(blk * B, B), 4 * d:4 * d + 4], ALU.add)
                        v.drain()
                        nc.vector.scalar_tensor_tensor(out=at[:, :, 1:B1], in0=at[:, :, 1:B1], scalar=0.2,
                                                       in1=at[:, :, 1:B1], op0=ALU.mult, op1=ALU.max)
                    else:
                        v.wait_ge(gat[u], (i + 1) * ngat)
                        for m in range(4):
                            pair = psE[m][:, :].rearrange("p (j n) -> p j n", j=2)
                            v.wait_ge(ep, blk * 4 + m + 1)
                            tt(ke[:, 2 * m:2 * m + 2, :], kv[:, u, 2 * m:2 * m + 2, 0:D], pair, ALU.add)
                            tt(kv[:, u, 2 * m:2 * m + 2, D:2 * D], kv[:, u, 2 * m:2 * m + 2, D:2 * D], pair,
                               ALU.add).then_inc(ed, 1)
                        v.drain()
                        tt(ke[:], ke[:], q[:, u, :, :], ALU.mult)
                        v.drain()
                        nc.vector.tensor_reduce(at[:, :, 1:B1].rearrange("p h b -> p b h"),
                                                ke[:].rearrange("p b (h k) -> p b h k", k=C), AX.X, ALU.add)
                    v.drain()
                    flat = lambda a: a.rearrange("p h b -> p (h b)")
                    nc.vector.tensor_tensor_scan(flat(mt[:]), flat(sepb[:]), flat(at[:]), 0.0, ALU.add, ALU.max)
                    v.drain()
                    tt(ex[:, 0, :, :], mt[:, :, 0:B], sepb[:, :, 1:B1], ALU.add)
                    tt(ex[:, 1, :, :], at[:, :, 1:B1], mt[:, :, 1:B1], ALU.subtract)
                    v.drain()
                    copy(at[:, :, 0], mt[:, :, B])
                    tt(ex[:, 0, :, :], ex[:, 0, :, :], mt[:, :, 1:B1], ALU.subtract).then_inc(exd, 1)
                    v.wait_ge(cwd, blk + 1)
                    nc.vector.tensor_tensor_scan(flat(den[:]), flat(cw[:, 0, :, :]), flat(cw[:, 1, :, :]), 0.0,
                                                 ALU.mult, ALU.add).then_inc(dnd, 1)
                    wt = lambda h0, n: cw[:, 1, h0:h0 + n, 1:B1].rearrange("p h b -> p b h").unsqueeze(3).to_broadcast([P, B, n, C])
                    msg = lambda a: a.rearrange("p b (h k) -> p b h k", k=C)
                    if layer == 0:
                        for d, g in enumerate((g1, g2)):
                            last = tt(msg(wv[:, :, P * d:P * d + P]), msg(g[:, u, :, 0:P]), wt(4 * d, 4), ALU.mult)
                    else:
                        last = tt(msg(wv[:]), msg(kv[:, u, :, D:2 * D]), wt(0, H), ALU.mult)
                    last.then_inc(used, 1)
                    v.drain()
                    v.wait_ge(free, blk + 1)
                    copy(cw[:, 1, :, 0], den[:, :, B])
                    for t in range(B):
                        old = st[:, u, t - 1, 0:D] if t else st[:, 1 - u, B - 1, 0:D]
                        tt(st[:, u, t, 0:D].rearrange("p (h k) -> p h k", k=C), old.rearrange("p (h k) -> p h k", k=C),
                           cw[:, 0, :, 1 + t].unsqueeze(2).to_broadcast([P, H, C]), ALU.mult)
                        v.drain()
                        last = tt(st[:, u, t, 0:D], st[:, u, t, 0:D], wv[:, t, :], ALU.add)
                        if t < B - 1:
                            v.drain()
                    last.then_inc(std, 1)
                    v.wait_ge(act_st, blk + 1)
            c.alone(v)
            v.drain()
            copy(c.tail[:], st[:, 1, B - 1, :])

        @block.scalar
        def _(act):
            with act.Fori(0, NBLK // U) as i:
                for u in range(U):
                    blk = i * U + u
                    if layer == 1:
                        for m in range(4):
                            act.wait_ge(tp, blk * 4 + m + 1)
                            nc.scalar.activation(eaT[:, m, :, :, :].rearrange("p a b c -> p (a b c)"), psT[m][:, :],
                                                 ACT.Copy).then_inc(tcp, 1)
                    act.wait_ge(exd, blk + 1)
                    nc.scalar.activation(cw[:, :, :, 1:B1].rearrange("p x h b -> p (x h) b"),
                                         ex[:].rearrange("p x h b -> p (x h) b"), ACT.Exp).then_inc(cwd, 1)
                    act.wait_ge(dnd, blk + 1)
                    act.wait_ge(free, blk + 1)
                    nc.scalar.activation(st[:, u, :, MX:SW].rearrange("p b h -> p h b"), mt[:, :, 1:B1], ACT.Copy)
                    nc.scalar.activation(st[:, u, :, DEN:MX].rearrange("p b h -> p h b"), den[:, :, 1:B1],
                                         ACT.Copy).then_inc(act_st, 1)

        if layer == 1:
            @block.tensor
            def _(pe):
                pe.wait_ge(ld, 16)
                with pe.Fori(0, NBLK // U) as i:
                    for u in range(U):
                        blk = i * U + u
                        pe.wait_ge(eg[u], (i + 1) * (B * 16))

                        def turn(m):
                            for j in range(2):
                                for k in range(2):
                                    o = (2 * j + k) * P
                                    last = nc.tensor.transpose(psT[m][:, o:o + P], ea[:, u, 2 * m + j, k * P:(k + 1) * P],
                                                               c.ident[:])
                            last.then_inc(tp, 1)

                        def product(m):
                            pe.wait_ge(tcp, blk * 4 + m + 1)
                            pe.wait_ge(ed, blk * 4 + m + 1)
                            for j in range(2):
                                for k in range(2):
                                    last = nc.tensor.matmul(psE[m][:, j * D:(j + 1) * D], eaT[:, m, j, k, :], we[:, k, :],
                                                            start=(k == 0), stop=(k == 1))
                            last.then_inc(ep, 1)

                        turn(0)
                        turn(1)
                        product(0)
                        turn(2)
                        product(1)
                        turn(3)
                        product(2)
                        product(3)


def join_tails(c, layer):
    nc = c.nc
    nd = 2 if layer == 0 else 1
    hd = H // nd
    wd = hd * C
    with ExitStack() as s:
        sb = lambda n, shape, dt=FP32: s.enter_context(nc.sbuf_tensor(f"j{layer}_{n}", shape, dt))
        sem = c.semaphores(s, f"j{layer}_")
        pb = lambda n: s.enter_context(nc.psum_tensor(f"j{layer}_{n}", [P, 512], FP32))
        nxt = sb("nxt", [P, nd], I32)
        last, opened, key, first, before = (sb(n, [P, nd]) for n in ("last", "open", "key", "first", "before"))
        same, pen = sb("same", [P, nd, P]), sb("pen", [P, nd, P])
        junk = sb("junk", [P, nd, P])
        mrow = sb("mrow", [P, H, P])
        top, fac = sb("top", [P, H]), sb("fac", [P, H])
        scaled = sb("scaled", [P, nd, wd + hd])
        psK = [pb("psK0"), pb("psK1")]
        psM = [pb("psM0"), pb("psM1")]
        psG = [pb("psG0"), pb("psG1")]
        nz, nl, kd, kr, mr, xd, fd, sd, gd = (sem(n) for n in ("nz", "nl", "kd", "kr", "mr", "xd", "fd", "sd", "gd"))
        block = s.enter_context(nc.Block())

        @block.sync
        def _(sp):
            sp.wait_ge(nz, 1)
            for d, rec in enumerate((c.rec_d, c.rec_s)[0:nd]):
                with nc.allow_non_contiguous_dma("one word of each partition's first record"):
                    sp.dma_start(nxt[0:P - 1, d:d + 1],
                                 rec.rearrange("(p t) w -> p t w", t=T)[1:P, 0, d:d + 1]).then_inc(nl, 16)
            sp.wait_ge(nl, 16 * nd)

        @block.vector
        def _(v):
            tt, ts, copy = nc.vector.tensor_tensor, nc.vector.tensor_scalar, nc.vector.tensor_copy
            nc.vector.memset(nxt[:], -1).then_inc(nz, 1)
            for d in range(nd):
                copy(last[:, d:d + 1], c.rec[:, d, T - 1, d:d + 1])
            v.wait_ge(nl, 16 * nd)
            v.drain()
            tt(opened[:], last[:], nxt[:], ALU.is_equal)
            ts(last[:], last[:], 1.0, None, ALU.add)
            v.drain()
            tt(key[:], last[:], opened[:], ALU.mult)
            v.drain()
            ts(key[:], key[:], 1.0, None, ALU.subtract)
            v.drain()
            copy(junk[:, 0, 0:nd], key[:]).then_inc(kd, 1)
            v.wait_ge(kr, 1)
            for d in range(nd):
                ts(same[:, d, :], psK[d][:, 0:P], key[:, d:d + 1], None, ALU.is_equal)
            v.drain()
            for d in range(nd):
                nc.vector.scalar_tensor_tensor(out=junk[:, d, :], in0=same[:, d, :], scalar=1.0, in1=c.tri[:],
                                               op0=ALU.mult, op1=ALU.mult, accum_out=before[:, d:d + 1])
            ts(pen[:], same[:], 1.0, BIG, ALU.subtract, ALU.mult)
            v.drain()
            ts(first[:], before[:], 0.5, None, ALU.is_lt)
            v.wait_ge(mr, 1)
            for h in range(H):
                tt(mrow[:, h, :], psM[h // 4][:, (h % 4) * P:(h % 4 + 1) * P], pen[:, h // hd, :], ALU.add)
            v.drain()
            tt(first[:], first[:], opened[:], ALU.mult)
            nc.vector.tensor_reduce(top[:], mrow[:], AX.X, ALU.max)
            v.drain()
            tt(first[:], first[:], last[:], ALU.mult)
            tt(fac[:], c.tail[:, MX:SW], top[:], ALU.subtract).then_inc(xd, 1)
            v.drain()
            ts(c.fkey[:, 0:nd], first[:], 1.0, None, ALU.subtract)
            v.wait_ge(fd, 1)
            for d in range(nd):
                tt(scaled[:, d, 0:wd].rearrange("p (h k) -> p h k", k=C),
                   c.tail[:, d * wd:(d + 1) * wd].rearrange("p (h k) -> p h k", k=C),
                   fac[:, d * hd:(d + 1) * hd].unsqueeze(2).to_broadcast([P, hd, C]), ALU.mult)
                op = tt(scaled[:, d, wd:wd + hd], c.tail[:, DEN + d * hd:DEN + (d + 1) * hd],
                        fac[:, d * hd:(d + 1) * hd], ALU.mult)
            op.then_inc(sd, 1)
            v.wait_ge(gd, 1)
            g = c.carry[:, 0:nd * (wd + 2 * hd + 1)].rearrange("p (d w) -> p d w", d=nd)
            for d in range(nd):
                copy(g[:, d, 0:wd + hd], psG[d][:, 0:wd + hd])
                copy(g[:, d, wd + hd:wd + 2 * hd], top[:, d * hd:(d + 1) * hd])
            nc.vector.memset(g[:, :, wd + 2 * hd:wd + 2 * hd + 1], 1.0)
            v.drain()

        @block.scalar
        def _(act):
            act.wait_ge(xd, 1)
            nc.scalar.activation(fac[:], fac[:], ACT.Exp).then_inc(fd, 1)

        @block.tensor
        def _(pe):
            for h in range(H):
                op = nc.tensor.matmul(psM[h // 4][:, (h % 4) * P:(h % 4 + 1) * P],
                                      c.tail[:, MX + h:MX + h + 1].to_broadcast([P, P]), c.ident[:], start=True, stop=True)
            op.then_inc(mr, 1)
            pe.wait_ge(kd, 1)
            for d in range(nd):
                op = nc.tensor.matmul(psK[d][:, 0:P], key[:, d:d + 1].to_broadcast([P, P]), c.ident[:], start=True, stop=True)
            op.then_inc(kr, 1)
            pe.wait_ge(sd, 1)
            for d in range(nd):
                op = nc.tensor.matmul(psG[d][:, 0:wd + hd], same[:, d, :], scaled[:, d, :], start=True, stop=True)
            op.then_inc(gd, 1)


def combine(c, layer):
    nc, A = c.nc, c.A
    nd = 2 if layer == 0 else 1
    hd = H // nd
    wd = hd * C
    wc = wd + 2 * hd + 1
    parts = 3 if layer == 0 else 2
    with ExitStack() as s:
        sb = lambda n, shape, dt=FP32: s.enter_context(nc.sbuf_tensor(f"c{layer}_{n}", shape, dt))
        sem = c.semaphores(s, f"c{layer}_")
        pb = lambda n: s.enter_context(nc.psum_tensor(f"c{layer}_{n}", [P, 512], FP32))
        endn = sb("endn", [P, nd, NI], I32)
        idx = sb("idx", [P, nd, GT], I32)
        r = sb("r", [P, nd, GT, SW])
        nrow = sb("nrow", [P, P])
        oh = sb("oh", [P, nd, GT, P])
        cc = sb("cc", [P, nd, GT, wc])
        own = sb("own", [P, 2, GT, TW])
        top = sb("top", [P, nd, GT, hd])
        mc = sb("mc", [P, nd, GT, hd])
        eself = sb("eself", [P, nd, GT, hd])
        xa = sb("xa", [P, nd, parts, GT, hd])
        dsum, dtmp = sb("dsum", [P, nd, GT, hd]), sb("dtmp", [P, nd, parts, GT, hd])
        pres = sb("pres", [P, nd, GT])
        num, tmp = sb("num", [P, GT, D]), sb("tmp", [P, GT, D])
        psC = [pb("psC0"), pb("psC1")]
        ld, gat, tl, ohd, cm, ccd, xd, fd, used, tr, tc, mm, fs = (sem(n) for n in (
            "ld", "gat", "tl", "ohd", "cm", "ccd", "xd", "fd", "used", "tr", "tc", "mm", "fs"))
        catd = sem("catd")
        if layer == 0:
            cT = sb("cT", [P, 2, GT * P])
            wf = sb("wf", [P, 2, D])
            vec = sb("vec", [P, 6, D])
            psT, psF = [pb("psT0"), pb("psT1")], [pb("psF0"), pb("psF1")]
        nld = 16 * (nd + (8 if layer == 0 else 0))
        block = s.enter_context(nc.Block())

        @block.sync
        def _(sp):
            for d in range(nd):
                sp.dma_start(endn[:, d, :], c.ends[d][1][0:NI * P].rearrange("(p i) -> p i", i=NI)).then_inc(ld, 16)
            if layer == 0:
                sp.dma_start(wf[:], A["L0_gnn_W_fuse"].rearrange("(k p) n -> p k n", p=P)).then_inc(ld, 16)
                sp.dma_start(vec[:, 0, 0:P], row_bcast(A["L0_gnn_b_f"], 0, P)).then_inc(ld, 16)
                sp.dma_start(vec[:, 0, P:D], row_bcast(A["L0_gnn_b_b"], 0, P)).then_inc(ld, 16)
                for n, name in enumerate(("b_fuse", "run_mean", "run_var", "gamma", "beta")):
                    sp.dma_start(vec[:, 1 + n, :], row_bcast(A["L0_gnn_" + name], 0, D)).then_inc(ld, 16)
                with sp.Fori(0, NG) as g:
                    sp.wait_ge(used, g + 1)
                    for d, tab in enumerate((c.t1, c.t2)):
                        sp.dma_start(own[:, d, :, :],
                                     tab.rearrange("(p i) w -> p (i w)", i=NI)[:, bass.ds(g * (GT * TW), GT * TW)]).then_inc(tl, 16)

        @block.gpsimd
        def _(pool):
            pool.wait_ge(ld, nld)
            with pool.Fori(0, NG) as g:
                pool.wait_ge(used, g + 1)
                c.alone(pool)
                nc.gpsimd.tensor_copy(idx[:], endn[:, :, bass.ds(g * GT, GT)])
                pool.drain()
                for d in range(nd):
                    for j in range(GT):
                        pool.indirect_dma_start(r[:, d, j, :], None, c.state[layer],
                                                bass.IndirectOffsetOnAxis(ap=idx[:, d, j:j + 1], axis=0)).then_inc(gat, 16)

        @block.vector
        def _(v):
            tt, ts, copy = nc.vector.tensor_tensor, nc.vector.tensor_scalar, nc.vector.tensor_copy
            v.sem_inc(used, 1)
            v.wait_ge(ld, nld)
            ts(nrow[:], c.cols[:], float(NI), None, ALU.mult)
            if layer == 0:
                ts(vec[:, 3, :], vec[:, 3, :], BN_EPS, None, ALU.add).then_inc(xd, 1)
                v.wait_ge(fd, 1)
                nc.vector.reciprocal(vec[:, 3, :], vec[:, 3, :])
                tt(vec[:, 1, :], vec[:, 1, :], vec[:, 2, :], ALU.subtract)
                v.drain()
                tt(vec[:, 4, :], vec[:, 4, :], vec[:, 3, :], ALU.mult)
                v.drain()
                tt(vec[:, 1, :], vec[:, 1, :], vec[:, 4, :], ALU.mult)
                v.drain()
                tt(vec[:, 5, :], vec[:, 5, :], vec[:, 1, :], ALU.add)
            x0 = 1 if layer == 0 else 0
            v.drain()
            with v.Fori(0, NG) as g:
                for d in range(nd):
                    for j in range(GT):
                        last = ts(oh[:, d, j, :], nrow[:], float(j), c.fkey[:, d:d + 1], ALU.add, ALU.is_equal)
                last.then_inc(ohd, 1)
                v.drain()
                ts(nrow[:], nrow[:], float(GT), None, ALU.add)
                v.wait_ge(ccd, (g + 1) * (nd * GT))
                v.wait_ge(gat, (g + 1) * (nd * GT * 16))
                if layer == 0:
                    v.wait_ge(tl, (g + 1) * 32)
                ts(pres[:], cc[:, :, :, wc - 1], 1.0, BIG, ALU.subtract, ALU.mult)
                if layer == 0:
                    tt(eself[:], own[:, :, :, 128:132], own[:, :, :, 132:136], ALU.add)
                v.drain()
                for d in range(nd):
                    tt(mc[:, d], cc[:, d, :, wd + hd:wd + 2 * hd], pres[:, d, :].unsqueeze(2).to_broadcast([P, GT, hd]), ALU.add)
                    if layer == 0:
                        nc.vector.scalar_tensor_tensor(out=eself[:, d], in0=eself[:, d], scalar=0.2, in1=eself[:, d],
                                                       op0=ALU.mult, op1=ALU.max)
                v.drain()
                for d in range(nd):
                    tt(top[:, d], mc[:, d], r[:, d, :, MX + d * hd:MX + (d + 1) * hd], ALU.max)
                v.drain()
                if layer == 0:
                    tt(top[:], top[:], eself[:], ALU.max)
                    v.drain()
                for d in range(nd):
                    tt(xa[:, d, 0], r[:, d, :, MX + d * hd:MX + (d + 1) * hd], top[:, d], ALU.subtract)
                    last = tt(xa[:, d, 1], mc[:, d], top[:, d], ALU.subtract)
                    if layer == 0:
                        last = tt(xa[:, d, 2], eself[:, d], top[:, d], ALU.subtract)
                last.then_inc(xd, 1)
                v.wait_ge(fd, g + 1 + x0)
                for d in range(nd):
                    tt(dtmp[:, d, 0], r[:, d, :, DEN + d * hd:DEN + (d + 1) * hd], xa[:, d, 0], ALU.mult)
                    tt(dtmp[:, d, 1], cc[:, d, :, wd:wd + hd], xa[:, d, 1], ALU.mult)
                v.drain()
                tt(dsum[:], dtmp[:, :, 0], dtmp[:, :, 1], ALU.add)
                v.drain()
                if layer == 0:
                    tt(dsum[:], dsum[:], xa[:, :, 2], ALU.add)
                    v.drain()
                    ts(dsum[:], dsum[:], 1e-16, None, ALU.add)
                else:
                    ts(dsum[:], dsum[:], 1e-30, None, ALU.max)
                v.drain()
                nc.vector.reciprocal(dsum[:], dsum[:])
                v.drain()
                for d in range(nd):
                    for n in range(parts):
                        tt(xa[:, d, n], xa[:, d, n], dsum[:, d], ALU.mult)
                v.drain()
                hk = lambda a: a.rearrange("p i (h k) -> p i h k", k=C)
                for n in range(parts):
                    for d in range(nd):
                        src = (r[:, d, :, d * wd:(d + 1) * wd], cc[:, d, :, 0:wd], own[:, d, :, 0:wd] if layer == 0 else None)[n]
                        dst = num if n == 0 else tmp
                        tt(hk(dst[:, :, d * wd:(d + 1) * wd]), hk(src),
                           xa[:, d, n].unsqueeze(3).to_broadcast([P, GT, hd, C]), ALU.mult)
                    v.drain()
                    if n:
                        tt(num[:], num[:], tmp[:], ALU.add)
                        v.drain()
                xg = c.x[:, bass.ds(g * (GT * D), GT * D)]
                flat = lambda a: a.rearrange("p i d -> p (i d)")
                if layer == 0:
                    tt(num[:], num[:], vec[:, 0, :].unsqueeze(1).to_broadcast([P, GT, D]), ALU.add).then_inc(catd, 1)
                    v.sem_inc(used, 1)
                    for j in range(GT):
                        v.wait_ge(mm, g * GT + j + 1)
                        tt(tmp[:, j, :], psF[j % 2][:, 0:D], vec[:, 4, :], ALU.mult).then_inc(fs, 1)
                    v.drain()
                    tt(tmp[:], tmp[:], vec[:, 5, :].unsqueeze(1).to_broadcast([P, GT, D]), ALU.add)
                    v.drain()
                    nc.vector.scalar_tensor_tensor(out=xg, in0=flat(tmp[:]), scalar=0.0, in1=xg, op0=ALU.max, op1=ALU.add)
                else:
                    tt(xg, xg, flat(num[:]), ALU.add).then_inc(used, 1)
                v.drain()

        @block.scalar
        def _(act):
            if layer == 0:
                act.wait_ge(xd, 1)
                nc.scalar.activation(vec[:, 3, :], vec[:, 3, :], ACT.Sqrt).then_inc(fd, 1)
            x0 = 1 if layer == 0 else 0
            with act.Fori(0, NG) as g:
                for n in range(nd * GT):
                    act.wait_ge(cm, g * (nd * GT) + n + 1)
                    nc.scalar.activation(cc[:, n // GT, n % GT, :], psC[n % 2][:, 0:wc], ACT.Copy).then_inc(ccd, 1)
                act.wait_ge(xd, g + 1 + x0)
                nc.scalar.activation(xa[:].rearrange("p a b i h -> p (a b i h)"),
                                     xa[:].rearrange("p a b i h -> p (a b i h)"), ACT.Exp).then_inc(fd, 1)
                if layer == 0:
                    for j in range(GT):
                        act.wait_ge(tr, g * GT + j + 1)
                        nc.scalar.activation(cT[:, :, j * P:(j + 1) * P],
                                             psT[j % 2][:, 0:2 * P].rearrange("p (k n) -> p k n", k=2), ACT.Copy).then_inc(tc, 1)

        @block.tensor
        def _(pe):
            pe.wait_ge(ld, nld)
            with pe.Fori(0, NG) as g:
                pe.wait_ge(ohd, g + 1)
                for n in range(nd * GT):
                    if n >= 2:
                        pe.wait_ge(ccd, g * (nd * GT) + n - 1)
                    nc.tensor.matmul(psC[n % 2][:, 0:wc], oh[:, n // GT, n % GT, :],
                                     c.carry[:, (n // GT) * wc:(n // GT + 1) * wc], start=True, stop=True).then_inc(cm, 1)
                if layer == 0:
                    pe.wait_ge(catd, g + 1)
                    for j in range(GT):
                        if j >= 2:
                            pe.wait_ge(tc, g * GT + j - 1)
                        for k in range(2):
                            last = nc.tensor.transpose(psT[j % 2][:, k * P:(k + 1) * P], num[:, j, k * P:(k + 1) * P], c.ident[:])
                        last.then_inc(tr, 1)
                    for j in range(GT):
                        pe.wait_ge(tc, g * GT + j + 1)
                        if j >= 2:
                            pe.wait_ge(fs, g * GT + j - 1)
                        for k in range(2):
                            last = nc.tensor.matmul(psF[j % 2][:, 0:D], cT[:, k, j * P:(j + 1) * P], wf[:, k, :],
                                                    start=(k == 0), stop=(k == 1))
                        last.then_inc(mm, 1)
                pe.wait_ge(ccd, (g + 1) * (nd * GT))


def normalize_group(c, v, w, xln, g, vin, root, xr):
    layernorm_stats(c, v, w, lambda j: c.x[:, bass.ds((g * GT + j) * D, D)], GT, vin, root, g + 1)
    for j in range(GT):
        c.nc.vector.tensor_scalar(xln[:, j, 0:D], c.x[:, bass.ds((g * GT + j) * D, D)], w["mv"][:, j, 0:1],
                                  w["rstd"][:, j:j + 1], ALU.subtract, ALU.mult).then_inc(xr, 1)


def root_and_copies(c, act, w, g, vin, root, tr, tc, psT, xT):
    act.wait_ge(vin, g + 1)
    c.nc.scalar.activation(w["rstd"][:], w["rstd"][:], ACT.Sqrt).then_inc(root, 1)
    for j in range(GT):
        act.wait_ge(tr, g * GT + j + 1)
        c.nc.scalar.activation(xT[:, :, j * P:(j + 1) * P], psT[j % 2][:, 0:2 * P].rearrange("p (k n) -> p k n", k=2),
                               ACT.Copy).then_inc(tc, 1)


def transposes(c, pe, xln, g, xr, tr, tc, psT):
    for j in range(GT):
        pe.wait_ge(xr, g * GT + j + 1)
        if j >= 2:
            pe.wait_ge(tc, g * GT + j - 1)
        for k in range(2):
            last = c.nc.tensor.transpose(psT[j % 2][:, k * P:(k + 1) * P], xln[:, j, k * P:(k + 1) * P], c.ident[:])
        last.then_inc(tr, 1)


def experts(c):
    nc, A = c.nc, c.A
    HC = HID // P
    halves = ((0, 4), (4, 3))
    with ExitStack() as s:
        sb = lambda n, shape, dt=FP32: s.enter_context(nc.sbuf_tensor("m_" + n, shape, dt))
        sem = c.semaphores(s, "m_")
        pb = lambda n: s.enter_context(nc.psum_tensor("m_" + n, [P, 512], FP32))
        w1, w2 = sb("w1", [P, EXP, 2, HID]), sb("w2", [P, EXP, HC, D])
        wg, bg = sb("wg", [P, 2, EXP]), sb("bg", [P, EXP])
        b1, b2 = sb("b1", [P, EXP, HC]), sb("b2", [EXP, D])
        w = {"stats": sb("st", [P, GT, 6]), "mv": sb("mv", [P, GT, 2]), "rstd": sb("rs", [P, GT])}
        xln, xT = sb("xln", [P, GT, D]), sb("xT", [P, 2, GT * P])
        hT = sb("hT", [P, 2, HC, 512])
        gate, rank, mask = sb("gate", [P, GT, EXP]), sb("rank", [P, GT, EXP]), sb("mask", [P, GT, EXP])
        gt, eq = sb("gt", [P, GT, EXP, EXP]), sb("eq", [P, GT, EXP, EXP])
        lower = sb("lower", [P, EXP, EXP])
        maskT = sb("maskT", [EXP, GT * P])
        psM = [pb("psM0"), pb("psM1")]
        psH = [pb(f"psH{n}") for n in range(HC)]
        psY = [pb("psY0"), pb("psY1")]
        ld, lw, vin, root, xr, tr, tc, gd, md, mt_, mc, bt, ba, hp, gelud, yd, ya, gfree = (sem(n) for n in (
            "ld", "lw", "vin", "root", "xr", "tr", "tc", "gd", "md", "mt", "mc", "bt", "ba", "hp", "gelud", "yd", "ya", "gfree"))
        block = s.enter_context(nc.Block())

        @block.sync
        def _(sp):
            sp.dma_start(wg[:], A["L0_ffn_Wg"].rearrange("(k p) n -> p k n", p=P)).then_inc(ld, 16)
            sp.dma_start(bg[:], row_bcast(A["L0_ffn_bg"], 0, EXP)).then_inc(ld, 16)
            sp.dma_start(b2[:], A["L0_ffn_b2"]).then_inc(ld, 16)
            with nc.allow_non_contiguous_dma("biases one word per partition"):
                for e in range(EXP):
                    sp.dma_start(b1[:, e, :], A["L0_ffn_b1"][e, :].rearrange("(k p) -> p k", p=P)).then_inc(ld, 16)
            for e in range(EXP):
                sp.dma_start(w1[:, e, :, :], A["L0_ffn_W1"][e].rearrange("(k p) n -> p k n", p=P)).then_inc(ld, 16)
                sp.dma_start(w2[:, e, :, :], A["L0_ffn_W2"][e].rearrange("(k p) n -> p k n", p=P)).then_inc(ld, 16)
            sp.wait_ge(ld, 16 * (3 + 3 * EXP))

        @block.gpsimd
        def _(pool):
            nc.gpsimd.memset(lower[:], 1.0)
            pool.drain()
            nc.gpsimd.affine_select(out=lower[:], in_=lower[:], compare_op=ALU.is_gt, fill=0.0, base=0,
                                    pattern=[[1, EXP], [-1, EXP]], channel_multiplier=0).then_inc(lw, 1)

        @block.vector
        def _(v):
            tt, ts = nc.vector.tensor_tensor, nc.vector.tensor_scalar
            v.wait_ge(lw, 1)
            v.wait_ge(ld, 16 * (3 + 3 * EXP))
            v.sem_inc(ya, 2)
            with v.Fori(0, NG) as g:
                normalize_group(c, v, w, xln, g, vin, root, xr)
                v.wait_ge(gd, g + 1)
                tt(gate[:], psM[0][:, 0:GT * EXP].rearrange("p (i e) -> p i e", e=EXP),
                   bg[:].unsqueeze(1).to_broadcast([P, GT, EXP]), ALU.add)
                v.drain()
                gj = gate[:].unsqueeze(2).to_broadcast([P, GT, EXP, EXP])
                gi = gate[:].unsqueeze(3).to_broadcast([P, GT, EXP, EXP])
                tt(gt[:], gj, gi, ALU.is_gt)
                tt(eq[:], gj, gi, ALU.is_equal)
                v.drain()
                tt(eq[:], eq[:], lower[:].unsqueeze(1).to_broadcast([P, GT, EXP, EXP]), ALU.mult)
                v.drain()
                tt(gt[:], gt[:], eq[:], ALU.add)
                v.drain()
                nc.vector.tensor_reduce(rank[:], gt[:], AX.X, ALU.add)
                v.drain()
                ts(mask[:], rank[:], 1.5, None, ALU.is_lt).then_inc(md, 1)
                v.drain()
                for j in range(GT):
                    v.wait_ge(bt, g * GT + j + 1)
                    xj = c.x[:, bass.ds((g * GT + j) * D, D)]
                    tt(xj, psM[j % 2][:, 0:D], xj, ALU.add).then_inc(ba, 1)
                v.drain()
                for e in range(EXP):
                    for t0, n in halves:
                        for t in range(t0, t0 + n):
                            y = e * GT + t
                            v.wait_ge(yd, g * (EXP * GT) + y + 1)
                            xj = c.x[:, bass.ds((g * GT + t) * D, D)]
                            nc.vector.scalar_tensor_tensor(out=xj, in0=psY[y % 2][:, 0:D], scalar=mask[:, t, e:e + 1],
                                                           in1=xj, op0=ALU.mult, op1=ALU.add).then_inc(ya, 1)
                        v.drain()

        @block.scalar
        def _(act):
            act.wait_ge(ld, 16 * (3 + 3 * EXP))
            with act.Fori(0, NG) as g:
                root_and_copies(c, act, w, g, vin, root, tr, tc, psM, xT)
                for q in range(2):
                    act.wait_ge(mt_, g * 2 + q + 1)
                    t0, n = halves[q]
                    nc.scalar.activation(maskT[:, t0 * P:(t0 + n) * P], psM[q][0:EXP, 0:n * P], ACT.Copy).then_inc(mc, 1)
                for u in range(2 * EXP):
                    n = halves[u % 2][1] * P
                    for k in range(HC):
                        act.wait_ge(hp, (g * (2 * EXP) + u) * HC + k + 1)
                        nc.scalar.activation(hT[:, u % 2, k, 0:n], psH[k][:, 0:n], ACT.Gelu,
                                             bias=b1[:, u // 2, k:k + 1]).then_inc(gelud, 1)

        @block.tensor
        def _(pe):
            mm = nc.tensor.matmul
            pe.wait_ge(ld, 16 * (3 + 3 * EXP))
            pe.sem_inc(gelud, HC)
            with pe.Fori(0, NG) as g:
                transposes(c, pe, xln, g, xr, tr, tc, psM)
                pe.wait_ge(tc, (g + 1) * GT)
                for j in range(GT):
                    for k in range(2):
                        last = mm(psM[0][:, j * EXP:(j + 1) * EXP], xT[:, k, j * P:(j + 1) * P], wg[:, k, :],
                                  start=(k == 0), stop=(k == 1))
                last.then_inc(gd, 1)
                pe.wait_ge(md, g + 1)
                for q, (t0, n) in enumerate(halves):
                    for j in range(n):
                        last = nc.tensor.transpose(psM[q][0:EXP, j * P:(j + 1) * P], mask[:, t0 + j, :], c.ident[:])
                    last.then_inc(mt_, 1)
                pe.wait_ge(mc, g * 2 + 2)
                for j in range(GT):
                    if j >= 2:
                        pe.wait_ge(ba, g * GT + j - 1)
                    mm(psM[j % 2][:, 0:D], maskT[:, j * P:(j + 1) * P], b2[:], start=True, stop=True).then_inc(bt, 1)

                def hidden(u):
                    t0, n = halves[u % 2]
                    for k in range(HC):
                        pe.wait_ge(gelud, (g * (2 * EXP) + u) * HC + k + 1)
                        for q in range(2):
                            last = mm(psH[k][:, 0:n * P], w1[:, u // 2, q, k * P:(k + 1) * P],
                                      xT[:, q, t0 * P:(t0 + n) * P], start=(q == 0), stop=(q == 1))
                        last.then_inc(hp, 1)

                def output(u):
                    t0, n = halves[u % 2]
                    pe.wait_ge(gelud, (g * (2 * EXP) + u) * HC + 2 * HC)
                    for t in range(t0, t0 + n):
                        y = (u // 2) * GT + t
                        pe.wait_ge(ya, g * (EXP * GT) + y + 1)
                        for k in range(HC):
                            last = mm(psY[y % 2][:, 0:D], hT[:, u % 2, k, (t - t0) * P:(t - t0 + 1) * P], w2[:, u // 2, k, :],
                                      start=(k == 0), stop=(k == HC - 1))
                        last.then_inc(yd, 1)

                hidden(0)
                for u in range(1, 2 * EXP):
                    hidden(u)
                    output(u - 1)
                output(2 * EXP - 1)
                pe.wait_ge(ba, (g + 1) * GT)


def layer1_tables(c):
    nc, A = c.nc, c.A
    with ExitStack() as s:
        sb = lambda n, shape, dt=FP32: s.enter_context(nc.sbuf_tensor("q_" + n, shape, dt))
        sem = c.semaphores(s, "q_")
        pb = lambda n: s.enter_context(nc.psum_tensor("q_" + n, [P, 512], FP32))
        wall, ball = sb("w", [P, 2, 4 * D]), sb("b", [P, 4 * D])
        w = {"stats": sb("st", [P, GT, 6]), "mv": sb("mv", [P, GT, 2]), "rstd": sb("rs", [P, GT])}
        xln, xT = sb("xln", [P, GT, D]), sb("xT", [P, 2, GT * P])
        qrow, kvrow, srow = sb("qrow", [P, GT, D]), sb("kvrow", [P, GT, 2 * D]), sb("srow", [P, GT, D])
        psT = [pb("psT0"), pb("psT1")]
        psO = [[pb(f"psO{r}{n}") for n in range(2)] for r in range(2)]
        ld, vin, root, xr, tr, tc, mm, od, rows, st = (sem(n) for n in (
            "ld", "vin", "root", "xr", "tr", "tc", "mm", "od", "rows", "st"))
        block = s.enter_context(nc.Block())

        @block.sync
        def _(sp):
            for n, (wn, bn) in enumerate((("Wq", "bq"), ("Wk", "bk"), ("Wv", "bv"), ("Ws", "bs"))):
                sp.dma_start(wall[:, :, n * D:(n + 1) * D], A["L1_gnn_" + wn].rearrange("(k p) n -> p k n", p=P)).then_inc(ld, 16)
                sp.dma_start(ball[:, n * D:(n + 1) * D], row_bcast(A["L1_gnn_" + bn], 0, D)).then_inc(ld, 16)
            with sp.Fori(0, NG) as g:
                sp.wait_ge(rows, g + 1)
                sp.dma_start(c.q.rearrange("(p i) w -> p (i w)", i=NI)[:, bass.ds(g * (GT * D), GT * D)], qrow[:]).then_inc(st, 16)
                sp.dma_start(c.kv.rearrange("(p i) w -> p (i w)", i=NI)[:, bass.ds(g * (2 * GT * D), 2 * GT * D)],
                             kvrow[:]).then_inc(st, 16)
            sp.wait_ge(st, 32 * NG)

        @block.vector
        def _(v):
            tt = nc.vector.tensor_tensor
            v.wait_ge(ld, 128)
            with v.Fori(0, NG) as g:
                normalize_group(c, v, w, xln, g, vin, root, xr)
                for j in range(GT):
                    v.wait_ge(mm, g * GT + j + 1)
                    o = psO[j % 2]
                    tt(qrow[:, j, :], o[0][:, 0:D], ball[:, 0:D], ALU.add)
                    tt(kvrow[:, j, 0:D], o[0][:, D:2 * D], ball[:, D:2 * D], ALU.add)
                    tt(kvrow[:, j, D:2 * D], o[1][:, 0:D], ball[:, 2 * D:3 * D], ALU.add)
                    tt(srow[:, j, :], o[1][:, D:2 * D], ball[:, 3 * D:4 * D], ALU.add).then_inc(od, 1)
                v.drain()
                nc.vector.tensor_scalar(qrow[:], qrow[:], float(C) ** -0.5, None, ALU.mult).then_inc(rows, 1)
                xg = c.x[:, bass.ds(g * (GT * D), GT * D)]
                tt(xg, xg, srow[:].rearrange("p i d -> p (i d)"), ALU.add)
                v.drain()
                v.wait_ge(st, (g + 1) * 32)

        @block.scalar
        def _(act):
            with act.Fori(0, NG) as g:
                root_and_copies(c, act, w, g, vin, root, tr, tc, psT, xT)

        @block.tensor
        def _(pe):
            pe.wait_ge(ld, 128)
            with pe.Fori(0, NG) as g:
                transposes(c, pe, xln, g, xr, tr, tc, psT)
                for j in range(GT):
                    pe.wait_ge(tc, g * GT + j + 1)
                    if j >= 2:
                        pe.wait_ge(od, g * GT + j - 1)
                    for n in range(2):
                        for k in range(2):
                            last = nc.tensor.matmul(psO[j % 2][n][:, :], xT[:, k, j * P:(j + 1) * P],
                                                    wall[:, k, n * 512:(n + 1) * 512], start=(k == 0), stop=(k == 1))
                    last.then_inc(mm, 1)
                pe.wait_ge(od, (g + 1) * GT)


def reload_edges(c):
    nc = c.nc
    with ExitStack() as s:
        rl = s.enter_context(nc.semaphore("r_ld"))
        block = s.enter_context(nc.Block())

        @block.sync
        def _(sp):
            sp.dma_start(c.rec[:, 0, :, :], c.rec_d.rearrange("(p t) w -> p t w", p=P)).then_inc(rl, 16)
            sp.wait_ge(rl, 16)

        @block.vector
        def _(v):
            v.wait_ge(rl, 16)
            k = c.rec[:, 0, :, 0]
            nc.vector.memset(c.sep[:, 0, 0:1], 0.0)
            nc.vector.tensor_tensor(c.sep[:, 0, 1:T], k[:, 1:T], k[:, 0:T - 1], ALU.is_equal)
            v.drain()
            nc.vector.tensor_scalar(c.sep[:], c.sep[:], 1.0, BIG, ALU.subtract, ALU.mult)
            v.drain()


SH, SG, SC = 8, 64, 64
SQ = SH * SG // P


def slice_attention(c):
    nc, A = c.nc, c.A
    ones = D
    XW = D + 1
    with ExitStack() as s:
        sb = lambda n, shape, dt=FP32: s.enter_context(nc.sbuf_tensor("f_" + n, shape, dt))
        sem = c.semaphores(s, "f_")
        wx, wfx = sb("wx", [P, 2, 512]), sb("wfx", [P, 2, 512])
        wsl, wqkv = sb("wsl", [SC, SG]), sb("wqkv", [SC, 3, SC])
        wout = sb("wout", [SC, SH, D])
        bx = sb("bx", [SC, SH])
        bsl, bfx, bout, temp = sb("bsl", [P, SG]), sb("bfx", [SG, 512]), sb("bout", [P, D]), sb("temp", [P, SH])
        wxT = sb("wxT", [SC, SH, 2, P])
        wc, bc = sb("wc", [P, 2, 512]), sb("bc", [P, 512])
        with ExitStack() as s1:
            psA = [s1.enter_context(nc.psum_tensor(f"f1_psA{n}", [P, 512], FP32)) for n in range(4)]
            psW = [s1.enter_context(nc.psum_tensor(f"f1_psW{n}", [P, 512], FP32)) for n in range(2)]
            psB = s1.enter_context(nc.psum_tensor("f1_psB", [P, 512], FP32))
            ld, t1, t1c, w1, td = (sem(n) for n in ("ld", "t1", "t1c", "w1", "td"))
            block = s1.enter_context(nc.Block())

            @block.sync
            def _(sp):
                f = "L1_ffn_"
                sp.dma_start(wx[:], A[f + "W_x"].rearrange("(k p) n -> p k n", p=P)).then_inc(ld, 16)
                sp.dma_start(wfx[:], A[f + "W_fx"].rearrange("(k p) n -> p k n", p=P)).then_inc(ld, 16)
                sp.dma_start(wsl[:], A[f + "W_slice"]).then_inc(ld, 16)
                for n, name in enumerate(("W_q", "W_k", "W_v")):
                    sp.dma_start(wqkv[:, n, :], A[f + name]).then_inc(ld, 16)
                sp.dma_start(wout[:], A[f + "W_out"].rearrange("(h c) n -> c h n", c=SC)).then_inc(ld, 16)
                with nc.allow_non_contiguous_dma("biases one word per partition"):
                    sp.dma_start(bx[:], A[f + "b_x"].rearrange("(h c) -> c h", c=SC)).then_inc(ld, 16)
                sp.dma_start(bsl[:], row_bcast(A[f + "b_slice"], 0, SG)).then_inc(ld, 16)
                sp.dma_start(bfx[:], A[f + "b_fx"].rearrange("(a n) -> a n", a=1).to_broadcast([SG, 512])).then_inc(ld, 16)
                sp.dma_start(bout[:], row_bcast(A[f + "b_out"], 0, D)).then_inc(ld, 16)
                sp.dma_start(temp[:], A[f + "temperature"].rearrange("a h b c -> a (h b c)").to_broadcast([P, SH])).then_inc(ld, 16)
                sp.wait_ge(ld, 192)

            @block.tensor
            def _(pe):
                pe.wait_ge(ld, 192)
                for h in range(SH):
                    for k in range(2):
                        o = ((h % 2) * 2 + k) * P
                        last = nc.tensor.transpose(psA[h // 2][0:SC, o:o + P], wx[:, k, h * SC:(h + 1) * SC], c.ident[:])
                last.then_inc(t1, 1)
                pe.wait_ge(t1c, 1)
                for h in range(SH):
                    for k in range(2):
                        nc.tensor.matmul(psW[k][:, h * SG:(h + 1) * SG], wxT[:, h, k, :], wsl[:], start=True, stop=True)
                    last = nc.tensor.matmul(psB[:, h * SG:(h + 1) * SG], bx[:, h:h + 1].to_broadcast([SC, P]), wsl[:],
                                            start=True, stop=True)
                last.then_inc(w1, 1)

            @block.scalar
            def _(act):
                act.wait_ge(t1, 1)
                for q in range(4):
                    last = nc.scalar.activation(wxT[:, 2 * q:2 * q + 2, :, :].rearrange("p a b c -> p (a b c)"),
                                                psA[q][0:SC, :], ACT.Copy)
                last.then_inc(t1c, 1)

            @block.vector
            def _(v):
                tt, ts = nc.vector.tensor_tensor, nc.vector.tensor_scalar
                v.wait_ge(ld, 192)
                ts(temp[:], temp[:], 0.1, 5.0, ALU.max, ALU.min)
                v.drain()
                nc.vector.reciprocal(temp[:], temp[:])
                v.wait_ge(w1, 1)
                v.drain()
                hg = lambda a: a.rearrange("p (h g) -> p h g", g=SG)
                it = temp[:].unsqueeze(2).to_broadcast([P, SH, SG])
                for k in range(2):
                    tt(hg(wc[:, k, :]), hg(psW[k][:, :]), it, ALU.mult)
                tt(hg(bc[:]), hg(psB[:, :]), bsl[:].unsqueeze(1).to_broadcast([P, SH, SG]), ALU.add)
                v.drain()
                tt(hg(bc[:]), hg(bc[:]), it, ALU.mult)
                v.drain()

        w = {"stats": sb("st", [P, GT, 6]), "mv": sb("mv", [P, GT, 2]), "rstd": sb("rs", [P, GT])}
        xln, xT = sb("xln", [P, GT, XW]), sb("xT", [P, 2, GT * P])
        real = sb("real", [P, NI])
        sums = sb("sums", [P, SQ, XW])
        with ExitStack() as s2:
            sb2 = lambda n, shape, dt=FP32: s2.enter_context(nc.sbuf_tensor("f2_" + n, shape, dt))
            wt = sb2("wt", [P, GT, 512])
            wtT = sb2("wtT", [P, SQ, GT * P])
            mx, dn = sb2("mx", [P, GT, SH]), sb2("dn", [P, GT, SH])
            pb2 = lambda n: s2.enter_context(nc.psum_tensor("f2_" + n, [P, 512], FP32))
            psT = [pb2("psT0"), pb2("psT1")]
            psL = [pb2("psL0"), pb2("psL1")]
            psS = [pb2(f"psS{q}") for q in range(SQ)]
            ri, one, vin, root, xr, tr, tc, lg, lgd, ex, exd, wd, wr, wrc, acc, st, sd = (sem("2" + n) for n in (
                "ri", "one", "vin", "root", "xr", "tr", "tc", "lg", "lgd", "ex", "exd", "wd", "wr", "wrc", "acc", "st", "sd"))
            block = s2.enter_context(nc.Block())
            flat = lambda a: a.rearrange("p i n -> p (i n)")

            @block.sync
            def _(sp):
                with sp.Fori(0, NG) as g:
                    sp.wait_ge(wrc, (g + 1) * GT)
                    sp.dma_start(c.wT[:, bass.ds(g * (SQ * GT * P), SQ * GT * P)], wtT[:]).then_inc(st, 16)
                sp.wait_ge(st, 16 * NG)

            @block.gpsimd
            def _(pool):
                nc.gpsimd.iota(real[:], [[1, NI]], base=0, channel_multiplier=NI,
                               allow_small_or_imprecise_dtypes=True).then_inc(ri, 1)

            @block.vector
            def _(v):
                tt, ts = nc.vector.tensor_tensor, nc.vector.tensor_scalar
                nc.vector.memset(xln[:, :, ones:XW], 1.0).then_inc(one, 1)
                v.wait_ge(ri, 1)
                ts(real[:], real[:], N - 0.5, None, ALU.is_lt)
                v.drain()
                hg = lambda a: a.rearrange("p i (h g) -> p (i h) g", g=SG)
                ih = lambda a: a.rearrange("p i h -> p (i h)").unsqueeze(2).to_broadcast([P, GT * SH, SG])
                with v.Fori(0, NG) as g:
                    normalize_group(c, v, w, xln, g, vin, root, xr)
                    for j in range(GT):
                        v.wait_ge(lg, g * GT + j + 1)
                        tt(wt[:, j, :], psL[j % 2][:, :], bc[:], ALU.add).then_inc(lgd, 1)
                    v.drain()
                    nc.vector.tensor_reduce(mx[:], wt[:].rearrange("p i (h g) -> p i h g", g=SG), AX.X, ALU.max)
                    v.drain()
                    tt(hg(wt[:]), hg(wt[:]), ih(mx[:]), ALU.subtract).then_inc(ex, 1)
                    v.wait_ge(exd, g + 1)
                    nc.vector.tensor_reduce(dn[:], wt[:].rearrange("p i (h g) -> p i h g", g=SG), AX.X, ALU.add)
                    v.drain()
                    nc.vector.reciprocal(dn[:], dn[:])
                    v.drain()
                    tt(dn[:], dn[:], real[:, bass.ds(g * GT, GT)].unsqueeze(2).to_broadcast([P, GT, SH]), ALU.mult)
                    v.drain()
                    tt(hg(wt[:]), hg(wt[:]), ih(dn[:]), ALU.mult).then_inc(wd, 1)
                    v.drain()
                    v.wait_ge(acc, g + 1)
                v.wait_ge(sd, 1)
                for q in range(SQ):
                    nc.vector.tensor_copy(sums[:, q, :], psS[q][:, 0:XW])
                v.drain()

            @block.scalar
            def _(act):
                with act.Fori(0, NG) as g:
                    root_and_copies(c, act, w, g, vin, root, tr, tc, psT, xT)
                    act.wait_ge(ex, g + 1)
                    nc.scalar.activation(flat(wt[:]), flat(wt[:]), ACT.Exp).then_inc(exd, 1)
                    for j in range(GT):
                        act.wait_ge(wr, g * GT + j + 1)
                        nc.scalar.activation(wtT[:, :, j * P:(j + 1) * P],
                                             psT[j % 2][:, :].rearrange("p (q n) -> p q n", q=SQ), ACT.Copy).then_inc(wrc, 1)
                    act.wait_ge(st, (g + 1) * 16)

            @block.tensor
            def _(pe):
                mm = nc.tensor.matmul
                for q in range(SQ):
                    mm(psS[q][:, 0:XW], c.zrow[:, 0:P], c.zrow[:, 0:XW], start=True, stop=False)
                pe.wait_ge(one, 1)
                with pe.Fori(0, NG) as g:
                    transposes(c, pe, xln, g, xr, tr, tc, psT)
                    for j in range(GT):
                        pe.wait_ge(tc, g * GT + j + 1)
                        if j >= 2:
                            pe.wait_ge(lgd, g * GT + j - 1)
                        for k in range(2):
                            last = mm(psL[j % 2][:, :], xT[:, k, j * P:(j + 1) * P], wc[:, k, :], start=(k == 0), stop=(k == 1))
                        last.then_inc(lg, 1)
                    pe.wait_ge(wd, g + 1)
                    for j in range(GT):
                        if j >= 2:
                            pe.wait_ge(wrc, g * GT + j - 1)
                        for q in range(SQ):
                            last = nc.tensor.transpose(psT[j % 2][:, q * P:(q + 1) * P], wt[:, j, q * P:(q + 1) * P], c.ident[:])
                        last.then_inc(wr, 1)
                        for q in range(SQ):
                            last = mm(psS[q][:, 0:XW], wt[:, j, q * P:(q + 1) * P], xln[:, j, :], start=False, stop=False)
                    last.then_inc(acc, 1)
                    pe.wait_ge(wrc, (g + 1) * GT)
                for q in range(SQ):
                    last = mm(psS[q][:, 0:XW], c.zrow[:, 0:P], c.zrow[:, 0:XW], start=False, stop=True)
                last.then_inc(sd, 1)

        ow = sb("ow", [P, SQ, D])
        with ExitStack() as s3:
            sb3 = lambda n, shape, dt=FP32: s3.enter_context(nc.sbuf_tensor("f3_" + n, shape, dt))
            pb3 = lambda n: s3.enter_context(nc.psum_tensor("f3_" + n, [P, 512], FP32))
            sh = sb3("sh", [SG, SH, XW])
            shT = sb3("shT", [P, 2, SH, SG])
            rn, nm = sb3("rn", [SG, SH]), sb3("nm", [SG, SH])
            tok, bt = sb3("tok", [SG, SH, SC]), sb3("bt", [SG, SH, SC])
            tokT, qT, kT = sb3("tokT", [SC, SH, SG]), sb3("qT", [SC, SH, SG]), sb3("kT", [SC, SH, SG])
            vv = sb3("vv", [SG, SH, SC])
            at, atT = sb3("at", [SG, SH, SG]), sb3("atT", [SG, SH, SG])
            mx, dn = sb3("mx", [SG, SH]), sb3("dn", [SG, SH])
            oT = sb3("oT", [SC, SH, SG])
            owh = sb3("owh", [SG, SH, D])
            ps = [pb3(f"ps{n}") for n in range(8)]
            mv, step, back, fin = (sem("3" + n) for n in ("mv", "step", "back", "fin"))
            block = s3.enter_context(nc.Block())
            f3 = lambda a: a.rearrange("p h g -> p (h g)")

            @block.sync
            def _(sp):
                for half in range(2):
                    sp.dma_start(sh[:].rearrange("g (q b) w -> g q b w", b=2)[:, :, half, :],
                                 sums[half * SG:(half + 1) * SG, :, :]).then_inc(mv, 16)
                sp.wait_ge(mv, 32)
                sp.wait_ge(back, 9)
                for half in range(2):
                    sp.dma_start(ow[half * SG:(half + 1) * SG, :, :],
                                 owh[:].rearrange("g (q b) w -> g q b w", b=2)[:, :, half, :]).then_inc(fin, 16)
                sp.wait_ge(fin, 32)

            @block.tensor
            def _(pe):
                mm, turn = nc.tensor.matmul, nc.tensor.transpose
                pe.wait_ge(mv, 32)
                for k in range(2):
                    for h in range(SH):
                        last = turn(ps[k][:, h * SG:(h + 1) * SG], sh[:, h, k * P:(k + 1) * P], c.ident[0:SG, 0:SG])
                last.then_inc(step, 1)
                pe.wait_ge(back, 1)
                for h in range(SH):
                    for k in range(2):
                        last = mm(ps[2][0:SG, h * SC:(h + 1) * SC], shT[:, k, h, :], wfx[:, k, h * SC:(h + 1) * SC],
                                  start=(k == 0), stop=(k == 1))
                last.then_inc(step, 1)
                pe.wait_ge(back, 2)
                for h in range(SH):
                    last = turn(ps[3][0:SC, h * SG:(h + 1) * SG], tok[:, h, :], c.ident[0:SG, 0:SG])
                last.then_inc(step, 1)
                pe.wait_ge(back, 3)
                mm(ps[4][0:SC, :], wqkv[:, 0, :], f3(tokT[:]), start=True, stop=True)
                mm(ps[5][0:SC, :], wqkv[:, 1, :], f3(tokT[:]), start=True, stop=True)
                for h in range(SH):
                    last = mm(ps[6][0:SG, h * SC:(h + 1) * SC], tokT[:, h, :], wqkv[:, 2, :], start=True, stop=True)
                last.then_inc(step, 1)
                pe.wait_ge(back, 4)
                for h in range(SH):
                    last = mm(ps[7][0:SG, h * SG:(h + 1) * SG], qT[:, h, :], kT[:, h, :], start=True, stop=True)
                last.then_inc(step, 1)
                pe.wait_ge(back, 6)
                for h in range(SH):
                    last = turn(ps[0][0:SG, h * SG:(h + 1) * SG], at[:, h, :], c.ident[0:SG, 0:SG])
                last.then_inc(step, 1)
                pe.wait_ge(back, 7)
                for h in range(SH):
                    last = mm(ps[1][0:SC, h * SG:(h + 1) * SG], vv[:, h, :], atT[:, h, :], start=True, stop=True)
                last.then_inc(step, 1)
                pe.wait_ge(back, 8)
                for h in range(SH):
                    last = mm(ps[2 + h // 2][0:SG, (h % 2) * D:(h % 2 + 1) * D], oT[:, h, :], wout[:, h, :], start=True, stop=True)
                last.then_inc(step, 1)

            @block.scalar
            def _(act):
                act.wait_ge(back, 5)
                nc.scalar.activation(f3(at[:]), f3(at[:]), ACT.Exp).then_inc(mv, 1)

            @block.vector
            def _(v):
                tt, ts, copy = nc.vector.tensor_tensor, nc.vector.tensor_scalar, nc.vector.tensor_copy
                hsc = lambda a: a.unsqueeze(2).to_broadcast([SG, SH, SC])
                h3 = lambda a: a.rearrange("p (h g) -> p h g", h=SH)
                v.wait_ge(step, 1)
                copy(shT[:, 0, :, :], h3(ps[0][:, :]))
                copy(shT[:, 1, :, :], h3(ps[1][:, :])).then_inc(back, 1)
                copy(nm[:], sh[:, :, ones])
                ts(rn[:], sh[:, :, ones], 1e-5, None, ALU.add)
                v.drain()
                nc.vector.reciprocal(rn[:], rn[:])
                tt(bt[:], h3(bfx[:]), hsc(nm[:]), ALU.mult)
                v.wait_ge(step, 2)
                v.drain()
                tt(tok[:], h3(ps[2][0:SG, :]), bt[:], ALU.add)
                v.drain()
                tt(tok[:], tok[:], hsc(rn[:]), ALU.mult).then_inc(back, 1)
                v.wait_ge(step, 3)
                copy(f3(tokT[:]), ps[3][0:SC, :]).then_inc(back, 1)
                v.wait_ge(step, 4)
                ts(f3(qT[:]), ps[4][0:SC, :], float(SC) ** -0.5, None, ALU.mult)
                copy(f3(kT[:]), ps[5][0:SC, :])
                copy(f3(vv[:]), ps[6][0:SG, :]).then_inc(back, 1)
                v.wait_ge(step, 5)
                nc.vector.tensor_reduce(mx[:], h3(ps[7][0:SG, :]), AX.X, ALU.max)
                v.drain()
                tt(at[:], h3(ps[7][0:SG, :]), hsc(mx[:]), ALU.subtract).then_inc(back, 1)
                v.wait_ge(mv, 33)
                nc.vector.tensor_reduce(dn[:], at[:], AX.X, ALU.add)
                v.drain()
                nc.vector.reciprocal(dn[:], dn[:])
                v.drain()
                tt(at[:], at[:], hsc(dn[:]), ALU.mult).then_inc(back, 1)
                v.wait_ge(step, 6)
                copy(f3(atT[:]), ps[0][0:SG, :]).then_inc(back, 1)
                v.wait_ge(step, 7)
                copy(f3(oT[:]), ps[1][0:SC, :]).then_inc(back, 1)
                v.wait_ge(step, 8)
                for q in range(SQ):
                    last = copy(owh[:, 2 * q:2 * q + 2, :].rearrange("p h d -> p (h d)"), ps[2 + q][0:SG, :])
                last.then_inc(back, 1)
                v.drain()

        with ExitStack() as s4:
            wtT = s4.enter_context(nc.sbuf_tensor("f4_wtT", [P, 2, SQ, GT * P], FP32))
            psO = [s4.enter_context(nc.psum_tensor(f"f4_psO{n}", [P, 512], FP32)) for n in range(GT)]
            lw0, lw1, mmd, od, so = (sem("4" + n) for n in ("lw0", "lw1", "mm", "od", "so"))
            lw = [lw0, lw1]
            block = s4.enter_context(nc.Block())

            @block.sync
            def _(sp):
                for g in range(NG):
                    if g >= 2:
                        sp.wait_ge(mmd, g - 1)
                    sp.dma_start(wtT[:, g % 2, :, :], c.wT[:, g * SQ * GT * P:(g + 1) * SQ * GT * P]).then_inc(lw[g % 2], 16)
                sp.wait_ge(od, NG)
                full = (P - 1) * NI
                sp.dma_start(c.out[0:full, :].rearrange("(p i) d -> p (i d)", i=NI), c.x[0:P - 1, :]).then_inc(so, 16)
                sp.dma_start(c.out[full:N, :].rearrange("(p i) d -> p (i d)", p=1), c.x[P - 1:P, 0:(N - full) * D]).then_inc(so, 16)
                sp.wait_ge(so, 32)

            @block.tensor
            def _(pe):
                for g in range(NG):
                    pe.wait_ge(lw[g % 2], 16 * (g // 2 + 1))
                    if g:
                        pe.wait_ge(od, g)
                    for j in range(GT):
                        for q in range(SQ):
                            last = nc.tensor.matmul(psO[j][:, 0:D], wtT[:, g % 2, q, j * P:(j + 1) * P], ow[:, q, :],
                                                    start=(q == 0), stop=(q == SQ - 1))
                    last.then_inc(mmd, 1)

            @block.vector
            def _(v):
                tt = nc.vector.tensor_tensor
                tt(c.x[:].rearrange("p (i d) -> p i d", d=D), c.x[:].rearrange("p (i d) -> p i d", d=D),
                   bout[:].unsqueeze(1).to_broadcast([P, NI, D]), ALU.add)
                v.drain()
                for g in range(NG):
                    v.wait_ge(mmd, g + 1)
                    for j in range(GT):
                        xj = c.x[:, (g * GT + j) * D:(g * GT + j + 1) * D]
                        last = tt(xj, psO[j][:, 0:D], xj, ALU.add)
                    last.then_inc(od, 1)


def build(nc, A, out):
    c = Chip()
    c.nc, c.A, c.out = nc, A, out
    dram = lambda n, shape, dt=FP32: nc.dram_tensor(n, shape, dt).ap()
    c.t1, c.t2 = dram("t1", (NI * P, TW)), dram("t2", (NI * P, TW))
    c.rec_d, c.rec_s = dram("rec_d", (EP, 4), I32), dram("rec_s", (EP, 4), I32)
    c.ends = [[dram(f"{w}_{k}", (KEYS,), I32) for w in ("start", "end")] for k in ("d", "s")]
    c.st_f, c.st_b = dram("st_f", (EP + KEYS, 4)), dram("st_b", (EP + KEYS, 4))
    c.state = [dram("state0", (EP + 1, SW)), dram("state1", (EP + 1, SW))]
    c.wT = dram("wT", (P, SQ * NI * P))
    c.kv, c.q = dram("kv", (NI * P, 512)), dram("q", (NI * P, D))
    with ExitStack() as s:
        sb = lambda n, shape, dt=FP32: s.enter_context(nc.sbuf_tensor(n, shape, dt))
        c.x = sb("x", [P, NI * D])
        c.ident, c.tri, c.triT, c.cols = (sb(n, [P, P]) for n in ("ident", "tri", "triT", "cols"))
        c.identb, c.colsb = sb("identb", [P, P], BF16), sb("colsb", [P, P], BF16)
        c.zrow, c.one = sb("zrow", [P, T * 4]), sb("one", [P, 1])
        c.tail = sb("tail", [P, SW])
        c.carry, c.fkey = sb("carry", [P, 2 * 137]), sb("fkey", [P, 2])
        c.placed = s.enter_context(nc.semaphore("placed"))
        constants(c)
        layer0_tables(c)
        sort_edges(c)
        edges = s.enter_context(ExitStack())
        se = lambda n, shape, dt=FP32: edges.enter_context(nc.sbuf_tensor(n, shape, dt))
        c.rec, c.sep, c.ar = se("rec", [P, 2, T, 4], I32), se("sep", [P, 2, T]), se("ar", [P, T, 8])
        targets_logits(c)
        edge_pass(c, 0)
        join_tails(c, 0)
        edges.close()
        combine(c, 0)
        experts(c)
        layer1_tables(c)
        edges = s.enter_context(ExitStack())
        se = lambda n, shape, dt=FP32: edges.enter_context(nc.sbuf_tensor(n, shape, dt))
        c.rec, c.sep = se("rec1", [P, 1, T, 4], I32), se("sep1", [P, 1, T])
        reload_edges(c)
        edge_pass(c, 1)
        join_tails(c, 1)
        edges.close()
        combine(c, 1)
        slice_attention(c)


_INS = [
    'x', 'src', 'dst', 'edge_attr_256', 'L0_gnn_W_f',
    'L0_gnn_a_src_f', 'L0_gnn_a_dst_f', 'L0_gnn_b_f', 'L0_gnn_W_b', 'L0_gnn_a_src_b',
    'L0_gnn_a_dst_b', 'L0_gnn_b_b', 'L0_gnn_W_fuse', 'L0_gnn_b_fuse', 'L0_gnn_gamma',
    'L0_gnn_beta', 'L0_gnn_run_mean', 'L0_gnn_run_var', 'L0_ffn_Wg', 'L0_ffn_bg',
    'L0_ffn_W1', 'L0_ffn_b1', 'L0_ffn_W2', 'L0_ffn_b2', 'L1_gnn_Wq',
    'L1_gnn_bq', 'L1_gnn_Wk', 'L1_gnn_bk', 'L1_gnn_Wv', 'L1_gnn_bv',
    'L1_gnn_We', 'L1_gnn_Ws', 'L1_gnn_bs', 'L1_ffn_W_fx', 'L1_ffn_b_fx',
    'L1_ffn_W_x', 'L1_ffn_b_x', 'L1_ffn_W_slice', 'L1_ffn_b_slice', 'L1_ffn_W_q',
    'L1_ffn_W_k', 'L1_ffn_W_v', 'L1_ffn_W_out', 'L1_ffn_b_out', 'L1_ffn_temperature']


def kernel(**inputs):
    import numpy as _np
    import concourse.bacc as _bacc
    from concourse import mybir as _mybir
    from concourse.bass_utils import run_bass_kernel_spmd as _run

    nc = _bacc.Bacc("TRN2", target_bir_lowering=False, num_devices=1)
    arrays, args = {}, {}
    for name in _INS:
        a = _np.ascontiguousarray(inputs[name])
        arrays[f"in_{name}"] = a
        args[name] = nc.dram_tensor(f"in_{name}", a.shape, _mybir.dt.from_np(a.dtype), kind="ExternalInput").ap()
    out = nc.dram_tensor("out_x", (6250, 256), _mybir.dt.float32, kind="ExternalOutput").ap()
    build(nc, args, out)
    r = _run(nc, [arrays], core_ids=[0])
    return r.results[0]["out_x"]
```

```python
import concourse.bass as bass
from concourse import mybir
from contextlib import ExitStack

FP32 = mybir.dt.float32
BF16 = mybir.dt.bfloat16
I32 = mybir.dt.int32
ALU = mybir.AluOpType
ACT = mybir.ActivationFunctionType
AX = mybir.AxisListType

P = 128
N, D = 6250, 256
E = 100000
NI = -(-N // P)
NG, GT = 7, 7
assert NG * GT == NI
B = 8
T = 784
EP = P * T
NBLK = T // B
LO = 64
KEYS = P * LO
H, C = 8, 32
DEN, MX = H * C, H * C + H
SW = H * C + 2 * H
TW = 136
BIG = 1.0e30
LN_EPS = BN_EPS = 1e-5
EXP = 8
HID = 512


class Chip:

    def semaphores(self, phase, prefix):
        made = []

        def semaphore(name):
            made.append(self.nc.alloc_semaphore(prefix + name))
            return made[-1]

        def clear():
            self.nc.clear_and_free_semaphores(made)
            self.nc.all_engine_barrier()

        phase.callback(clear)
        return semaphore

    def flag_on(self, eng):
        return eng.value_load(self.flag[0:1, 0:1], min_val=0, max_val=EP)

    def alone(self, eng):
        eng.sem_inc(self.placed, 1)


def row_bcast(v, lo, n):
    return v[lo:lo + n].rearrange("(a n) -> a n", a=1).to_broadcast([P, n])


def layernorm_stats(c, v, w, x_of, n, sqrt_in, sqrt_out, turn):
    for j in range(n):
        c.nc.vector.bn_stats(w["stats"][:, j, :], x_of(j))
    v.drain()
    for j in range(n):
        c.nc.vector.bn_aggr(w["mv"][:, j, :], w["stats"][:, j, :])
    v.drain()
    c.nc.vector.tensor_scalar(w["rstd"][:, 0:n], w["mv"][:, 0:n, 1], LN_EPS, None, ALU.add).then_inc(sqrt_in, 1)
    v.wait_ge(sqrt_out, turn)
    c.nc.vector.reciprocal(w["rstd"][:, 0:n], w["rstd"][:, 0:n])
    v.drain()


def constants(c):
    nc = c.nc
    with ExitStack() as s:
        made = s.enter_context(nc.semaphore("const_made"))
        got = s.enter_context(nc.semaphore("x_loaded"))
        zero = s.enter_context(nc.semaphore("pad_zeroed"))
        block = s.enter_context(nc.Block())

        @block.gpsimd
        def _(pool):
            nc.gpsimd.memset(c.ident[:], 0.0)
            nc.gpsimd.memset(c.tri[:], 1.0)
            nc.gpsimd.memset(c.triT[:], 1.0)
            pool.drain()
            nc.gpsimd.affine_select(out=c.ident[:], in_=c.ident[:], compare_op=ALU.not_equal, fill=1.0,
                                    base=0, pattern=[[-1, P]], channel_multiplier=1)
            nc.gpsimd.affine_select(out=c.tri[:], in_=c.tri[:], compare_op=ALU.is_gt, fill=0.0,
                                    base=0, pattern=[[-1, P]], channel_multiplier=1)
            nc.gpsimd.affine_select(out=c.triT[:], in_=c.triT[:], compare_op=ALU.is_gt, fill=0.0,
                                    base=0, pattern=[[1, P]], channel_multiplier=-1)
            nc.gpsimd.iota(c.cols[:], [[1, P]], base=0, channel_multiplier=0,
                           allow_small_or_imprecise_dtypes=True)
            pool.drain()
            nc.gpsimd.memset(c.one[:], 1.0)
            nc.gpsimd.memset(c.zrow[:], 0.0).then_inc(made, 1)


        @block.vector
        def _(v):
            nc.vector.memset(c.x[96:128, :], 0.0).then_inc(zero, 1)
            v.wait_ge(made, 1)
            nc.vector.tensor_copy(c.identb[:], c.ident[:])
            nc.vector.tensor_copy(c.colsb[:], c.cols[:])
            v.drain()

        @block.sync
        def _(sp):
            x = c.A["x"]
            full = (P - 1) * NI
            sp.wait_ge(zero, 1)
            for p0, p1 in slices_of(0, P - 1):
                sp.dma_start(c.x[p0:p1, :], x[p0 * NI:p1 * NI, :].rearrange("(p i) d -> p (i d)", i=NI)).then_inc(got, 16)
            sp.dma_start(c.x[P - 1:P, 0:(N - full) * D],
                         x[full:N, :].rearrange("(p i) d -> p (i d)", p=1)).then_inc(got, 16)
            sp.wait_ge(got, 48)


def layer0_tables(c):
    nc, A = c.nc, c.A
    with ExitStack() as s:
        sb = lambda n, shape, dt=FP32: s.enter_context(nc.sbuf_tensor(n, shape, dt))
        sem = lambda n: s.enter_context(nc.semaphore(n))
        pb = lambda n: s.enter_context(nc.psum_tensor(n, [P, 512], FP32))
        W = sb("t_W", [P, 2, 2 * TW])
        av = sb("t_av", [P, 4, 4])
        WT = sb("t_WT", [P, 2, 2, P])
        w = {"stats": sb("t_st", [P, GT, 6]), "mv": sb("t_mv", [P, GT, 2]), "rstd": sb("t_rs", [P, GT])}
        xln = sb("t_xln", [P, GT, D])
        xT = sb("t_xT", [P, 2, GT * P])
        row = sb("t_row", [P, 2, GT, TW])
        psT = [pb("t_psT0"), pb("t_psT1")]
        psO = [pb("t_psO0"), pb("t_psO1")]
        loaded, zeroed, wt, wtc, wa, ready = (sem("t_" + n) for n in ("ld", "z", "wt", "wtc", "wa", "rdy"))
        vin, root, xr, tr, tc, mm, oc, st = (sem("t_" + n) for n in ("vin", "root", "xr", "tr", "tc", "mm", "oc", "st"))
        block = s.enter_context(nc.Block())
        names = [("L0_gnn_a_src_f", 0), ("L0_gnn_a_dst_f", 1), ("L0_gnn_a_src_b", 2), ("L0_gnn_a_dst_b", 3)]

        @block.sync
        def _(sp):
            for d, name in enumerate(("L0_gnn_W_f", "L0_gnn_W_b")):
                sp.dma_start(W[:, :, d * TW:d * TW + P], A[name].rearrange("(k p) c -> p k c", p=P)).then_inc(loaded, 16)
            sp.wait_ge(zeroed, 1)
            for name, at in names:
                for h in range(4):
                    sp.dma_start(av[h * 32:(h + 1) * 32, at, h:h + 1],
                                 A[name][h:h + 1, :].rearrange("a c -> c a")).then_inc(loaded, 16)
            with sp.Fori(0, NG) as g:
                sp.wait_ge(oc, (g + 1) * GT)
                sp.wait_ge(loaded, 16 * 18)
                for d, tab in enumerate((c.t1, c.t2)):
                    sp.dma_start(tab.rearrange("(p i) w -> p (i w)", i=NI)[:, bass.ds(g * (GT * TW), GT * TW)],
                                 row[:, d, :, :]).then_inc(st, 16)
            sp.wait_ge(st, 32 * NG)

        @block.vector
        def _(v):
            nc.vector.memset(av[:], 0.0).then_inc(zeroed, 1)
            with v.Fori(0, NG) as g:
                layernorm_stats(c, v, w, lambda j: c.x[:, bass.ds((g * GT + j) * D, D)], GT, vin, root, g + 1)
                for j in range(GT):
                    nc.vector.tensor_scalar(xln[:, j, :], c.x[:, bass.ds((g * GT + j) * D, D)], w["mv"][:, j, 0:1],
                                            w["rstd"][:, j:j + 1], ALU.subtract, ALU.mult).then_inc(xr, 1)
                v.wait_ge(tr, (g + 1) * GT)

        @block.scalar
        def _(act):
            for d in range(2):
                act.wait_ge(wt, d + 1)
                nc.scalar.activation(WT[:, d, :, :], psT[d][:, 0:2 * P], ACT.Copy).then_inc(wtc, 1)
            act.wait_ge(wa, 1)
            for k in range(2):
                for d in range(2):
                    for q in range(2):
                        o = (k * 4 + d * 2 + q) * 4
                        last = nc.scalar.activation(W[:, k, d * TW + P + 4 * q:d * TW + P + 4 * q + 4],
                                                    psO[0][:, o:o + 4], ACT.Copy)
            last.then_inc(ready, 1)
            with act.Fori(0, NG) as g:
                act.wait_ge(vin, g + 1)
                nc.scalar.activation(w["rstd"][:], w["rstd"][:], ACT.Sqrt).then_inc(root, 1)
                for j in range(GT):
                    act.wait_ge(tr, g * GT + j + 1)
                    nc.scalar.activation(xT[:, :, j * P:(j + 1) * P],
                                         psT[j % 2][:, 0:2 * P].rearrange("p (k n) -> p k n", k=2),
                                         ACT.Copy).then_inc(tc, 1)
                for j in range(GT):
                    act.wait_ge(mm, g * GT + j + 1)
                    nc.scalar.activation(row[:, :, j, :], psO[j % 2][:, 0:2 * TW].rearrange("p (d w) -> p d w", d=2),
                                         ACT.Copy).then_inc(oc, 1)
                act.wait_ge(st, (g + 1) * 32)

        @block.tensor
        def _(pe):
            pe.wait_ge(loaded, 16 * 18)
            for d in range(2):
                for k in range(2):
                    last = nc.tensor.transpose(psT[d][:, k * P:(k + 1) * P], W[:, k, d * TW:d * TW + P], c.ident[:])
                last.then_inc(wt, 1)
            pe.wait_ge(wtc, 2)
            for k in range(2):
                for d in range(2):
                    for q in range(2):
                        o = (k * 4 + d * 2 + q) * 4
                        last = nc.tensor.matmul(psO[0][:, o:o + 4], WT[:, d, k, :], av[:, 2 * d + q, :],
                                                start=True, stop=True)
            last.then_inc(wa, 1)
            pe.wait_ge(ready, 1)
            with pe.Fori(0, NG) as g:
                for j in range(GT):
                    pe.wait_ge(xr, g * GT + j + 1)
                    if j >= 2:
                        pe.wait_ge(tc, g * GT + j - 1)
                    for k in range(2):
                        last = nc.tensor.transpose(psT[j % 2][:, k * P:(k + 1) * P], xln[:, j, k * P:(k + 1) * P], c.ident[:])
                    last.then_inc(tr, 1)
                for j in range(GT):
                    pe.wait_ge(tc, g * GT + j + 1)
                    if j >= 2:
                        pe.wait_ge(oc, g * GT + j - 1)
                    for k in range(2):
                        last = nc.tensor.matmul(psO[j % 2][:, 0:2 * TW], xT[:, k, j * P:(j + 1) * P], W[:, k, :],
                                                start=(k == 0), stop=(k == 1))
                    last.then_inc(mm, 1)
                pe.wait_ge(oc, (g + 1) * GT)


def slices_of(p0, p1):
    return [(p0, 112), (112, p1)]


def sort_edges(c):
    nc, A = c.nc, c.A
    U = 2
    with ExitStack() as s:
        sb = lambda n, shape, dt=FP32: s.enter_context(nc.sbuf_tensor(n, shape, dt))
        key = sb("s_key", [P, 2, T], I32)
        dig = sb("s_dig", [P, 2, 2, T + B], I32)
        rec = sb("s_rec", [P, T, 4], I32)
        oh = sb("s_oh", [P, U, 2, B, P], BF16)
        ol = sb("s_ol", [P, U, 2, B, LO], BF16)
        base = sb("s_base", [P, 2, LO])
        full = (P - 1) * T

        def one_hots(t0, u, k):
            nc.vector.tensor_tensor(oh[:, u, k, :, :], c.colsb[:, :].unsqueeze(1).to_broadcast([P, B, P]),
                                    dig[:, k, 0, bass.ds(t0, B)].unsqueeze(2).to_broadcast([P, B, P]), ALU.is_equal)
            return nc.vector.tensor_tensor(ol[:, u, k, :, :], c.colsb[:, 0:LO].unsqueeze(1).to_broadcast([P, B, LO]),
                                           dig[:, k, 1, bass.ds(t0, B)].unsqueeze(2).to_broadcast([P, B, LO]), ALU.is_equal)

        with ExitStack() as s1:
            sb1 = lambda n, shape, dt=FP32: s1.enter_context(nc.sbuf_tensor(n, shape, dt))
            sem = c.semaphores(s1, "h_")
            pb = lambda n: s1.enter_context(nc.psum_tensor(n, [P, 512], FP32))
            nxt = sb1("h_nxt", [P, 1], I32)
            down = sb1("h_down", [P, T])
            viol = sb1("h_viol", [P, 2])
            hist, tmp = sb1("h_hist", [P, 2, LO]), sb1("h_tmp", [P, LO])
            junk, tot, offs = sb1("h_junk", [P, P]), sb1("h_tot", [P, 2]), sb1("h_offs", [P, 2])
            nid = sb1("h_nid", [P, LO])
            zeros = sb1("h_zeros", [P, T * 4])
            ends = sb1("h_ends", [P, 2, 2, LO], I32)
            psH = [pb("h_psH0"), pb("h_psH1")]
            psR, psV = pb("h_psR"), pb("h_psV")
            kz, kld, made, used, hd, hc, off, bd, rz, wr, ids, rd, rw, vs, vd = (sem(n) for n in (
                "kz", "kld", "made", "used", "hd", "hc", "off", "bd", "rz", "wr", "ids", "rd", "rw", "vs", "vd"))
            block = s1.enter_context(nc.Block())

            @block.sync
            def _(sp):
                sp.wait_ge(kz, 1)
                for k, name in enumerate(("dst", "src")):
                    a = A[name]
                    for p0, p1 in slices_of(0, P - 1):
                        sp.dma_start(key[p0:p1, k, :], a[p0 * T:p1 * T].rearrange("(p t) -> p t", t=T)).then_inc(kld, 16)
                    sp.dma_start(key[P - 1:P, k, 0:E - full], a[full:E].rearrange("(p t) -> p t", p=1)).then_inc(kld, 16)
                with nc.allow_non_contiguous_dma("one word per partition"):
                    sp.dma_start(nxt[0:P - 1, :], A["dst"][T - 0:T + (P - 2) * T + 1:T].rearrange("(p a) -> p a", a=1)).then_inc(kld, 16)
                ea = A["edge_attr_256"]
                sp.dma_start(c.ea_tail[0:E - 112 * T, :].rearrange("(a n) w -> a (n w)", a=16),
                             ea[112 * T:E, :].rearrange("(a n) w -> a (n w)", a=16)).then_inc(rz, 16)
                sp.dma_start(c.ea_tail[E - 112 * T:16 * T, :].rearrange("(a n) w -> a (n w)", a=16),
                             ea[0:EP - E, :].rearrange("(a n) w -> a (n w)", a=16)).then_inc(rz, 16)
                for a in (c.st_f, c.st_b):
                    sp.dma_start(a[0:EP, :].rearrange("(p t) w -> p (t w)", p=P), zeros[:]).then_inc(rz, 16)
                sp.wait_ge(rd, 1)
                sp.dma_start(c.rec_d.rearrange("(p t) w -> p t w", p=P), rec[:]).then_inc(rw, 16)
                sp.wait_ge(bd, 1)
                for k in range(2):
                    for q in range(2):
                        sp.dma_start(c.ends[k][q].rearrange("(p l) -> p l", l=LO), ends[:, k, q, :]).then_inc(wr, 16)
                sp.wait_ge(wr, 64)
                sp.wait_ge(rw, 16)
                sp.wait_ge(rz, 64)

            @block.vector
            def _(v):
                nc.vector.memset(key[:], N)
                nc.vector.memset(zeros[:], 0.0)
                nc.vector.memset(nxt[:], N).then_inc(kz, 1)
                nc.vector.memset(dig[:, :, :, T:T + B], 0)
                v.wait_ge(kld, 112)
                nc.vector.tensor_scalar(dig[:, :, 0, 0:T], key[:], 6, None, ALU.logical_shift_right)
                nc.vector.tensor_scalar(dig[:, :, 1, 0:T], key[:], LO - 1, None, ALU.bitwise_and)
                v.drain()
                v.sem_inc(used, U)
                with v.Fori(0, NBLK // U) as i:
                    for u in range(U):
                        v.wait_ge(used, i * U + u + 1)
                        one_hots((i * U + u) * B, u, 0)
                        one_hots((i * U + u) * B, u, 1).then_inc(made, 1)
                nc.vector.tensor_tensor(down[:, 1:T], key[:, 0, 1:T], key[:, 0, 0:T - 1], ALU.is_lt)
                nc.vector.tensor_tensor(down[:, 0:1], nxt[:], key[:, 0, T - 1:T], ALU.is_lt)
                v.drain()
                nc.vector.tensor_reduce(viol[:, 0:1], down[:], AX.X, ALU.add)
                v.wait_ge(ids, 1)
                nc.vector.tensor_copy(rec[:, :, 0:2], key[:].rearrange("p k t -> p t k")).then_inc(rd, 1)
                v.drain()
                nc.vector.tensor_copy(viol[:, 1:2], viol[:, 0:1]).then_inc(vs, 1)
                v.wait_ge(hd, 1)
                for k in range(2):
                    nc.vector.tensor_copy(hist[:, k, :], psH[k][:, 0:LO])
                nc.vector.tensor_copy(c.flag[:], psV[:, 0:1])
                v.drain()
                for k in range(2):
                    nc.vector.tensor_reduce(tot[:, k:k + 1], hist[:, k, :], AX.X, ALU.add)
                v.drain()
                nc.vector.tensor_copy(junk[:, 0:2], tot[:]).then_inc(hc, 1)
                v.wait_ge(off, 1)
                nc.vector.tensor_copy(offs[:], psR[:, 0:2])
                nc.vector.memset(tmp[:], 0.0)
                v.drain()
                for k in range(2):
                    nc.vector.tensor_tensor_scan(base[:, k, :], hist[:, k, :], tmp[:], offs[:, k:k + 1], ALU.add, ALU.add)
                v.drain()
                for k in range(2):
                    nc.vector.tensor_scalar(tmp[:], hist[:, k, :], 0.5, None, ALU.is_ge)
                    nc.vector.tensor_scalar(junk[:, 0:LO], base[:, k, :], -1.0 - EP, None, ALU.add)
                    v.drain()
                    nc.vector.tensor_tensor(base[:, k, :], base[:, k, :], hist[:, k, :], ALU.subtract)
                    nc.vector.tensor_tensor(junk[:, 0:LO], junk[:, 0:LO], tmp[:], ALU.mult)
                    v.drain()
                    nc.vector.tensor_tensor(junk[:, LO:2 * LO], base[:, k, :], nid[:], ALU.subtract)
                    nc.vector.tensor_scalar(ends[:, k, 1, :], junk[:, 0:LO], float(EP), None, ALU.add)
                    v.drain()
                    nc.vector.tensor_tensor(junk[:, LO:2 * LO], junk[:, LO:2 * LO], tmp[:], ALU.mult)
                    v.drain()
                    nc.vector.tensor_tensor(ends[:, k, 0, :], junk[:, LO:2 * LO], nid[:], ALU.add)
                    v.drain()
                nc.vector.tensor_copy(tmp[:], base[:, 0, :]).then_inc(bd, 1)

            @block.tensor
            def _(pe):
                for k in range(2):
                    nc.tensor.matmul(psH[k][:, 0:LO], c.zrow[:, 0:P], c.zrow[:, 0:LO], start=True, stop=False)
                with pe.Fori(0, NBLK // U) as i:
                    for u in range(U):
                        pe.wait_ge(made, i * U + u + 1)
                        for k in range(2):
                            for j in range(B):
                                last = nc.tensor.matmul(psH[k][:, 0:LO], oh[:, u, k, j, :], ol[:, u, k, j, :],
                                                        start=False, stop=False)
                        last.then_inc(used, 1)
                pe.wait_ge(vs, 1)
                nc.tensor.matmul(psV[:, 0:1], c.one[:, 0:1].to_broadcast([P, P]), viol[:, 1:2], start=True, stop=True)
                for k in range(2):
                    last = nc.tensor.matmul(psH[k][:, 0:LO], c.zrow[:, 0:P], c.zrow[:, 0:LO], start=False, stop=True)
                last.then_inc(hd, 1)
                pe.wait_ge(hc, 1)
                nc.tensor.matmul(psR[:, 0:2], c.triT[:], tot[:], start=True, stop=True).then_inc(off, 1)

            @block.gpsimd
            def _(pool):
                nc.gpsimd.iota(rec[:, :, 2], [[1, T]], base=0, channel_multiplier=T)
                nc.gpsimd.iota(nid[:], [[1, LO]], base=EP, channel_multiplier=LO, allow_small_or_imprecise_dtypes=True)
                nc.gpsimd.memset(rec[:, :, 3], 0)
                pool.drain()
                nc.gpsimd.tensor_scalar(rec[:, :, 2], rec[:, :, 2], E - 1, None, ALU.min).then_inc(ids, 1)

        def rank_pass(k, rec_out, only_if_unsorted):
            with ExitStack() as s2:
                sb2 = lambda n, shape, dt=FP32: s2.enter_context(nc.sbuf_tensor(f"s{k}_{n}", shape, dt))
                sem = c.semaphores(s2, f"s{k}_")
                pb = lambda n, shape=(P, 512), dt=FP32: s2.enter_context(nc.psum_tensor(f"s{k}_{n}", list(shape), dt))
                keyf = sb2("kf", [P, U, B])
                oht = sb2("oht", [P, U, B, P])
                tab = sb2("tab", [P, B, LO])
                junk = sb2("junk", [P, B, P], BF16)
                hit = sb2("hit", [P, B, LO])
                rank = sb2("rank", [P, 2, B])
                pos = sb2("pos", [P, U, B], I32)
                row = sb2("row", [P, U, B, 4], I32)
                psT = [pb(f"psT{u}", (P, 1024), BF16) for u in range(U)]
                psK = [pb(f"psK{q}") for q in range(2)]
                psR = [pb(f"psR{u}") for u in range(U)]
                psH = pb("psH")
                made, tp, tpc, kr, eqd, tbc, lk, lkd, hu, pd, sct0, sct1, rows_free = (sem(n) for n in (
                    "made", "tp", "tpc", "kr", "eqd", "tbc", "lk", "lkd", "hu", "pd", "sct0", "sct1", "rows_free"))
                sct = [sct0, sct1]
                block = s2.enter_context(nc.Block())

                def when(eng):
                    if not only_if_unsorted:
                        return ExitStack()
                    return eng.If(c.flag_on(eng) > 0)

                @block.sync
                def _(sp):
                    with when(sp):
                        sp.sem_inc(rows_free, U)
                        with sp.Fori(0, NBLK // U) as i:
                            for u in range(U):
                                sp.wait_ge(sct[u], (i + 1) * (16 * B))
                                sp.sem_inc(rows_free, 1)

                @block.vector
                def _(v):
                    with when(v):
                        nc.vector.tensor_copy(keyf[:, 0, :], key[:, k, 0:B])
                        one_hots(0, 0, k).then_inc(made, 1)
                        with v.Fori(0, NBLK // U) as i:
                            for u in range(U):
                                blk = i * U + u
                                v.wait_ge(hu, (blk + U) * B)
                                nc.vector.tensor_copy(keyf[:, 1 - u, :], dig[:, k, 0, bass.ds((blk + 1) * B, B)])
                                v.drain()
                                nc.vector.scalar_tensor_tensor(out=keyf[:, 1 - u, :], in0=keyf[:, 1 - u, :], scalar=float(LO),
                                                               in1=dig[:, k, 1, bass.ds((blk + 1) * B, B)],
                                                               op0=ALU.mult, op1=ALU.add)
                                one_hots((blk + 1) * B, 1 - u, k).then_inc(made, 1)
                                for j in range(B):
                                    if j % 4 == 0:
                                        v.wait_ge(kr, blk * 2 + j // 4 + 1)
                                    last = nc.vector.scalar_tensor_tensor(
                                        out=junk[:, j, :], in0=psK[j // 4][:, (j % 4) * P:(j % 4 + 1) * P],
                                        scalar=keyf[:, u, j:j + 1], in1=c.tri[:], op0=ALU.is_equal, op1=ALU.mult,
                                        accum_out=rank[:, 0, j:j + 1])
                                    if j % 4 == 3:
                                        last.then_inc(eqd, 1)
                                v.wait_ge(lk, blk + 1)
                                nc.vector.tensor_tensor(hit[:], psR[u][:, :].rearrange("p (j l) -> p j l", l=LO),
                                                        ol[:, u, k, :, :], ALU.mult).then_inc(lkd, 1)
                                v.drain()
                                nc.vector.tensor_reduce(rank[:, 1, :], hit[:], AX.X, ALU.add)
                                v.drain()
                                v.wait_ge(rows_free, blk + 1)
                                nc.vector.tensor_tensor(pos[:, u, :], rank[:, 0, :], rank[:, 1, :], ALU.add)
                                nc.vector.tensor_copy(row[:, u, :, :], rec[:, bass.ds(blk * B, B), :]).then_inc(pd, 1)

                @block.scalar
                def _(act):
                    with when(act):
                        with act.Fori(0, NBLK // U) as i:
                            for u in range(U):
                                blk = i * U + u
                                act.wait_ge(tp, blk + 1)
                                nc.scalar.activation(oht[:, u, :, :].rearrange("p j n -> p (j n)"), psT[u][:, :],
                                                     ACT.Copy).then_inc(tpc, 1)
                                for j in range(B):
                                    act.wait_ge(hu, (blk + U) * B + j)
                                    nc.scalar.activation(tab[:, j, :], psH[:, 0:LO], ACT.Copy).then_inc(tbc, 1)

                @block.tensor
                def _(pe):
                    with when(pe):
                        nc.tensor.matmul(psH[:, 0:LO], c.ident[:], base[:, k, :], start=True, stop=True).then_inc(hu, U * B)
                        pe.sem_inc(eqd, 2)
                        pe.sem_inc(lkd, U)
                        with pe.Fori(0, NBLK // U) as i:
                            for u in range(U):
                                blk = i * U + u
                                pe.wait_ge(made, blk + 1)
                                for j in range(B):
                                    last = nc.tensor.transpose(psT[u][:, j * P:(j + 1) * P], oh[:, u, k, j, :], c.identb[:])
                                last.then_inc(tp, 1)
                                for q in range(2):
                                    pe.wait_ge(eqd, blk * 2 + q + 1)
                                    for j in range(4 * q, 4 * q + 4):
                                        last = nc.tensor.matmul(psK[q][:, (j % 4) * P:(j % 4 + 1) * P],
                                                                keyf[:, u, j:j + 1].to_broadcast([P, P]), c.ident[:],
                                                                start=True, stop=True)
                                    last.then_inc(kr, 1)
                                pe.wait_ge(lkd, blk + 1)
                                for j in range(B):
                                    pe.wait_ge(tbc, blk * B + j + 1)
                                    last = nc.tensor.matmul(psR[u][:, j * LO:(j + 1) * LO], oht[:, u, j, :], tab[:, j, :],
                                                            start=True, stop=True)
                                    if j == B - 1:
                                        last.then_inc(lk, 1)
                                    nc.tensor.matmul(psH[:, 0:LO], oh[:, u, k, j, :], ol[:, u, k, j, :],
                                                     start=False, stop=True, skip_group_check=True).then_inc(hu, 1)

                @block.gpsimd
                def _(pool):
                    with when(pool):
                        with pool.Fori(0, NBLK // U) as i:
                            for u in range(U):
                                pool.wait_ge(pd, i * U + u + 1)
                                c.alone(pool)
                                for j in range(B):
                                    pool.indirect_dma_start(rec_out, bass.IndirectOffsetOnAxis(ap=pos[:, u, j:j + 1], axis=0),
                                                            row[:, u, j, :], None).then_inc(sct[u], 16)
                        for u in range(U):
                            pool.wait_ge(sct[u], 16 * B * (NBLK // U))

        rank_pass(1, c.rec_s, False)
        rank_pass(0, c.rec_d, True)


def targets_logits(c):
    nc = c.nc
    with ExitStack() as s:
        sb = lambda n, shape, dt=FP32: s.enter_context(nc.sbuf_tensor(n, shape, dt))
        sem = c.semaphores(s, "a_")
        startn = sb("a_start", [P, 2, NI], I32)
        logit = sb("a_logit", [P, 2, NI, 4])
        idx = sb("a_idx", [P, 2, GT], I32)
        rows = sb("a_rows", [P, 2, GT, 4])
        val = sb("a_val", [P, 2, T, 4])
        first = sb("a_first", [P, 2, TW])
        ld, rl, sc, fg, vl, chunk = (sem(n) for n in ("ld", "rl", "sc", "fg", "vl", "chunk"))
        block = s.enter_context(nc.Block())

        @block.sync
        def _(sp):
            for d, (tab, rec) in enumerate(((c.t1, c.rec_d), (c.t2, c.rec_s))):
                sp.dma_start(c.rec[:, d, :, :], rec.rearrange("(p t) w -> p t w", p=P)).then_inc(rl, 16)
                sp.dma_start(startn[:, d, :], c.ends[d][0][0:NI * P].rearrange("(p i) -> p i", i=NI)).then_inc(ld, 16)
                sp.dma_start(logit[:, d, :, :], tab.rearrange("(p i) w -> p i w", i=NI)[:, :, 132:136]).then_inc(ld, 16)
            sp.wait_ge(sc, NG * 2 * GT * 16)
            for d, st in enumerate((c.st_f, c.st_b)):
                sp.dma_start(val[:, d, :, :], st[0:EP, :].rearrange("(p t) w -> p t w", p=P)).then_inc(vl, 16)
            sp.wait_ge(vl, 32)

        @block.gpsimd
        def _(pool):
            pool.wait_ge(ld, 64)
            pool.wait_ge(rl, 32)
            with pool.Fori(0, NG) as g:
                nc.gpsimd.tensor_copy(idx[:], startn[:, :, bass.ds(g * GT, GT)])
                nc.gpsimd.tensor_copy(rows[:], logit[:, :, bass.ds(g * GT, GT), :])
                pool.drain()
                for j in range(GT):
                    for d, st in enumerate((c.st_f, c.st_b)):
                        pool.indirect_dma_start(st, bass.IndirectOffsetOnAxis(ap=idx[:, d, j:j + 1], axis=0),
                                                rows[:, d, j, :], None).then_inc(sc, 16)
                pool.wait_ge(sc, (g + 1) * (2 * GT * 16))
                c.alone(pool)
            for d, (tab, col) in enumerate(((c.t1, 0), (c.t2, 1))):
                pool.indirect_dma_start(first[:, d, :], None, tab,
                                        bass.IndirectOffsetOnAxis(ap=c.rec[:, d, 0, col:col + 1], axis=0)).then_inc(fg, 16)
            pool.wait_ge(fg, 32)

        @block.vector
        def _(v):
            v.wait_ge(rl, 32)
            for d in range(2):
                k = c.rec[:, d, :, d]
                nc.vector.memset(c.sep[:, d, 0:1], 0.0)
                nc.vector.tensor_tensor(c.sep[:, d, 1:T], k[:, 1:T], k[:, 0:T - 1], ALU.is_equal)
            v.wait_ge(fg, 32)
            v.wait_ge(vl, 32)
            nc.vector.tensor_copy(val[:, :, 0, :], first[:, :, 132:136])
            v.drain()
            for d in range(2):
                for h in range(4):
                    nc.vector.tensor_tensor_scan(c.ar[:, :, 4 * d + h], c.sep[:, d, :], val[:, d, :, h], 0.0,
                                                 ALU.mult, ALU.add)
            v.drain()
            nc.vector.tensor_scalar(c.sep[:], c.sep[:], 1.0, BIG, ALU.subtract, ALU.mult)
            v.drain()


def order_attributes(c):
    nc, A = c.nc, c.A
    U = 2
    with ExitStack() as s:
        sb = lambda n, shape, dt=FP32: s.enter_context(nc.sbuf_tensor("o_" + n, shape, dt))
        sem = c.semaphores(s, "o_")
        idx, rows = sb("idx", [P, U, B, 4], I32), sb("rows", [P, U, B, D])
        staged, so0, so1, g0, g1, free = (sem(n) for n in ("staged", "so0", "so1", "g0", "g1", "free"))
        so, got = [so0, so1], [g0, g1]
        block = s.enter_context(nc.Block())

        @block.gpsimd
        def _(pool):
            with pool.If(c.flag_on(pool) > 0):
                with pool.Fori(0, NBLK // U) as i:
                    for u in range(U):
                        pool.wait_ge(free, i * U + u + 1)
                        c.alone(pool)
                        nc.gpsimd.tensor_copy(idx[:, u], c.rec[:, 0, bass.ds((i * U + u) * B, B), :]).then_inc(staged, 1)
                        pool.wait_ge(staged, i * U + u + 1)
                        c.alone(pool)
                        for j in range(B):
                            pool.indirect_dma_start(rows[:, u, j, :], None, A["edge_attr_256"],
                                                    bass.IndirectOffsetOnAxis(ap=idx[:, u, j, 2:3], axis=0)).then_inc(got[u], 16)

        @block.sync
        def _(sp):
            with sp.If(c.flag_on(sp) > 0):
                sp.sem_inc(free, U)
                with sp.Fori(0, NBLK // U) as i:
                    for u in range(U):
                        sp.wait_ge(got[u], (i + 1) * (16 * B))
                        sp.dma_start(c.ea_sorted.rearrange("(p t) w -> p (t w)", p=P)[:, bass.ds((i * U + u) * (B * D), B * D)],
                                     rows[:, u, :, :]).then_inc(so[u], 16)
                        sp.wait_ge(so[u], (i + 1) * 16)
                        sp.sem_inc(free, 1)


def edge_pass(c, layer):
    nc, A = c.nc, c.A
    U = 2
    B1 = B + 1
    state = c.state[layer]
    with ExitStack() as s:
        sb = lambda n, shape, dt=FP32: s.enter_context(nc.sbuf_tensor(f"e{layer}_{n}", shape, dt))
        sem = c.semaphores(s, f"e{layer}_")
        pb = lambda n: s.enter_context(nc.psum_tensor(f"e{layer}_{n}", [P, 512], FP32))
        idx = sb("idx", [P, U, 2, B, 4], I32)
        if layer == 0:
            g1, g2 = sb("g1", [P, U, B, TW]), sb("g2", [P, U, B, TW])
        else:
            kv, q, ea = sb("kv", [P, U, B, 512]), sb("q", [P, U, B, D]), sb("ea", [P, U, B, D])
            eaT = sb("eaT", [P, 4, 2, 2, P])
            we = sb("we", [P, 2, D])
            psT = [pb(f"psT{n}") for n in range(4)]
            psE = [pb(f"psE{n}") for n in range(4)]
        sepb = sb("sepb", [P, H, B1])
        at = sb("at", [P, H, B1])
        mt = sb("mt", [P, H, B1])
        ex = sb("ex", [P, 2, H, B])
        cw = sb("cw", [P, 2, H, B1])
        den = sb("den", [P, H, B1])
        fx = sb("fx", [P, D, B1])
        wv = sb("wv", [P, D, B1])
        st = sb("st", [P, U, B, SW])
        ld, gat0, gat1, eg0, eg1, used, exd, cwd, dnd, std, act_st, so0, so1, free, dump, tp, tcp, ep, ed = (
            sem(n) for n in ("ld", "gat0", "gat1", "eg0", "eg1", "used", "exd", "cwd", "dnd", "std", "acts", "so0",
                             "so1", "free", "dump", "tp", "tcp", "ep", "ed"))
        gat, eg, so = [gat0, gat1], [eg0, eg1], [so0, so1]
        q_used = sem("q_used")
        staged, fxd, act_mt = sem("staged"), sem("fxd"), sem("act_mt")
        block = s.enter_context(nc.Block())
        ngat = 2 * B * 16

        @block.sync
        def _(sp):
            if layer == 1:
                sp.dma_start(we[:], A["L1_gnn_We"].rearrange("(k p) n -> p k n", p=P)).then_inc(ld, 16)
            sp.wait_ge(dump, 1)
            sp.dma_start(state[EP:EP + 1, :], st[0:1, 1, B - 1, :]).then_inc(so[1], 16)
            sp.wait_ge(so[1], 16)
            sp.sem_inc(free, 1)
            unsorted = c.flag_on(sp) if layer == 1 else None

            def load_attributes(b, u):
                at_ = bass.ds(b * (B * D), B * D)
                rows = lambda a: a.rearrange("(p t) w -> p (t w)", t=T)[:, at_]
                with sp.If(unsorted > 0):
                    sp.dma_start(ea[0:112, u, :, :], rows(c.ea_sorted[0:112 * T, :])).then_inc(eg[u], 16)
                    sp.dma_start(ea[112:P, u, :, :], rows(c.ea_sorted[112 * T:EP, :])).then_inc(eg[u], 16)
                with sp.Else():
                    sp.dma_start(ea[0:112, u, :, :], rows(A["edge_attr_256"][0:112 * T, :])).then_inc(eg[u], 16)
                    sp.dma_start(ea[112:P, u, :, :], rows(c.ea_tail)).then_inc(eg[u], 16)

            def store(i, u):
                blk = i * U + u
                sp.wait_ge(act_st, blk + 2)
                sp.dma_start(state[0:EP, :].rearrange("(p t) w -> p (t w)", p=P)[:, bass.ds(blk * (B * SW), B * SW)],
                             st[:, u, :, :]).then_inc(so[u], 16)
                sp.wait_ge(so[1 - u], (i + 1) * 16)
                sp.sem_inc(free, 1)

            if layer == 1:
                load_attributes(0, 0)
                load_attributes(1, 1)
            with sp.Fori(0, NBLK // U - 1) as i:
                for u in range(U):
                    if layer == 1:
                        sp.wait_ge(tp, (i * U + u + 1) * 4)
                        c.alone(sp)
                        load_attributes(i * U + u + U, u)
                    store(i, u)
            store(NBLK // U - 1, 0)
            store(NBLK // U - 1, 1)
            sp.wait_ge(so[1], (NBLK // U + 1) * 16)

        @block.gpsimd
        def _(pool):
            pool.sem_inc(used, U)
            pool.sem_inc(q_used, U)
            with pool.Fori(0, NBLK // U) as i:
                for u in range(U):
                    blk = i * U + u
                    first_free = used if layer == 0 else q_used
                    pool.wait_ge(first_free, blk + 1)
                    c.alone(pool)
                    nd = 2 if layer == 0 else 1
                    for d in range(nd):
                        last = nc.gpsimd.tensor_copy(idx[:, u, d, :, :], c.rec[:, d, bass.ds(blk * B, B), :])
                    last.then_inc(staged, 1)
                    pool.wait_ge(staged, blk + 1)
                    c.alone(pool)
                    at_ = lambda d, j, w: bass.IndirectOffsetOnAxis(ap=idx[:, u, d, j, w:w + 1], axis=0)
                    for j in range(B):
                        if layer == 0:
                            pool.indirect_dma_start(g1[:, u, j, :], None, c.t1, at_(0, j, 1)).then_inc(gat[u], 16)
                            pool.indirect_dma_start(g2[:, u, j, :], None, c.t2, at_(1, j, 0)).then_inc(gat[u], 16)
                        else:
                            pool.indirect_dma_start(q[:, u, j, :], None, c.q, at_(0, j, 0)).then_inc(gat[u], 16)
                    if layer == 1:
                        pool.wait_ge(used, blk + 1)
                        c.alone(pool)
                        for j in range(B):
                            pool.indirect_dma_start(kv[:, u, j, :], None, c.kv, at_(0, j, 1)).then_inc(gat[u], 16)

        @block.vector
        def _(v):
            tt, copy = nc.vector.tensor_tensor, nc.vector.tensor_copy
            nc.vector.memset(st[:, :, :, 0:MX], 0.0)
            nc.vector.memset(st[:, :, :, MX:SW], -BIG)
            nc.vector.memset(sepb[:], -BIG)
            nc.vector.memset(at[:], -BIG)
            nc.vector.memset(cw[:], 0.0)
            nc.vector.memset(wv[:], 0.0)
            v.drain()
            nc.vector.memset(den[:], 0.0).then_inc(dump, 1)
            if layer == 1:
                v.sem_inc(ed, 4)
            with v.Fori(0, NBLK // U) as i:
                for u in range(U):
                    blk = i * U + u
                    for d in range(2):
                        k = d if layer == 0 else 0
                        copy(sepb[:, 4 * d:4 * d + 4, 1:B1],
                             c.sep[:, k, bass.ds(blk * B, B)].unsqueeze(1).to_broadcast([P, 4, B]))
                    if layer == 0:
                        v.wait_ge(gat[u], (i + 1) * ngat)
                        for d, g in enumerate((g1, g2)):
                            tt(at[:, 4 * d:4 * d + 4, 1:B1].rearrange("p h b -> p b h"), g[:, u, :, P:P + 4],
                               c.ar[:, bass.ds(blk * B, B), 4 * d:4 * d + 4], ALU.add)
                        v.drain()
                        nc.vector.scalar_tensor_tensor(out=at[:, :, 1:B1], in0=at[:, :, 1:B1], scalar=0.2,
                                                       in1=at[:, :, 1:B1], op0=ALU.mult, op1=ALU.max)
                    else:
                        v.wait_ge(gat[u], (i + 1) * ngat)
                        for m in range(4):
                            pair = psE[m][:, :].rearrange("p (j n) -> p j n", j=2)
                            v.wait_ge(ep, blk * 4 + m + 1)
                            tt(kv[:, u, 2 * m:2 * m + 2, 0:D], kv[:, u, 2 * m:2 * m + 2, 0:D], pair, ALU.add)
                            tt(kv[:, u, 2 * m:2 * m + 2, D:2 * D], kv[:, u, 2 * m:2 * m + 2, D:2 * D], pair,
                               ALU.add).then_inc(ed, 1)
                        v.drain()
                        tt(q[:, u, :, :], kv[:, u, :, 0:D], q[:, u, :, :], ALU.mult)
                        v.drain()
                        nc.vector.tensor_reduce(at[:, :, 1:B1].rearrange("p h b -> p b h"),
                                                q[:, u, :, :].rearrange("p b (h k) -> p b h k", k=C), AX.X,
                                                ALU.add).then_inc(q_used, 1)
                    v.drain()
                    flat = lambda a: a.rearrange("p h b -> p (h b)")
                    nc.vector.tensor_tensor_scan(flat(mt[:]), flat(sepb[:]), flat(at[:]), 0.0, ALU.add, ALU.max)
                    v.drain()
                    tt(ex[:, 0, :, :], mt[:, :, 0:B], sepb[:, :, 1:B1], ALU.add)
                    tt(ex[:, 1, :, :], at[:, :, 1:B1], mt[:, :, 1:B1], ALU.subtract)
                    v.drain()
                    copy(at[:, :, 0], mt[:, :, B])
                    tt(ex[:, 0, :, :], ex[:, 0, :, :], mt[:, :, 1:B1], ALU.subtract).then_inc(exd, 1)
                    v.wait_ge(cwd, blk + 1)
                    nc.vector.tensor_tensor_scan(flat(den[:]), flat(cw[:, 0, :, :]), flat(cw[:, 1, :, :]), 0.0,
                                                 ALU.mult, ALU.add).then_inc(dnd, 1)
                    wt = lambda h0, n: cw[:, 1, h0:h0 + n, 1:B1].rearrange("p h b -> p b h").unsqueeze(3).to_broadcast([P, B, n, C])
                    msg = lambda a: a.rearrange("p b (h k) -> p b h k", k=C)
                    by_edge = wv[:, :, 1:B1].rearrange("p n b -> p b n")
                    v.wait_ge(act_st, blk + 1)
                    if layer == 0:
                        for d, g in enumerate((g1, g2)):
                            last = tt(msg(by_edge[:, :, P * d:P * d + P]), msg(g[:, u, :, 0:P]), wt(4 * d, 4), ALU.mult)
                    else:
                        last = tt(msg(by_edge), msg(kv[:, u, :, D:2 * D]), wt(0, H), ALU.mult)
                    last.then_inc(used, 1)
                    v.drain()
                    copy(cw[:, 1, :, 0], den[:, :, B])
                    v.wait_ge(fxd, blk + 1)
                    nc.vector.tensor_tensor_scan(wv[:].rearrange("p n b -> p (n b)"), fx[:].rearrange("p n b -> p (n b)"),
                                                 wv[:].rearrange("p n b -> p (n b)"), 0.0, ALU.mult, ALU.add).then_inc(std, 1)
                    v.wait_ge(act_mt, blk + 1)
            c.alone(v)
            v.drain()
            v.wait_ge(act_st, NBLK + 1)
            copy(c.tail[:], st[:, 1, B - 1, :])

        @block.scalar
        def _(act):
            act.sem_inc(act_st, 1)

            def transposed_attributes(blk):
                if layer == 1:
                    for m in range(4):
                        act.wait_ge(tp, blk * 4 + m + 1)
                        nc.scalar.activation(eaT[:, m, :, :, :].rearrange("p a b c -> p (a b c)"), psT[m][:, :],
                                             ACT.Copy).then_inc(tcp, 1)

            def one_block(blk, u, ahead):
                if ahead:
                    transposed_attributes(blk + 1)
                act.wait_ge(exd, blk + 1)
                nc.scalar.activation(cw[:, :, :, 1:B1].rearrange("p x h b -> p (x h) b"),
                                     ex[:].rearrange("p x h b -> p (x h) b"), ACT.Exp).then_inc(cwd, 1)
                act.wait_ge(cwd, blk + 1)
                nc.scalar.activation(fx[:].rearrange("p (h k) b -> p h k b", k=C),
                                     cw[:, 0, :, :].unsqueeze(2).to_broadcast([P, H, C, B1]), ACT.Copy).then_inc(fxd, 1)
                act.wait_ge(dnd, blk + 1)
                act.wait_ge(free, blk + 1)
                nc.scalar.activation(st[:, u, :, MX:SW].rearrange("p b h -> p h b"), mt[:, :, 1:B1], ACT.Copy)
                nc.scalar.activation(st[:, u, :, DEN:MX].rearrange("p b h -> p h b"), den[:, :, 1:B1],
                                     ACT.Copy).then_inc(act_mt, 1)
                act.wait_ge(std, blk + 1)
                nc.scalar.activation(wv[:, :, 0], wv[:, :, B], ACT.Copy)
                nc.scalar.activation(st[:, u, :, 0:D], wv[:, :, 1:B1].rearrange("p n b -> p b n"),
                                     ACT.Copy).then_inc(act_st, 1)

            transposed_attributes(0)
            with act.Fori(0, NBLK // U - 1) as i:
                for u in range(U):
                    one_block(i * U + u, u, True)
            one_block(NBLK - 2, 0, True)
            one_block(NBLK - 1, 1, False)

        if layer == 1:
            @block.tensor
            def _(pe):
                pe.wait_ge(ld, 16)
                with pe.Fori(0, NBLK // U) as i:
                    for u in range(U):
                        blk = i * U + u
                        pe.wait_ge(eg[u], (i + 1) * 32)

                        def turn(m):
                            for j in range(2):
                                for k in range(2):
                                    o = (2 * j + k) * P
                                    last = nc.tensor.transpose(psT[m][:, o:o + P], ea[:, u, 2 * m + j, k * P:(k + 1) * P],
                                                               c.ident[:])
                            last.then_inc(tp, 1)

                        def product(m):
                            pe.wait_ge(tcp, blk * 4 + m + 1)
                            pe.wait_ge(ed, blk * 4 + m + 1)
                            for j in range(2):
                                for k in range(2):
                                    last = nc.tensor.matmul(psE[m][:, j * D:(j + 1) * D], eaT[:, m, j, k, :], we[:, k, :],
                                                            start=(k == 0), stop=(k == 1))
                            last.then_inc(ep, 1)

                        for m in range(4):
                            turn(m)
                        for m in range(4):
                            product(m)


def join_tails(c, layer):
    nc = c.nc
    nd = 2 if layer == 0 else 1
    hd = H // nd
    wd = hd * C
    with ExitStack() as s:
        sb = lambda n, shape, dt=FP32: s.enter_context(nc.sbuf_tensor(f"j{layer}_{n}", shape, dt))
        sem = c.semaphores(s, f"j{layer}_")
        pb = lambda n: s.enter_context(nc.psum_tensor(f"j{layer}_{n}", [P, 512], FP32))
        nxt = sb("nxt", [P, nd], I32)
        last, opened, key, first, before = (sb(n, [P, nd]) for n in ("last", "open", "key", "first", "before"))
        same, pen = sb("same", [P, nd, P]), sb("pen", [P, nd, P])
        junk = sb("junk", [P, nd, P])
        mrow = sb("mrow", [P, H, P])
        top, fac = sb("top", [P, H]), sb("fac", [P, H])
        scaled = sb("scaled", [P, nd, wd + hd])
        psK = [pb("psK0"), pb("psK1")]
        psM = [pb("psM0"), pb("psM1")]
        psG = [pb("psG0"), pb("psG1")]
        nz, nl, kd, kr, mr, xd, fd, sd, gd = (sem(n) for n in ("nz", "nl", "kd", "kr", "mr", "xd", "fd", "sd", "gd"))
        block = s.enter_context(nc.Block())

        @block.sync
        def _(sp):
            sp.wait_ge(nz, 1)
            for d, rec in enumerate((c.rec_d, c.rec_s)[0:nd]):
                with nc.allow_non_contiguous_dma("one word of each partition's first record"):
                    sp.dma_start(nxt[0:P - 1, d:d + 1],
                                 rec.rearrange("(p t) w -> p t w", t=T)[1:P, 0, d:d + 1]).then_inc(nl, 16)
            sp.wait_ge(nl, 16 * nd)

        @block.vector
        def _(v):
            tt, ts, copy = nc.vector.tensor_tensor, nc.vector.tensor_scalar, nc.vector.tensor_copy
            nc.vector.memset(nxt[:], -1).then_inc(nz, 1)
            for d in range(nd):
                copy(last[:, d:d + 1], c.rec[:, d, T - 1, d:d + 1])
            v.wait_ge(nl, 16 * nd)
            v.drain()
            tt(opened[:], last[:], nxt[:], ALU.is_equal)
            ts(last[:], last[:], 1.0, None, ALU.add)
            v.drain()
            tt(key[:], last[:], opened[:], ALU.mult)
            v.drain()
            ts(key[:], key[:], 1.0, None, ALU.subtract)
            v.drain()
            copy(junk[:, 0, 0:nd], key[:]).then_inc(kd, 1)
            v.wait_ge(kr, 1)
            for d in range(nd):
                ts(same[:, d, :], psK[d][:, 0:P], key[:, d:d + 1], None, ALU.is_equal)
            v.drain()
            for d in range(nd):
                nc.vector.scalar_tensor_tensor(out=junk[:, d, :], in0=same[:, d, :], scalar=1.0, in1=c.tri[:],
                                               op0=ALU.mult, op1=ALU.mult, accum_out=before[:, d:d + 1])
            ts(pen[:], same[:], 1.0, BIG, ALU.subtract, ALU.mult)
            v.drain()
            ts(first[:], before[:], 0.5, None, ALU.is_lt)
            v.wait_ge(mr, 1)
            for h in range(H):
                tt(mrow[:, h, :], psM[h // 4][:, (h % 4) * P:(h % 4 + 1) * P], pen[:, h // hd, :], ALU.add)
            v.drain()
            tt(first[:], first[:], opened[:], ALU.mult)
            nc.vector.tensor_reduce(top[:], mrow[:], AX.X, ALU.max)
            v.drain()
            tt(first[:], first[:], last[:], ALU.mult)
            tt(fac[:], c.tail[:, MX:SW], top[:], ALU.subtract).then_inc(xd, 1)
            v.drain()
            ts(c.fkey[:, 0:nd], first[:], 1.0, None, ALU.subtract)
            v.wait_ge(fd, 1)
            for d in range(nd):
                tt(scaled[:, d, 0:wd].rearrange("p (h k) -> p h k", k=C),
                   c.tail[:, d * wd:(d + 1) * wd].rearrange("p (h k) -> p h k", k=C),
                   fac[:, d * hd:(d + 1) * hd].unsqueeze(2).to_broadcast([P, hd, C]), ALU.mult)
                op = tt(scaled[:, d, wd:wd + hd], c.tail[:, DEN + d * hd:DEN + (d + 1) * hd],
                        fac[:, d * hd:(d + 1) * hd], ALU.mult)
            op.then_inc(sd, 1)
            v.wait_ge(gd, 1)
            g = c.carry[:, 0:nd * (wd + 2 * hd + 1)].rearrange("p (d w) -> p d w", d=nd)
            for d in range(nd):
                copy(g[:, d, 0:wd + hd], psG[d][:, 0:wd + hd])
                copy(g[:, d, wd + hd:wd + 2 * hd], top[:, d * hd:(d + 1) * hd])
            nc.vector.memset(g[:, :, wd + 2 * hd:wd + 2 * hd + 1], 1.0)
            v.drain()

        @block.scalar
        def _(act):
            act.wait_ge(xd, 1)
            nc.scalar.activation(fac[:], fac[:], ACT.Exp).then_inc(fd, 1)

        @block.tensor
        def _(pe):
            for h in range(H):
                op = nc.tensor.matmul(psM[h // 4][:, (h % 4) * P:(h % 4 + 1) * P],
                                      c.tail[:, MX + h:MX + h + 1].to_broadcast([P, P]), c.ident[:], start=True, stop=True)
            op.then_inc(mr, 1)
            pe.wait_ge(kd, 1)
            for d in range(nd):
                op = nc.tensor.matmul(psK[d][:, 0:P], key[:, d:d + 1].to_broadcast([P, P]), c.ident[:], start=True, stop=True)
            op.then_inc(kr, 1)
            pe.wait_ge(sd, 1)
            for d in range(nd):
                op = nc.tensor.matmul(psG[d][:, 0:wd + hd], same[:, d, :], scaled[:, d, :], start=True, stop=True)
            op.then_inc(gd, 1)


def combine(c, layer):
    nc, A = c.nc, c.A
    nd = 2 if layer == 0 else 1
    hd = H // nd
    wd = hd * C
    wc = wd + 2 * hd + 1
    parts = 3 if layer == 0 else 2
    with ExitStack() as s:
        sb = lambda n, shape, dt=FP32: s.enter_context(nc.sbuf_tensor(f"c{layer}_{n}", shape, dt))
        sem = c.semaphores(s, f"c{layer}_")
        pb = lambda n: s.enter_context(nc.psum_tensor(f"c{layer}_{n}", [P, 512], FP32))
        endn = sb("endn", [P, nd, NI], I32)
        idx = sb("idx", [P, nd, GT], I32)
        r = sb("r", [P, nd, GT, SW])
        nrow = sb("nrow", [P, P])
        oh = sb("oh", [P, nd, GT, P])
        cc = sb("cc", [P, nd, GT, wc])
        own = sb("own", [P, 2, GT, TW])
        top = sb("top", [P, nd, GT, hd])
        mc = sb("mc", [P, nd, GT, hd])
        eself = sb("eself", [P, nd, GT, hd])
        xa = sb("xa", [P, nd, parts, GT, hd])
        dsum, dtmp = sb("dsum", [P, nd, GT, hd]), sb("dtmp", [P, nd, parts, GT, hd])
        pres = sb("pres", [P, nd, GT])
        num, tmp = sb("num", [P, GT, D]), sb("tmp", [P, GT, D])
        psC = [pb("psC0"), pb("psC1")]
        ld, gat, tl, ohd, cm, ccd, xd, fd, used, tr, tc, mm, fs = (sem(n) for n in (
            "ld", "gat", "tl", "ohd", "cm", "ccd", "xd", "fd", "used", "tr", "tc", "mm", "fs"))
        catd = sem("catd")
        if layer == 0:
            cT = sb("cT", [P, 2, GT * P])
            wf = sb("wf", [P, 2, D])
            vec = sb("vec", [P, 6, D])
            psT, psF = [pb("psT0"), pb("psT1")], [pb("psF0"), pb("psF1")]
        nld = 16 * (nd + (8 if layer == 0 else 0))
        block = s.enter_context(nc.Block())

        @block.sync
        def _(sp):
            for d in range(nd):
                sp.dma_start(endn[:, d, :], c.ends[d][1][0:NI * P].rearrange("(p i) -> p i", i=NI)).then_inc(ld, 16)
            if layer == 0:
                sp.dma_start(wf[:], A["L0_gnn_W_fuse"].rearrange("(k p) n -> p k n", p=P)).then_inc(ld, 16)
                sp.dma_start(vec[:, 0, 0:P], row_bcast(A["L0_gnn_b_f"], 0, P)).then_inc(ld, 16)
                sp.dma_start(vec[:, 0, P:D], row_bcast(A["L0_gnn_b_b"], 0, P)).then_inc(ld, 16)
                for n, name in enumerate(("b_fuse", "run_mean", "run_var", "gamma", "beta")):
                    sp.dma_start(vec[:, 1 + n, :], row_bcast(A["L0_gnn_" + name], 0, D)).then_inc(ld, 16)
                with sp.Fori(0, NG) as g:
                    sp.wait_ge(used, g + 1)
                    for d, tab in enumerate((c.t1, c.t2)):
                        sp.dma_start(own[:, d, :, :],
                                     tab.rearrange("(p i) w -> p (i w)", i=NI)[:, bass.ds(g * (GT * TW), GT * TW)]).then_inc(tl, 16)

        @block.gpsimd
        def _(pool):
            pool.wait_ge(ld, nld)
            with pool.Fori(0, NG) as g:
                pool.wait_ge(used, g + 1)
                c.alone(pool)
                nc.gpsimd.tensor_copy(idx[:], endn[:, :, bass.ds(g * GT, GT)])
                pool.drain()
                for d in range(nd):
                    for j in range(GT):
                        pool.indirect_dma_start(r[:, d, j, :], None, c.state[layer],
                                                bass.IndirectOffsetOnAxis(ap=idx[:, d, j:j + 1], axis=0)).then_inc(gat, 16)

        @block.vector
        def _(v):
            tt, ts, copy = nc.vector.tensor_tensor, nc.vector.tensor_scalar, nc.vector.tensor_copy
            v.sem_inc(used, 1)
            v.wait_ge(ld, nld)
            ts(nrow[:], c.cols[:], float(NI), None, ALU.mult)
            if layer == 0:
                ts(vec[:, 3, :], vec[:, 3, :], BN_EPS, None, ALU.add).then_inc(xd, 1)
                v.wait_ge(fd, 1)
                nc.vector.reciprocal(vec[:, 3, :], vec[:, 3, :])
                tt(vec[:, 1, :], vec[:, 1, :], vec[:, 2, :], ALU.subtract)
                v.drain()
                tt(vec[:, 4, :], vec[:, 4, :], vec[:, 3, :], ALU.mult)
                v.drain()
                tt(vec[:, 1, :], vec[:, 1, :], vec[:, 4, :], ALU.mult)
                v.drain()
                tt(vec[:, 5, :], vec[:, 5, :], vec[:, 1, :], ALU.add)
            x0 = 1 if layer == 0 else 0
            v.drain()
            with v.Fori(0, NG) as g:
                for d in range(nd):
                    for j in range(GT):
                        last = ts(oh[:, d, j, :], nrow[:], float(j), c.fkey[:, d:d + 1], ALU.add, ALU.is_equal)
                last.then_inc(ohd, 1)
                v.drain()
                ts(nrow[:], nrow[:], float(GT), None, ALU.add)
                v.wait_ge(ccd, (g + 1) * (nd * GT))
                v.wait_ge(gat, (g + 1) * (nd * GT * 16))
                if layer == 0:
                    v.wait_ge(tl, (g + 1) * 32)
                ts(pres[:], cc[:, :, :, wc - 1], 1.0, BIG, ALU.subtract, ALU.mult)
                if layer == 0:
                    tt(eself[:], own[:, :, :, 128:132], own[:, :, :, 132:136], ALU.add)
                v.drain()
                for d in range(nd):
                    tt(mc[:, d], cc[:, d, :, wd + hd:wd + 2 * hd], pres[:, d, :].unsqueeze(2).to_broadcast([P, GT, hd]), ALU.add)
                    if layer == 0:
                        nc.vector.scalar_tensor_tensor(out=eself[:, d], in0=eself[:, d], scalar=0.2, in1=eself[:, d],
                                                       op0=ALU.mult, op1=ALU.max)
                v.drain()
                for d in range(nd):
                    tt(top[:, d], mc[:, d], r[:, d, :, MX + d * hd:MX + (d + 1) * hd], ALU.max)
                v.drain()
                if layer == 0:
                    tt(top[:], top[:], eself[:], ALU.max)
                    v.drain()
                for d in range(nd):
                    tt(xa[:, d, 0], r[:, d, :, MX + d * hd:MX + (d + 1) * hd], top[:, d], ALU.subtract)
                    last = tt(xa[:, d, 1], mc[:, d], top[:, d], ALU.subtract)
                    if layer == 0:
                        last = tt(xa[:, d, 2], eself[:, d], top[:, d], ALU.subtract)
                last.then_inc(xd, 1)
                v.wait_ge(fd, g + 1 + x0)
                for d in range(nd):
                    tt(dtmp[:, d, 0], r[:, d, :, DEN + d * hd:DEN + (d + 1) * hd], xa[:, d, 0], ALU.mult)
                    tt(dtmp[:, d, 1], cc[:, d, :, wd:wd + hd], xa[:, d, 1], ALU.mult)
                v.drain()
                tt(dsum[:], dtmp[:, :, 0], dtmp[:, :, 1], ALU.add)
                v.drain()
                if layer == 0:
                    tt(dsum[:], dsum[:], xa[:, :, 2], ALU.add)
                    v.drain()
                    ts(dsum[:], dsum[:], 1e-16, None, ALU.add)
                else:
                    ts(dsum[:], dsum[:], 1e-30, None, ALU.max)
                v.drain()
                nc.vector.reciprocal(dsum[:], dsum[:])
                v.drain()
                for d in range(nd):
                    for n in range(parts):
                        tt(xa[:, d, n], xa[:, d, n], dsum[:, d], ALU.mult)
                v.drain()
                hk = lambda a: a.rearrange("p i (h k) -> p i h k", k=C)
                for n in range(parts):
                    for d in range(nd):
                        src = (r[:, d, :, d * wd:(d + 1) * wd], cc[:, d, :, 0:wd], own[:, d, :, 0:wd] if layer == 0 else None)[n]
                        dst = num if n == 0 else tmp
                        tt(hk(dst[:, :, d * wd:(d + 1) * wd]), hk(src),
                           xa[:, d, n].unsqueeze(3).to_broadcast([P, GT, hd, C]), ALU.mult)
                    v.drain()
                    if n:
                        tt(num[:], num[:], tmp[:], ALU.add)
                        v.drain()
                xg = c.x[:, bass.ds(g * (GT * D), GT * D)]
                flat = lambda a: a.rearrange("p i d -> p (i d)")
                if layer == 0:
                    tt(num[:], num[:], vec[:, 0, :].unsqueeze(1).to_broadcast([P, GT, D]), ALU.add).then_inc(catd, 1)
                    v.sem_inc(used, 1)
                    for j in range(GT):
                        v.wait_ge(mm, g * GT + j + 1)
                        tt(tmp[:, j, :], psF[j % 2][:, 0:D], vec[:, 4, :], ALU.mult).then_inc(fs, 1)
                    v.drain()
                    tt(tmp[:], tmp[:], vec[:, 5, :].unsqueeze(1).to_broadcast([P, GT, D]), ALU.add)
                    v.drain()
                    nc.vector.scalar_tensor_tensor(out=xg, in0=flat(tmp[:]), scalar=0.0, in1=xg, op0=ALU.max, op1=ALU.add)
                else:
                    tt(xg, xg, flat(num[:]), ALU.add).then_inc(used, 1)
                v.drain()

        @block.scalar
        def _(act):
            if layer == 0:
                act.wait_ge(xd, 1)
                nc.scalar.activation(vec[:, 3, :], vec[:, 3, :], ACT.Sqrt).then_inc(fd, 1)
            x0 = 1 if layer == 0 else 0
            with act.Fori(0, NG) as g:
                for n in range(nd * GT):
                    act.wait_ge(cm, g * (nd * GT) + n + 1)
                    nc.scalar.activation(cc[:, n // GT, n % GT, :], psC[n % 2][:, 0:wc], ACT.Copy).then_inc(ccd, 1)
                act.wait_ge(xd, g + 1 + x0)
                nc.scalar.activation(xa[:].rearrange("p a b i h -> p (a b i h)"),
                                     xa[:].rearrange("p a b i h -> p (a b i h)"), ACT.Exp).then_inc(fd, 1)
                if layer == 0:
                    for j in range(GT):
                        act.wait_ge(tr, g * GT + j + 1)
                        nc.scalar.activation(cT[:, :, j * P:(j + 1) * P],
                                             psT[j % 2][:, 0:2 * P].rearrange("p (k n) -> p k n", k=2), ACT.Copy).then_inc(tc, 1)

        @block.tensor
        def _(pe):
            pe.wait_ge(ld, nld)
            with pe.Fori(0, NG) as g:
                pe.wait_ge(ohd, g + 1)
                for n in range(nd * GT):
                    if n >= 2:
                        pe.wait_ge(ccd, g * (nd * GT) + n - 1)
                    nc.tensor.matmul(psC[n % 2][:, 0:wc], oh[:, n // GT, n % GT, :],
                                     c.carry[:, (n // GT) * wc:(n // GT + 1) * wc], start=True, stop=True).then_inc(cm, 1)
                if layer == 0:
                    pe.wait_ge(catd, g + 1)
                    for j in range(GT):
                        if j >= 2:
                            pe.wait_ge(tc, g * GT + j - 1)
                        for k in range(2):
                            last = nc.tensor.transpose(psT[j % 2][:, k * P:(k + 1) * P], num[:, j, k * P:(k + 1) * P], c.ident[:])
                        last.then_inc(tr, 1)
                    for j in range(GT):
                        pe.wait_ge(tc, g * GT + j + 1)
                        if j >= 2:
                            pe.wait_ge(fs, g * GT + j - 1)
                        for k in range(2):
                            last = nc.tensor.matmul(psF[j % 2][:, 0:D], cT[:, k, j * P:(j + 1) * P], wf[:, k, :],
                                                    start=(k == 0), stop=(k == 1))
                        last.then_inc(mm, 1)
                pe.wait_ge(ccd, (g + 1) * (nd * GT))


def normalize_group(c, v, w, xln, g, vin, root, xr):
    layernorm_stats(c, v, w, lambda j: c.x[:, bass.ds((g * GT + j) * D, D)], GT, vin, root, g + 1)
    for j in range(GT):
        c.nc.vector.tensor_scalar(xln[:, j, 0:D], c.x[:, bass.ds((g * GT + j) * D, D)], w["mv"][:, j, 0:1],
                                  w["rstd"][:, j:j + 1], ALU.subtract, ALU.mult).then_inc(xr, 1)


def root_and_copies(c, act, w, g, vin, root, tr, tc, psT, xT):
    act.wait_ge(vin, g + 1)
    c.nc.scalar.activation(w["rstd"][:], w["rstd"][:], ACT.Sqrt).then_inc(root, 1)
    for j in range(GT):
        act.wait_ge(tr, g * GT + j + 1)
        c.nc.scalar.activation(xT[:, :, j * P:(j + 1) * P], psT[j % 2][:, 0:2 * P].rearrange("p (k n) -> p k n", k=2),
                               ACT.Copy).then_inc(tc, 1)


def transposes(c, pe, xln, g, xr, tr, tc, psT):
    for j in range(GT):
        pe.wait_ge(xr, g * GT + j + 1)
        if j >= 2:
            pe.wait_ge(tc, g * GT + j - 1)
        for k in range(2):
            last = c.nc.tensor.transpose(psT[j % 2][:, k * P:(k + 1) * P], xln[:, j, k * P:(k + 1) * P], c.ident[:])
        last.then_inc(tr, 1)


def experts(c):
    nc, A = c.nc, c.A
    HC = HID // P
    halves = ((0, 4), (4, 3))
    with ExitStack() as s:
        sb = lambda n, shape, dt=FP32: s.enter_context(nc.sbuf_tensor("m_" + n, shape, dt))
        sem = c.semaphores(s, "m_")
        pb = lambda n: s.enter_context(nc.psum_tensor("m_" + n, [P, 512], FP32))
        w1, w2 = sb("w1", [P, EXP, 2, HID]), sb("w2", [P, EXP, HC, D])
        wg, bg = sb("wg", [P, 2, EXP]), sb("bg", [P, EXP])
        b1, b2 = sb("b1", [P, EXP, HC]), sb("b2", [EXP, D])
        w = {"stats": sb("st", [P, GT, 6]), "mv": sb("mv", [P, GT, 2]), "rstd": sb("rs", [P, GT])}
        xln, xT = sb("xln", [P, GT, D]), sb("xT", [P, 2, GT * P])
        hT = sb("hT", [P, 2, HC, 512])
        gate, rank, mask = sb("gate", [P, GT, EXP]), sb("rank", [P, GT, EXP]), sb("mask", [P, GT, EXP])
        gt, eq = sb("gt", [P, GT, EXP, EXP]), sb("eq", [P, GT, EXP, EXP])
        lower = sb("lower", [P, EXP, EXP])
        maskT = sb("maskT", [EXP, GT * P])
        psM = [pb("psM0"), pb("psM1")]
        psH = [pb(f"psH{n}") for n in range(HC)]
        psY = [pb("psY0"), pb("psY1")]
        ld, lw, vin, root, xr, tr, tc, gd, md, mt_, mc, bt, ba, hp, gelud, yd, ya, gfree = (sem(n) for n in (
            "ld", "lw", "vin", "root", "xr", "tr", "tc", "gd", "md", "mt", "mc", "bt", "ba", "hp", "gelud", "yd", "ya", "gfree"))
        block = s.enter_context(nc.Block())

        @block.sync
        def _(sp):
            sp.dma_start(wg[:], A["L0_ffn_Wg"].rearrange("(k p) n -> p k n", p=P)).then_inc(ld, 16)
            sp.dma_start(bg[:], row_bcast(A["L0_ffn_bg"], 0, EXP)).then_inc(ld, 16)
            sp.dma_start(b2[:], A["L0_ffn_b2"]).then_inc(ld, 16)
            with nc.allow_non_contiguous_dma("biases one word per partition"):
                for e in range(EXP):
                    sp.dma_start(b1[:, e, :], A["L0_ffn_b1"][e, :].rearrange("(k p) -> p k", p=P)).then_inc(ld, 16)
            for e in range(EXP):
                sp.dma_start(w1[:, e, :, :], A["L0_ffn_W1"][e].rearrange("(k p) n -> p k n", p=P)).then_inc(ld, 16)
                sp.dma_start(w2[:, e, :, :], A["L0_ffn_W2"][e].rearrange("(k p) n -> p k n", p=P)).then_inc(ld, 16)
            sp.wait_ge(ld, 16 * (3 + 3 * EXP))

        @block.gpsimd
        def _(pool):
            nc.gpsimd.memset(lower[:], 1.0)
            pool.drain()
            nc.gpsimd.affine_select(out=lower[:], in_=lower[:], compare_op=ALU.is_gt, fill=0.0, base=0,
                                    pattern=[[1, EXP], [-1, EXP]], channel_multiplier=0).then_inc(lw, 1)

        @block.vector
        def _(v):
            tt, ts = nc.vector.tensor_tensor, nc.vector.tensor_scalar
            v.wait_ge(lw, 1)
            v.wait_ge(ld, 16 * (3 + 3 * EXP))
            v.sem_inc(ya, 2)
            with v.Fori(0, NG) as g:
                normalize_group(c, v, w, xln, g, vin, root, xr)
                v.wait_ge(gd, g + 1)
                tt(gate[:], psM[0][:, 0:GT * EXP].rearrange("p (i e) -> p i e", e=EXP),
                   bg[:].unsqueeze(1).to_broadcast([P, GT, EXP]), ALU.add)
                v.drain()
                gj = gate[:].unsqueeze(2).to_broadcast([P, GT, EXP, EXP])
                gi = gate[:].unsqueeze(3).to_broadcast([P, GT, EXP, EXP])
                tt(gt[:], gj, gi, ALU.is_gt)
                tt(eq[:], gj, gi, ALU.is_equal)
                v.drain()
                tt(eq[:], eq[:], lower[:].unsqueeze(1).to_broadcast([P, GT, EXP, EXP]), ALU.mult)
                v.drain()
                tt(gt[:], gt[:], eq[:], ALU.add)
                v.drain()
                nc.vector.tensor_reduce(rank[:], gt[:], AX.X, ALU.add)
                v.drain()
                ts(mask[:], rank[:], 1.5, None, ALU.is_lt).then_inc(md, 1)
                v.drain()
                for j in range(GT):
                    v.wait_ge(bt, g * GT + j + 1)
                    xj = c.x[:, bass.ds((g * GT + j) * D, D)]
                    tt(xj, psM[j % 2][:, 0:D], xj, ALU.add).then_inc(ba, 1)
                v.drain()
                for e in range(EXP):
                    for t0, n in halves:
                        for t in range(t0, t0 + n):
                            y = e * GT + t
                            v.wait_ge(yd, g * (EXP * GT) + y + 1)
                            xj = c.x[:, bass.ds((g * GT + t) * D, D)]
                            nc.vector.scalar_tensor_tensor(out=xj, in0=psY[y % 2][:, 0:D], scalar=mask[:, t, e:e + 1],
                                                           in1=xj, op0=ALU.mult, op1=ALU.add).then_inc(ya, 1)
                        v.drain()

        @block.scalar
        def _(act):
            act.wait_ge(ld, 16 * (3 + 3 * EXP))
            with act.Fori(0, NG) as g:
                root_and_copies(c, act, w, g, vin, root, tr, tc, psM, xT)
                for q in range(2):
                    act.wait_ge(mt_, g * 2 + q + 1)
                    t0, n = halves[q]
                    nc.scalar.activation(maskT[:, t0 * P:(t0 + n) * P], psM[q][0:EXP, 0:n * P], ACT.Copy).then_inc(mc, 1)
                for u in range(2 * EXP):
                    n = halves[u % 2][1] * P
                    for k in range(HC):
                        act.wait_ge(hp, (g * (2 * EXP) + u) * HC + k + 1)
                        nc.scalar.activation(hT[:, u % 2, k, 0:n], psH[k][:, 0:n], ACT.Gelu,
                                             bias=b1[:, u // 2, k:k + 1]).then_inc(gelud, 1)

        @block.tensor
        def _(pe):
            mm = nc.tensor.matmul
            pe.wait_ge(ld, 16 * (3 + 3 * EXP))
            pe.sem_inc(gelud, HC)
            with pe.Fori(0, NG) as g:
                transposes(c, pe, xln, g, xr, tr, tc, psM)
                pe.wait_ge(tc, (g + 1) * GT)
                for j in range(GT):
                    for k in range(2):
                        last = mm(psM[0][:, j * EXP:(j + 1) * EXP], xT[:, k, j * P:(j + 1) * P], wg[:, k, :],
                                  start=(k == 0), stop=(k == 1))
                last.then_inc(gd, 1)
                pe.wait_ge(md, g + 1)
                for q, (t0, n) in enumerate(halves):
                    for j in range(n):
                        last = nc.tensor.transpose(psM[q][0:EXP, j * P:(j + 1) * P], mask[:, t0 + j, :], c.ident[:])
                    last.then_inc(mt_, 1)
                pe.wait_ge(mc, g * 2 + 2)
                for j in range(GT):
                    if j >= 2:
                        pe.wait_ge(ba, g * GT + j - 1)
                    mm(psM[j % 2][:, 0:D], maskT[:, j * P:(j + 1) * P], b2[:], start=True, stop=True).then_inc(bt, 1)

                def hidden(u):
                    t0, n = halves[u % 2]
                    for k in range(HC):
                        pe.wait_ge(gelud, (g * (2 * EXP) + u) * HC + k + 1)
                        for q in range(2):
                            last = mm(psH[k][:, 0:n * P], w1[:, u // 2, q, k * P:(k + 1) * P],
                                      xT[:, q, t0 * P:(t0 + n) * P], start=(q == 0), stop=(q == 1))
                        last.then_inc(hp, 1)

                def output(u):
                    t0, n = halves[u % 2]
                    pe.wait_ge(gelud, (g * (2 * EXP) + u) * HC + 2 * HC)
                    for t in range(t0, t0 + n):
                        y = (u // 2) * GT + t
                        pe.wait_ge(ya, g * (EXP * GT) + y + 1)
                        for k in range(HC):
                            last = mm(psY[y % 2][:, 0:D], hT[:, u % 2, k, (t - t0) * P:(t - t0 + 1) * P], w2[:, u // 2, k, :],
                                      start=(k == 0), stop=(k == HC - 1))
                        last.then_inc(yd, 1)

                hidden(0)
                for u in range(1, 2 * EXP):
                    hidden(u)
                    output(u - 1)
                output(2 * EXP - 1)
                pe.wait_ge(ba, (g + 1) * GT)


def layer1_tables(c):
    nc, A = c.nc, c.A
    with ExitStack() as s:
        sb = lambda n, shape, dt=FP32: s.enter_context(nc.sbuf_tensor("q_" + n, shape, dt))
        sem = c.semaphores(s, "q_")
        pb = lambda n: s.enter_context(nc.psum_tensor("q_" + n, [P, 512], FP32))
        wall, ball = sb("w", [P, 2, 4 * D]), sb("b", [P, 4 * D])
        w = {"stats": sb("st", [P, GT, 6]), "mv": sb("mv", [P, GT, 2]), "rstd": sb("rs", [P, GT])}
        xln, xT = sb("xln", [P, GT, D]), sb("xT", [P, 2, GT * P])
        qrow, kvrow, srow = sb("qrow", [P, GT, D]), sb("kvrow", [P, GT, 2 * D]), sb("srow", [P, GT, D])
        psT = [pb("psT0"), pb("psT1")]
        psO = [[pb(f"psO{r}{n}") for n in range(2)] for r in range(2)]
        ld, vin, root, xr, tr, tc, mm, od, rows, st = (sem(n) for n in (
            "ld", "vin", "root", "xr", "tr", "tc", "mm", "od", "rows", "st"))
        block = s.enter_context(nc.Block())

        @block.sync
        def _(sp):
            for n, (wn, bn) in enumerate((("Wq", "bq"), ("Wk", "bk"), ("Wv", "bv"), ("Ws", "bs"))):
                sp.dma_start(wall[:, :, n * D:(n + 1) * D], A["L1_gnn_" + wn].rearrange("(k p) n -> p k n", p=P)).then_inc(ld, 16)
                sp.dma_start(ball[:, n * D:(n + 1) * D], row_bcast(A["L1_gnn_" + bn], 0, D)).then_inc(ld, 16)
            with sp.Fori(0, NG) as g:
                sp.wait_ge(rows, g + 1)
                sp.dma_start(c.q.rearrange("(p i) w -> p (i w)", i=NI)[:, bass.ds(g * (GT * D), GT * D)], qrow[:]).then_inc(st, 16)
                sp.dma_start(c.kv.rearrange("(p i) w -> p (i w)", i=NI)[:, bass.ds(g * (2 * GT * D), 2 * GT * D)],
                             kvrow[:]).then_inc(st, 16)
            sp.wait_ge(st, 32 * NG)

        @block.vector
        def _(v):
            tt = nc.vector.tensor_tensor
            v.wait_ge(ld, 128)
            with v.Fori(0, NG) as g:
                normalize_group(c, v, w, xln, g, vin, root, xr)
                for j in range(GT):
                    v.wait_ge(mm, g * GT + j + 1)
                    o = psO[j % 2]
                    tt(qrow[:, j, :], o[0][:, 0:D], ball[:, 0:D], ALU.add)
                    tt(kvrow[:, j, 0:D], o[0][:, D:2 * D], ball[:, D:2 * D], ALU.add)
                    tt(kvrow[:, j, D:2 * D], o[1][:, 0:D], ball[:, 2 * D:3 * D], ALU.add)
                    tt(srow[:, j, :], o[1][:, D:2 * D], ball[:, 3 * D:4 * D], ALU.add).then_inc(od, 1)
                v.drain()
                nc.vector.tensor_scalar(qrow[:], qrow[:], float(C) ** -0.5, None, ALU.mult).then_inc(rows, 1)
                xg = c.x[:, bass.ds(g * (GT * D), GT * D)]
                tt(xg, xg, srow[:].rearrange("p i d -> p (i d)"), ALU.add)
                v.drain()
                v.wait_ge(st, (g + 1) * 32)

        @block.scalar
        def _(act):
            with act.Fori(0, NG) as g:
                root_and_copies(c, act, w, g, vin, root, tr, tc, psT, xT)

        @block.tensor
        def _(pe):
            pe.wait_ge(ld, 128)
            with pe.Fori(0, NG) as g:
                transposes(c, pe, xln, g, xr, tr, tc, psT)
                for j in range(GT):
                    pe.wait_ge(tc, g * GT + j + 1)
                    if j >= 2:
                        pe.wait_ge(od, g * GT + j - 1)
                    for n in range(2):
                        for k in range(2):
                            last = nc.tensor.matmul(psO[j % 2][n][:, :], xT[:, k, j * P:(j + 1) * P],
                                                    wall[:, k, n * 512:(n + 1) * 512], start=(k == 0), stop=(k == 1))
                    last.then_inc(mm, 1)
                pe.wait_ge(od, (g + 1) * GT)


def reload_edges(c):
    nc = c.nc
    with ExitStack() as s:
        rl = s.enter_context(nc.semaphore("r_ld"))
        block = s.enter_context(nc.Block())

        @block.sync
        def _(sp):
            sp.dma_start(c.rec[:, 0, :, :], c.rec_d.rearrange("(p t) w -> p t w", p=P)).then_inc(rl, 16)
            sp.wait_ge(rl, 16)

        @block.vector
        def _(v):
            v.wait_ge(rl, 16)
            k = c.rec[:, 0, :, 0]
            nc.vector.memset(c.sep[:, 0, 0:1], 0.0)
            nc.vector.tensor_tensor(c.sep[:, 0, 1:T], k[:, 1:T], k[:, 0:T - 1], ALU.is_equal)
            v.drain()
            nc.vector.tensor_scalar(c.sep[:], c.sep[:], 1.0, BIG, ALU.subtract, ALU.mult)
            v.drain()


SH, SG, SC = 8, 64, 64
SQ = SH * SG // P


def slice_attention(c):
    nc, A = c.nc, c.A
    ones = D
    XW = D + 1
    with ExitStack() as s:
        sb = lambda n, shape, dt=FP32: s.enter_context(nc.sbuf_tensor("f_" + n, shape, dt))
        sem = c.semaphores(s, "f_")
        wx, wfx = sb("wx", [P, 2, 512]), sb("wfx", [P, 2, 512])
        wsl, wqkv = sb("wsl", [SC, SG]), sb("wqkv", [SC, 3, SC])
        wout = sb("wout", [SC, SH, D])
        bx = sb("bx", [SC, SH])
        bsl, bfx, bout, temp = sb("bsl", [P, SG]), sb("bfx", [SG, 512]), sb("bout", [P, D]), sb("temp", [P, SH])
        wxT = sb("wxT", [SC, SH, 2, P])
        wc, bc = sb("wc", [P, 2, 512]), sb("bc", [P, 512])
        with ExitStack() as s1:
            psA = [s1.enter_context(nc.psum_tensor(f"f1_psA{n}", [P, 512], FP32)) for n in range(4)]
            psW = [s1.enter_context(nc.psum_tensor(f"f1_psW{n}", [P, 512], FP32)) for n in range(2)]
            psB = s1.enter_context(nc.psum_tensor("f1_psB", [P, 512], FP32))
            ld, t1, t1c, w1, td = (sem(n) for n in ("ld", "t1", "t1c", "w1", "td"))
            block = s1.enter_context(nc.Block())

            @block.sync
            def _(sp):
                f = "L1_ffn_"
                sp.dma_start(wx[:], A[f + "W_x"].rearrange("(k p) n -> p k n", p=P)).then_inc(ld, 16)
                sp.dma_start(wfx[:], A[f + "W_fx"].rearrange("(k p) n -> p k n", p=P)).then_inc(ld, 16)
                sp.dma_start(wsl[:], A[f + "W_slice"]).then_inc(ld, 16)
                for n, name in enumerate(("W_q", "W_k", "W_v")):
                    sp.dma_start(wqkv[:, n, :], A[f + name]).then_inc(ld, 16)
                sp.dma_start(wout[:], A[f + "W_out"].rearrange("(h c) n -> c h n", c=SC)).then_inc(ld, 16)
                with nc.allow_non_contiguous_dma("biases one word per partition"):
                    sp.dma_start(bx[:], A[f + "b_x"].rearrange("(h c) -> c h", c=SC)).then_inc(ld, 16)
                sp.dma_start(bsl[:], row_bcast(A[f + "b_slice"], 0, SG)).then_inc(ld, 16)
                sp.dma_start(bfx[:], A[f + "b_fx"].rearrange("(a n) -> a n", a=1).to_broadcast([SG, 512])).then_inc(ld, 16)
                sp.dma_start(bout[:], row_bcast(A[f + "b_out"], 0, D)).then_inc(ld, 16)
                sp.dma_start(temp[:], A[f + "temperature"].rearrange("a h b c -> a (h b c)").to_broadcast([P, SH])).then_inc(ld, 16)
                sp.wait_ge(ld, 192)

            @block.tensor
            def _(pe):
                pe.wait_ge(ld, 192)
                for h in range(SH):
                    for k in range(2):
                        o = ((h % 2) * 2 + k) * P
                        last = nc.tensor.transpose(psA[h // 2][0:SC, o:o + P], wx[:, k, h * SC:(h + 1) * SC], c.ident[:])
                last.then_inc(t1, 1)
                pe.wait_ge(t1c, 1)
                for h in range(SH):
                    for k in range(2):
                        nc.tensor.matmul(psW[k][:, h * SG:(h + 1) * SG], wxT[:, h, k, :], wsl[:], start=True, stop=True)
                    last = nc.tensor.matmul(psB[:, h * SG:(h + 1) * SG], bx[:, h:h + 1].to_broadcast([SC, P]), wsl[:],
                                            start=True, stop=True)
                last.then_inc(w1, 1)

            @block.scalar
            def _(act):
                act.wait_ge(t1, 1)
                for q in range(4):
                    last = nc.scalar.activation(wxT[:, 2 * q:2 * q + 2, :, :].rearrange("p a b c -> p (a b c)"),
                                                psA[q][0:SC, :], ACT.Copy)
                last.then_inc(t1c, 1)

            @block.vector
            def _(v):
                tt, ts = nc.vector.tensor_tensor, nc.vector.tensor_scalar
                v.wait_ge(ld, 192)
                ts(temp[:], temp[:], 0.1, 5.0, ALU.max, ALU.min)
                v.drain()
                nc.vector.reciprocal(temp[:], temp[:])
                v.wait_ge(w1, 1)
                v.drain()
                hg = lambda a: a.rearrange("p (h g) -> p h g", g=SG)
                it = temp[:].unsqueeze(2).to_broadcast([P, SH, SG])
                for k in range(2):
                    tt(hg(wc[:, k, :]), hg(psW[k][:, :]), it, ALU.mult)
                tt(hg(bc[:]), hg(psB[:, :]), bsl[:].unsqueeze(1).to_broadcast([P, SH, SG]), ALU.add)
                v.drain()
                tt(hg(bc[:]), hg(bc[:]), it, ALU.mult)
                v.drain()

        w = {"stats": sb("st", [P, GT, 6]), "mv": sb("mv", [P, GT, 2]), "rstd": sb("rs", [P, GT])}
        xln, xT = sb("xln", [P, GT, XW]), sb("xT", [P, 2, GT * P])
        real = sb("real", [P, NI])
        sums = sb("sums", [P, SQ, XW])
        with ExitStack() as s2:
            sb2 = lambda n, shape, dt=FP32: s2.enter_context(nc.sbuf_tensor("f2_" + n, shape, dt))
            wt = sb2("wt", [P, GT, 512])
            wtT = sb2("wtT", [P, SQ, GT * P])
            mx, dn = sb2("mx", [P, GT, SH]), sb2("dn", [P, GT, SH])
            pb2 = lambda n: s2.enter_context(nc.psum_tensor("f2_" + n, [P, 512], FP32))
            psT = [pb2("psT0"), pb2("psT1")]
            psL = [pb2("psL0"), pb2("psL1")]
            psS = [pb2(f"psS{q}") for q in range(SQ)]
            ri, one, vin, root, xr, tr, tc, lg, lgd, ex, exd, wd, wr, wrc, acc, st, sd = (sem("2" + n) for n in (
                "ri", "one", "vin", "root", "xr", "tr", "tc", "lg", "lgd", "ex", "exd", "wd", "wr", "wrc", "acc", "st", "sd"))
            block = s2.enter_context(nc.Block())
            flat = lambda a: a.rearrange("p i n -> p (i n)")

            @block.sync
            def _(sp):
                with sp.Fori(0, NG) as g:
                    sp.wait_ge(wrc, (g + 1) * GT)
                    sp.dma_start(c.wT[:, bass.ds(g * (SQ * GT * P), SQ * GT * P)], wtT[:]).then_inc(st, 16)
                sp.wait_ge(st, 16 * NG)

            @block.gpsimd
            def _(pool):
                nc.gpsimd.iota(real[:], [[1, NI]], base=0, channel_multiplier=NI,
                               allow_small_or_imprecise_dtypes=True).then_inc(ri, 1)

            @block.vector
            def _(v):
                tt, ts = nc.vector.tensor_tensor, nc.vector.tensor_scalar
                nc.vector.memset(xln[:, :, ones:XW], 1.0).then_inc(one, 1)
                v.wait_ge(ri, 1)
                ts(real[:], real[:], N - 0.5, None, ALU.is_lt)
                v.drain()
                hg = lambda a: a.rearrange("p i (h g) -> p (i h) g", g=SG)
                ih = lambda a: a.rearrange("p i h -> p (i h)").unsqueeze(2).to_broadcast([P, GT * SH, SG])
                with v.Fori(0, NG) as g:
                    normalize_group(c, v, w, xln, g, vin, root, xr)
                    for j in range(GT):
                        v.wait_ge(lg, g * GT + j + 1)
                        tt(wt[:, j, :], psL[j % 2][:, :], bc[:], ALU.add).then_inc(lgd, 1)
                    v.drain()
                    nc.vector.tensor_reduce(mx[:], wt[:].rearrange("p i (h g) -> p i h g", g=SG), AX.X, ALU.max)
                    v.drain()
                    tt(hg(wt[:]), hg(wt[:]), ih(mx[:]), ALU.subtract).then_inc(ex, 1)
                    v.wait_ge(exd, g + 1)
                    nc.vector.tensor_reduce(dn[:], wt[:].rearrange("p i (h g) -> p i h g", g=SG), AX.X, ALU.add)
                    v.drain()
                    nc.vector.reciprocal(dn[:], dn[:])
                    v.drain()
                    tt(dn[:], dn[:], real[:, bass.ds(g * GT, GT)].unsqueeze(2).to_broadcast([P, GT, SH]), ALU.mult)
                    v.drain()
                    tt(hg(wt[:]), hg(wt[:]), ih(dn[:]), ALU.mult).then_inc(wd, 1)
                    v.drain()
                    v.wait_ge(acc, g + 1)
                v.wait_ge(sd, 1)
                for q in range(SQ):
                    nc.vector.tensor_copy(sums[:, q, :], psS[q][:, 0:XW])
                v.drain()

            @block.scalar
            def _(act):
                with act.Fori(0, NG) as g:
                    root_and_copies(c, act, w, g, vin, root, tr, tc, psT, xT)
                    act.wait_ge(ex, g + 1)
                    nc.scalar.activation(flat(wt[:]), flat(wt[:]), ACT.Exp).then_inc(exd, 1)
                    for j in range(GT):
                        act.wait_ge(wr, g * GT + j + 1)
                        nc.scalar.activation(wtT[:, :, j * P:(j + 1) * P],
                                             psT[j % 2][:, :].rearrange("p (q n) -> p q n", q=SQ), ACT.Copy).then_inc(wrc, 1)
                    act.wait_ge(st, (g + 1) * 16)

            @block.tensor
            def _(pe):
                mm = nc.tensor.matmul
                for q in range(SQ):
                    mm(psS[q][:, 0:XW], c.zrow[:, 0:P], c.zrow[:, 0:XW], start=True, stop=False)
                pe.wait_ge(one, 1)
                with pe.Fori(0, NG) as g:
                    transposes(c, pe, xln, g, xr, tr, tc, psT)
                    for j in range(GT):
                        pe.wait_ge(tc, g * GT + j + 1)
                        if j >= 2:
                            pe.wait_ge(lgd, g * GT + j - 1)
                        for k in range(2):
                            last = mm(psL[j % 2][:, :], xT[:, k, j * P:(j + 1) * P], wc[:, k, :], start=(k == 0), stop=(k == 1))
                        last.then_inc(lg, 1)
                    pe.wait_ge(wd, g + 1)
                    for j in range(GT):
                        if j >= 2:
                            pe.wait_ge(wrc, g * GT + j - 1)
                        for q in range(SQ):
                            last = nc.tensor.transpose(psT[j % 2][:, q * P:(q + 1) * P], wt[:, j, q * P:(q + 1) * P], c.ident[:])
                        last.then_inc(wr, 1)
                        for q in range(SQ):
                            last = mm(psS[q][:, 0:XW], wt[:, j, q * P:(q + 1) * P], xln[:, j, :], start=False, stop=False)
                    last.then_inc(acc, 1)
                    pe.wait_ge(wrc, (g + 1) * GT)
                for q in range(SQ):
                    last = mm(psS[q][:, 0:XW], c.zrow[:, 0:P], c.zrow[:, 0:XW], start=False, stop=True)
                last.then_inc(sd, 1)

        ow = sb("ow", [P, SQ, D])
        with ExitStack() as s3:
            sb3 = lambda n, shape, dt=FP32: s3.enter_context(nc.sbuf_tensor("f3_" + n, shape, dt))
            pb3 = lambda n: s3.enter_context(nc.psum_tensor("f3_" + n, [P, 512], FP32))
            sh = sb3("sh", [SG, SH, XW])
            shT = sb3("shT", [P, 2, SH, SG])
            rn, nm = sb3("rn", [SG, SH]), sb3("nm", [SG, SH])
            tok, bt = sb3("tok", [SG, SH, SC]), sb3("bt", [SG, SH, SC])
            tokT, qT, kT = sb3("tokT", [SC, SH, SG]), sb3("qT", [SC, SH, SG]), sb3("kT", [SC, SH, SG])
            vv = sb3("vv", [SG, SH, SC])
            at, atT = sb3("at", [SG, SH, SG]), sb3("atT", [SG, SH, SG])
            mx, dn = sb3("mx", [SG, SH]), sb3("dn", [SG, SH])
            oT = sb3("oT", [SC, SH, SG])
            owh = sb3("owh", [SG, SH, D])
            ps = [pb3(f"ps{n}") for n in range(8)]
            mv, step, back, fin = (sem("3" + n) for n in ("mv", "step", "back", "fin"))
            block = s3.enter_context(nc.Block())
            f3 = lambda a: a.rearrange("p h g -> p (h g)")

            @block.sync
            def _(sp):
                for half in range(2):
                    sp.dma_start(sh[:].rearrange("g (q b) w -> g q b w", b=2)[:, :, half, :],
                                 sums[half * SG:(half + 1) * SG, :, :]).then_inc(mv, 16)
                sp.wait_ge(mv, 32)
                sp.wait_ge(back, 9)
                for half in range(2):
                    sp.dma_start(ow[half * SG:(half + 1) * SG, :, :],
                                 owh[:].rearrange("g (q b) w -> g q b w", b=2)[:, :, half, :]).then_inc(fin, 16)
                sp.wait_ge(fin, 32)

            @block.tensor
            def _(pe):
                mm, turn = nc.tensor.matmul, nc.tensor.transpose
                pe.wait_ge(mv, 32)
                for k in range(2):
                    for h in range(SH):
                        last = turn(ps[k][:, h * SG:(h + 1) * SG], sh[:, h, k * P:(k + 1) * P], c.ident[0:SG, 0:SG])
                last.then_inc(step, 1)
                pe.wait_ge(back, 1)
                for h in range(SH):
                    for k in range(2):
                        last = mm(ps[2][0:SG, h * SC:(h + 1) * SC], shT[:, k, h, :], wfx[:, k, h * SC:(h + 1) * SC],
                                  start=(k == 0), stop=(k == 1))
                last.then_inc(step, 1)
                pe.wait_ge(back, 2)
                for h in range(SH):
                    last = turn(ps[3][0:SC, h * SG:(h + 1) * SG], tok[:, h, :], c.ident[0:SG, 0:SG])
                last.then_inc(step, 1)
                pe.wait_ge(back, 3)
                mm(ps[4][0:SC, :], wqkv[:, 0, :], f3(tokT[:]), start=True, stop=True)
                mm(ps[5][0:SC, :], wqkv[:, 1, :], f3(tokT[:]), start=True, stop=True)
                for h in range(SH):
                    last = mm(ps[6][0:SG, h * SC:(h + 1) * SC], tokT[:, h, :], wqkv[:, 2, :], start=True, stop=True)
                last.then_inc(step, 1)
                pe.wait_ge(back, 4)
                for h in range(SH):
                    last = mm(ps[7][0:SG, h * SG:(h + 1) * SG], qT[:, h, :], kT[:, h, :], start=True, stop=True)
                last.then_inc(step, 1)
                pe.wait_ge(back, 6)
                for h in range(SH):
                    last = turn(ps[0][0:SG, h * SG:(h + 1) * SG], at[:, h, :], c.ident[0:SG, 0:SG])
                last.then_inc(step, 1)
                pe.wait_ge(back, 7)
                for h in range(SH):
                    last = mm(ps[1][0:SC, h * SG:(h + 1) * SG], vv[:, h, :], atT[:, h, :], start=True, stop=True)
                last.then_inc(step, 1)
                pe.wait_ge(back, 8)
                for h in range(SH):
                    last = mm(ps[2 + h // 2][0:SG, (h % 2) * D:(h % 2 + 1) * D], oT[:, h, :], wout[:, h, :], start=True, stop=True)
                last.then_inc(step, 1)

            @block.scalar
            def _(act):
                act.wait_ge(back, 5)
                nc.scalar.activation(f3(at[:]), f3(at[:]), ACT.Exp).then_inc(mv, 1)

            @block.vector
            def _(v):
                tt, ts, copy = nc.vector.tensor_tensor, nc.vector.tensor_scalar, nc.vector.tensor_copy
                hsc = lambda a: a.unsqueeze(2).to_broadcast([SG, SH, SC])
                h3 = lambda a: a.rearrange("p (h g) -> p h g", h=SH)
                v.wait_ge(step, 1)
                copy(shT[:, 0, :, :], h3(ps[0][:, :]))
                copy(shT[:, 1, :, :], h3(ps[1][:, :])).then_inc(back, 1)
                copy(nm[:], sh[:, :, ones])
                ts(rn[:], sh[:, :, ones], 1e-5, None, ALU.add)
                v.drain()
                nc.vector.reciprocal(rn[:], rn[:])
                tt(bt[:], h3(bfx[:]), hsc(nm[:]), ALU.mult)
                v.wait_ge(step, 2)
                v.drain()
                tt(tok[:], h3(ps[2][0:SG, :]), bt[:], ALU.add)
                v.drain()
                tt(tok[:], tok[:], hsc(rn[:]), ALU.mult).then_inc(back, 1)
                v.wait_ge(step, 3)
                copy(f3(tokT[:]), ps[3][0:SC, :]).then_inc(back, 1)
                v.wait_ge(step, 4)
                ts(f3(qT[:]), ps[4][0:SC, :], float(SC) ** -0.5, None, ALU.mult)
                copy(f3(kT[:]), ps[5][0:SC, :])
                copy(f3(vv[:]), ps[6][0:SG, :]).then_inc(back, 1)
                v.wait_ge(step, 5)
                nc.vector.tensor_reduce(mx[:], h3(ps[7][0:SG, :]), AX.X, ALU.max)
                v.drain()
                tt(at[:], h3(ps[7][0:SG, :]), hsc(mx[:]), ALU.subtract).then_inc(back, 1)
                v.wait_ge(mv, 33)
                nc.vector.tensor_reduce(dn[:], at[:], AX.X, ALU.add)
                v.drain()
                nc.vector.reciprocal(dn[:], dn[:])
                v.drain()
                tt(at[:], at[:], hsc(dn[:]), ALU.mult).then_inc(back, 1)
                v.wait_ge(step, 6)
                copy(f3(atT[:]), ps[0][0:SG, :]).then_inc(back, 1)
                v.wait_ge(step, 7)
                copy(f3(oT[:]), ps[1][0:SC, :]).then_inc(back, 1)
                v.wait_ge(step, 8)
                for q in range(SQ):
                    last = copy(owh[:, 2 * q:2 * q + 2, :].rearrange("p h d -> p (h d)"), ps[2 + q][0:SG, :])
                last.then_inc(back, 1)
                v.drain()

        with ExitStack() as s4:
            wtT = s4.enter_context(nc.sbuf_tensor("f4_wtT", [P, 2, SQ, GT * P], FP32))
            psO = [s4.enter_context(nc.psum_tensor(f"f4_psO{n}", [P, 512], FP32)) for n in range(GT)]
            lw0, lw1, mmd, od, so = (sem("4" + n) for n in ("lw0", "lw1", "mm", "od", "so"))
            lw = [lw0, lw1]
            block = s4.enter_context(nc.Block())

            @block.sync
            def _(sp):
                for g in range(NG):
                    if g >= 2:
                        sp.wait_ge(mmd, g - 1)
                    sp.dma_start(wtT[:, g % 2, :, :], c.wT[:, g * SQ * GT * P:(g + 1) * SQ * GT * P]).then_inc(lw[g % 2], 16)
                sp.wait_ge(od, NG)
                full = (P - 1) * NI
                for p0, p1 in slices_of(0, P - 1):
                    sp.dma_start(c.out[p0 * NI:p1 * NI, :].rearrange("(p i) d -> p (i d)", i=NI), c.x[p0:p1, :]).then_inc(so, 16)
                sp.dma_start(c.out[full:N, :].rearrange("(p i) d -> p (i d)", p=1), c.x[P - 1:P, 0:(N - full) * D]).then_inc(so, 16)
                sp.wait_ge(so, 48)

            @block.tensor
            def _(pe):
                for g in range(NG):
                    pe.wait_ge(lw[g % 2], 16 * (g // 2 + 1))
                    if g:
                        pe.wait_ge(od, g)
                    for j in range(GT):
                        for q in range(SQ):
                            last = nc.tensor.matmul(psO[j][:, 0:D], wtT[:, g % 2, q, j * P:(j + 1) * P], ow[:, q, :],
                                                    start=(q == 0), stop=(q == SQ - 1))
                    last.then_inc(mmd, 1)

            @block.vector
            def _(v):
                tt = nc.vector.tensor_tensor
                tt(c.x[:].rearrange("p (i d) -> p i d", d=D), c.x[:].rearrange("p (i d) -> p i d", d=D),
                   bout[:].unsqueeze(1).to_broadcast([P, NI, D]), ALU.add)
                v.drain()
                for g in range(NG):
                    v.wait_ge(mmd, g + 1)
                    for j in range(GT):
                        xj = c.x[:, (g * GT + j) * D:(g * GT + j + 1) * D]
                        last = tt(xj, psO[j][:, 0:D], xj, ALU.add)
                    last.then_inc(od, 1)


def build(nc, A, out):
    c = Chip()
    c.nc, c.A, c.out = nc, A, out
    dram = lambda n, shape, dt=FP32: nc.dram_tensor(n, shape, dt).ap()
    c.t1, c.t2 = dram("t1", (NI * P, TW)), dram("t2", (NI * P, TW))
    c.rec_d, c.rec_s = dram("rec_d", (EP, 4), I32), dram("rec_s", (EP, 4), I32)
    c.ends = [[dram(f"{w}_{k}", (KEYS,), I32) for w in ("start", "end")] for k in ("d", "s")]
    c.st_f, c.st_b = dram("st_f", (EP + KEYS, 4)), dram("st_b", (EP + KEYS, 4))
    c.state = [dram("state0", (EP + 1, SW)), dram("state1", (EP + 1, SW))]
    c.ea_sorted = dram("ea_sorted", (EP, D))
    c.ea_tail = dram("ea_tail", (16 * T, D))
    c.wT = dram("wT", (P, SQ * NI * P))
    c.kv, c.q = dram("kv", (NI * P, 512)), dram("q", (NI * P, D))
    with ExitStack() as s:
        sb = lambda n, shape, dt=FP32: s.enter_context(nc.sbuf_tensor(n, shape, dt))
        c.x = sb("x", [P, NI * D])
        c.ident, c.tri, c.triT, c.cols = (sb(n, [P, P]) for n in ("ident", "tri", "triT", "cols"))
        c.identb, c.colsb = sb("identb", [P, P], BF16), sb("colsb", [P, P], BF16)
        c.zrow, c.one = sb("zrow", [P, 2 * D]), sb("one", [P, 1])
        c.tail = sb("tail", [P, SW])
        c.carry, c.fkey = sb("carry", [P, 2 * 137]), sb("fkey", [P, 2])
        c.flag = sb("flag", [P, 1], I32)
        c.placed = s.enter_context(nc.semaphore("placed"))
        constants(c)
        layer0_tables(c)
        sort_edges(c)
        edges = s.enter_context(ExitStack())
        se = lambda n, shape, dt=FP32: edges.enter_context(nc.sbuf_tensor(n, shape, dt))
        c.rec, c.sep, c.ar = se("rec", [P, 2, T, 4], I32), se("sep", [P, 2, T]), se("ar", [P, T, 8])
        targets_logits(c)
        edge_pass(c, 0)
        join_tails(c, 0)
        edges.close()
        combine(c, 0)
        experts(c)
        layer1_tables(c)
        edges = s.enter_context(ExitStack())
        se = lambda n, shape, dt=FP32: edges.enter_context(nc.sbuf_tensor(n, shape, dt))
        c.rec, c.sep = se("rec1", [P, 1, T, 4], I32), se("sep1", [P, 1, T])
        reload_edges(c)
        order_attributes(c)
        edge_pass(c, 1)
        join_tails(c, 1)
        edges.close()
        combine(c, 1)
        slice_attention(c)


_INS = [
    'x', 'src', 'dst', 'edge_attr_256', 'L0_gnn_W_f',
    'L0_gnn_a_src_f', 'L0_gnn_a_dst_f', 'L0_gnn_b_f', 'L0_gnn_W_b', 'L0_gnn_a_src_b',
    'L0_gnn_a_dst_b', 'L0_gnn_b_b', 'L0_gnn_W_fuse', 'L0_gnn_b_fuse', 'L0_gnn_gamma',
    'L0_gnn_beta', 'L0_gnn_run_mean', 'L0_gnn_run_var', 'L0_ffn_Wg', 'L0_ffn_bg',
    'L0_ffn_W1', 'L0_ffn_b1', 'L0_ffn_W2', 'L0_ffn_b2', 'L1_gnn_Wq',
    'L1_gnn_bq', 'L1_gnn_Wk', 'L1_gnn_bk', 'L1_gnn_Wv', 'L1_gnn_bv',
    'L1_gnn_We', 'L1_gnn_Ws', 'L1_gnn_bs', 'L1_ffn_W_fx', 'L1_ffn_b_fx',
    'L1_ffn_W_x', 'L1_ffn_b_x', 'L1_ffn_W_slice', 'L1_ffn_b_slice', 'L1_ffn_W_q',
    'L1_ffn_W_k', 'L1_ffn_W_v', 'L1_ffn_W_out', 'L1_ffn_b_out', 'L1_ffn_temperature']


def kernel(**inputs):
    import numpy as _np
    import concourse.bacc as _bacc
    from concourse import mybir as _mybir
    from concourse.bass_utils import run_bass_kernel_spmd as _run

    nc = _bacc.Bacc("TRN2", target_bir_lowering=False, num_devices=1)
    arrays, args = {}, {}
    for name in _INS:
        a = _np.ascontiguousarray(inputs[name])
        arrays[f"in_{name}"] = a
        args[name] = nc.dram_tensor(f"in_{name}", a.shape, _mybir.dt.from_np(a.dtype), kind="ExternalInput").ap()
    out = nc.dram_tensor("out_x", (6250, 256), _mybir.dt.float32, kind="ExternalOutput").ap()
    build(nc, args, out)
    r = _run(nc, [arrays], core_ids=[0])
    return r.results[0]["out_x"]
```

```python
import concourse.bass as bass
from concourse import mybir
from contextlib import ExitStack

FP32 = mybir.dt.float32
BF16 = mybir.dt.bfloat16
I32 = mybir.dt.int32
ALU = mybir.AluOpType
ACT = mybir.ActivationFunctionType
AX = mybir.AxisListType

P = 128
N, D = 6250, 256
E = 100000
NI = -(-N // P)
NG, GT = 7, 7
assert NG * GT == NI
B = 8
T = 784
EP = P * T
NBLK = T // B
LO = 64
KEYS = P * LO
H, C = 8, 32
DEN, MX = H * C, H * C + H
SW = H * C + 2 * H
TW = 136
BIG = 1.0e30
LN_EPS = BN_EPS = 1e-5
EXP = 8
HID = 512


class Chip:

    def semaphores(self, phase, prefix):
        made = []

        def semaphore(name):
            made.append(self.nc.alloc_semaphore(prefix + name))
            return made[-1]

        def clear():
            self.nc.clear_and_free_semaphores(made)
            self.nc.all_engine_barrier()

        phase.callback(clear)
        return semaphore

    def flag_on(self, eng):
        return eng.value_load(self.flag[0:1, 0:1], min_val=0, max_val=EP)

    def alone(self, eng):
        eng.sem_inc(self.placed, 1)


def row_bcast(v, lo, n):
    return v[lo:lo + n].rearrange("(a n) -> a n", a=1).to_broadcast([P, n])


def layernorm_stats(c, v, w, x_of, n, sqrt_in, sqrt_out, turn):
    for j in range(n):
        c.nc.vector.bn_stats(w["stats"][:, j, :], x_of(j))
    v.drain()
    for j in range(n):
        c.nc.vector.bn_aggr(w["mv"][:, j, :], w["stats"][:, j, :])
    v.drain()
    c.nc.vector.tensor_scalar(w["rstd"][:, 0:n], w["mv"][:, 0:n, 1], LN_EPS, None, ALU.add).then_inc(sqrt_in, 1)
    v.wait_ge(sqrt_out, turn)
    c.nc.vector.reciprocal(w["rstd"][:, 0:n], w["rstd"][:, 0:n])
    v.drain()


def over_groups(eng, prepare, step):
    prepare(0, 0)
    with eng.Fori(0, NG // 2) as i:
        for par in range(2):
            step(i * 2 + par, par, True)
    step(NG - 1, 0, False)


def turns(g, par, k):
    return (g // 2 + 1) * k if isinstance(g, int) else (g - par) * (k // 2) + k


def constants(c):
    nc = c.nc
    with ExitStack() as s:
        made = s.enter_context(nc.semaphore("const_made"))
        got = s.enter_context(nc.semaphore("x_loaded"))
        zero = s.enter_context(nc.semaphore("pad_zeroed"))
        block = s.enter_context(nc.Block())

        @block.gpsimd
        def _(pool):
            nc.gpsimd.memset(c.ident[:], 0.0)
            nc.gpsimd.memset(c.tri[:], 1.0)
            nc.gpsimd.memset(c.triT[:], 1.0)
            pool.drain()
            nc.gpsimd.affine_select(out=c.ident[:], in_=c.ident[:], compare_op=ALU.not_equal, fill=1.0,
                                    base=0, pattern=[[-1, P]], channel_multiplier=1)
            nc.gpsimd.affine_select(out=c.tri[:], in_=c.tri[:], compare_op=ALU.is_gt, fill=0.0,
                                    base=0, pattern=[[-1, P]], channel_multiplier=1)
            nc.gpsimd.affine_select(out=c.triT[:], in_=c.triT[:], compare_op=ALU.is_gt, fill=0.0,
                                    base=0, pattern=[[1, P]], channel_multiplier=-1)
            nc.gpsimd.iota(c.cols[:], [[1, P]], base=0, channel_multiplier=0,
                           allow_small_or_imprecise_dtypes=True)
            pool.drain()
            nc.gpsimd.memset(c.one[:], 1.0)
            nc.gpsimd.memset(c.zrow[:], 0.0).then_inc(made, 1)

        @block.vector
        def _(v):
            nc.vector.memset(c.x[96:128, :], 0.0).then_inc(zero, 1)
            v.wait_ge(made, 1)
            nc.vector.tensor_copy(c.identb[:], c.ident[:])
            nc.vector.tensor_copy(c.colsb[:], c.cols[:])
            v.drain()

        @block.sync
        def _(sp):
            x = c.A["x"]
            full = (P - 1) * NI
            sp.wait_ge(zero, 1)
            for p0, p1 in slices_of(0, P - 1):
                sp.dma_start(c.x[p0:p1, :], x[p0 * NI:p1 * NI, :].rearrange("(p i) d -> p (i d)", i=NI)).then_inc(got, 16)
            sp.dma_start(c.x[P - 1:P, 0:(N - full) * D],
                         x[full:N, :].rearrange("(p i) d -> p (i d)", p=1)).then_inc(got, 16)
            sp.wait_ge(got, 48)


def layer0_tables(c):
    nc, A = c.nc, c.A
    with ExitStack() as s:
        sb = lambda n, shape, dt=FP32: s.enter_context(nc.sbuf_tensor(n, shape, dt))
        sem = lambda n: s.enter_context(nc.semaphore(n))
        pb = lambda n: s.enter_context(nc.psum_tensor(n, [P, 512], FP32))
        W = sb("t_W", [P, 2, 2 * TW])
        av = sb("t_av", [P, 4, 4])
        WT = sb("t_WT", [P, 2, 2, P])
        w = {"stats": sb("t_st", [P, GT, 6]), "mv": sb("t_mv", [P, GT, 2]), "rstd": sb("t_rs", [P, GT])}
        xln = sb("t_xln", [P, GT, D])
        xT = sb("t_xT", [P, 2, 2, GT * P])
        row = sb("t_row", [P, 2, 2, GT, TW])
        psT = [pb("t_psT0"), pb("t_psT1")]
        psO = [pb("t_psO0"), pb("t_psO1")]
        loaded, zeroed, wt, wtc, wa, ready = (sem("t_" + n) for n in ("ld", "z", "wt", "wtc", "wa", "rdy"))
        vin, root, xr, tr, tc, mm, oc = (sem("t_" + n) for n in ("vin", "root", "xr", "tr", "tc", "mm", "oc"))
        st = [sem("t_st0"), sem("t_st1")]
        block = s.enter_context(nc.Block())
        names = [("L0_gnn_a_src_f", 0), ("L0_gnn_a_dst_f", 1), ("L0_gnn_a_src_b", 2), ("L0_gnn_a_dst_b", 3)]

        @block.sync
        def _(sp):
            for d, name in enumerate(("L0_gnn_W_f", "L0_gnn_W_b")):
                sp.dma_start(W[:, :, d * TW:d * TW + P], A[name].rearrange("(k p) c -> p k c", p=P)).then_inc(loaded, 16)
            sp.wait_ge(zeroed, 1)
            for name, at in names:
                for h in range(4):
                    sp.dma_start(av[h * 32:(h + 1) * 32, at, h:h + 1],
                                 A[name][h:h + 1, :].rearrange("a c -> c a")).then_inc(loaded, 16)
            sp.wait_ge(loaded, 16 * 18)
            sp.sem_inc(st[0], 32)
            sp.sem_inc(st[1], 32)

            def step(g, par, ahead):
                sp.wait_ge(oc, (g + 1) * GT + 2)
                for d, tab in enumerate((c.t1, c.t2)):
                    sp.dma_start(tab.rearrange("(p i) w -> p (i w)", i=NI)[:, bass.ds(g * (GT * TW), GT * TW)],
                                 row[:, par, d, :, :]).then_inc(st[par], 16)

            over_groups(sp, lambda g, par: None, step)
            sp.wait_ge(st[0], 32 * (NG // 2 + 2))
            sp.wait_ge(st[1], 32 * (NG // 2 + 1))

        @block.vector
        def _(v):
            nc.vector.memset(av[:], 0.0).then_inc(zeroed, 1)

            def step(g, par, ahead):
                v.wait_ge(tr, (g + 1) * GT)
                if ahead:
                    normalize_group(c, v, w, xln, g + 1, vin, root, xr)

            over_groups(v, lambda g, par: normalize_group(c, v, w, xln, g, vin, root, xr), step)

        @block.scalar
        def _(act):
            for d in range(2):
                act.wait_ge(wt, d + 1)
                nc.scalar.activation(WT[:, d, :, :], psT[d][:, 0:2 * P], ACT.Copy).then_inc(wtc, 1)
            act.wait_ge(wa, 1)
            for k in range(2):
                for d in range(2):
                    for q in range(2):
                        o = (k * 4 + d * 2 + q) * 4
                        last = nc.scalar.activation(W[:, k, d * TW + P + 4 * q:d * TW + P + 4 * q + 4],
                                                    psO[0][:, o:o + 4], ACT.Copy)
            last.then_inc(ready, 1)

            def prepare(g, par):
                root_and_copies(c, act, w, g, vin, root, tr, tc, psT, xT[:, par])

            def step(g, par, ahead):
                act.wait_ge(st[par], turns(g, par, 32))
                if ahead:
                    act.wait_ge(vin, g + 2)
                    nc.scalar.activation(w["rstd"][:], w["rstd"][:], ACT.Sqrt).then_inc(root, 1)
                for j in range(GT):
                    act.wait_ge(mm, g * GT + j + 1)
                    nc.scalar.activation(row[:, par, :, j, :], psO[j % 2][:, 0:2 * TW].rearrange("p (d w) -> p d w", d=2),
                                         ACT.Copy).then_inc(oc, 1)
                    if ahead:
                        act.wait_ge(tr, (g + 1) * GT + j + 1)
                        nc.scalar.activation(xT[:, 1 - par, :, j * P:(j + 1) * P],
                                             psT[j % 2][:, 0:2 * P].rearrange("p (k n) -> p k n", k=2), ACT.Copy).then_inc(tc, 1)

            over_groups(act, prepare, step)

        @block.tensor
        def _(pe):
            pe.wait_ge(loaded, 16 * 18)
            for d in range(2):
                for k in range(2):
                    last = nc.tensor.transpose(psT[d][:, k * P:(k + 1) * P], W[:, k, d * TW:d * TW + P], c.ident[:])
                last.then_inc(wt, 1)
            pe.wait_ge(wtc, 2)
            for k in range(2):
                for d in range(2):
                    for q in range(2):
                        o = (k * 4 + d * 2 + q) * 4
                        last = nc.tensor.matmul(psO[0][:, o:o + 4], WT[:, d, k, :], av[:, 2 * d + q, :],
                                                start=True, stop=True)
            last.then_inc(wa, 1)
            pe.wait_ge(ready, 1)
            pe.sem_inc(oc, 2)

            def turn(g, j):
                pe.wait_ge(xr, g * GT + j + 1)
                if j >= 2:
                    pe.wait_ge(tc, g * GT + j - 1)
                for k in range(2):
                    last = nc.tensor.transpose(psT[j % 2][:, k * P:(k + 1) * P], xln[:, j, k * P:(k + 1) * P], c.ident[:])
                last.then_inc(tr, 1)

            def prepare(g, par):
                for j in range(GT):
                    turn(g, j)

            def step(g, par, ahead):
                pe.wait_ge(tc, (g + 1) * GT)
                for j in range(GT):
                    pe.wait_ge(oc, g * GT + j + (1 if j else 2))
                    for k in range(2):
                        last = nc.tensor.matmul(psO[j % 2][:, 0:2 * TW], xT[:, par, k, j * P:(j + 1) * P], W[:, k, :],
                                                start=(k == 0), stop=(k == 1))
                    last.then_inc(mm, 1)
                    if ahead:
                        turn(g + 1, j)

            over_groups(pe, prepare, step)


def slices_of(p0, p1):
    return [(p0, 112), (112, p1)]


def sort_edges(c):
    nc, A = c.nc, c.A
    U = 2
    with ExitStack() as s:
        sb = lambda n, shape, dt=FP32: s.enter_context(nc.sbuf_tensor(n, shape, dt))
        key = sb("s_key", [P, 2, T], I32)
        dig = sb("s_dig", [P, 2, 2, T + B], BF16)
        rec = sb("s_rec", [P, T, 4], I32)
        oh = sb("s_oh", [P, U, 2, P, B], BF16)
        ol = sb("s_ol", [P, U, 2, LO, B], BF16)
        places = sb("s_places", [P, P, B], BF16)
        base = sb("s_base", [P, 2, LO])
        full = (P - 1) * T

        def one_hots(t0, u, k):
            digit = lambda q, n: dig[:, k, q, bass.ds(t0, B)].unsqueeze(1).to_broadcast([P, n, B])
            nc.vector.tensor_tensor(oh[:, u, k, :, :], places[:], digit(0, P), ALU.is_equal)
            return nc.vector.tensor_tensor(ol[:, u, k, :, :], places[:, 0:LO, :], digit(1, LO), ALU.is_equal)

        with ExitStack() as s1:
            sb1 = lambda n, shape, dt=FP32: s1.enter_context(nc.sbuf_tensor(n, shape, dt))
            sem = c.semaphores(s1, "h_")
            pb = lambda n: s1.enter_context(nc.psum_tensor(n, [P, 512], FP32))
            nxt = sb1("h_nxt", [P, 1], I32)
            down = sb1("h_down", [P, T])
            viol = sb1("h_viol", [P, 2])
            hist, tmp = sb1("h_hist", [P, 2, LO]), sb1("h_tmp", [P, LO])
            junk, tot, offs = sb1("h_junk", [P, P]), sb1("h_tot", [P, 2]), sb1("h_offs", [P, 2])
            nid = sb1("h_nid", [P, LO])
            zeros = sb1("h_zeros", [P, T * 4])
            digits = sb1("h_digits", [P, 2, 2, T], I32)
            ends = sb1("h_ends", [P, 2, 2, LO], I32)
            psH = [pb("h_psH0"), pb("h_psH1")]
            psR, psV = pb("h_psR"), pb("h_psV")
            kz, kld, made, used, hd, hc, off, bd, rz, wr, ids, rd, rw, vs = (sem(n) for n in (
                "kz", "kld", "made", "used", "hd", "hc", "off", "bd", "rz", "wr", "ids", "rd", "rw", "vs"))
            block = s1.enter_context(nc.Block())

            @block.sync
            def _(sp):
                sp.wait_ge(kz, 1)
                for k, name in enumerate(("dst", "src")):
                    a = A[name]
                    for p0, p1 in slices_of(0, P - 1):
                        sp.dma_start(key[p0:p1, k, :], a[p0 * T:p1 * T].rearrange("(p t) -> p t", t=T)).then_inc(kld, 16)
                    sp.dma_start(key[P - 1:P, k, 0:E - full], a[full:E].rearrange("(p t) -> p t", p=1)).then_inc(kld, 16)
                with nc.allow_non_contiguous_dma("one word per partition"):
                    sp.dma_start(nxt[0:P - 1, :], A["dst"][T:(P - 1) * T + 1:T].rearrange("(p a) -> p a", a=1)).then_inc(kld, 16)
                ea = A["edge_attr_256"]
                sp.dma_start(c.ea_tail[0:E - 112 * T, :].rearrange("(a n) w -> a (n w)", a=16),
                             ea[112 * T:E, :].rearrange("(a n) w -> a (n w)", a=16)).then_inc(rz, 16)
                sp.dma_start(c.ea_tail[E - 112 * T:16 * T, :].rearrange("(a n) w -> a (n w)", a=16),
                             ea[0:EP - E, :].rearrange("(a n) w -> a (n w)", a=16)).then_inc(rz, 16)
                for a in (c.st_f, c.st_b):
                    sp.dma_start(a[0:EP, :].rearrange("(p t) w -> p (t w)", p=P), zeros[:]).then_inc(rz, 16)
                sp.wait_ge(rd, 1)
                sp.dma_start(c.rec_d.rearrange("(p t) w -> p t w", p=P), rec[:]).then_inc(rw, 16)
                sp.wait_ge(bd, 1)
                for k in range(2):
                    for q in range(2):
                        sp.dma_start(c.ends[k][q].rearrange("(p l) -> p l", l=LO), ends[:, k, q, :]).then_inc(wr, 16)
                sp.wait_ge(wr, 64)
                sp.wait_ge(rw, 16)
                sp.wait_ge(rz, 64)

            @block.vector
            def _(v):
                nc.vector.memset(key[:], N)
                nc.vector.memset(zeros[:], 0.0)
                nc.vector.memset(nxt[:], N).then_inc(kz, 1)
                nc.vector.memset(dig[:, :, :, T:T + B], 0)
                v.wait_ge(kld, 112)
                nc.vector.tensor_copy(places[:], c.colsb[:].unsqueeze(2).to_broadcast([P, P, B]))
                nc.vector.tensor_scalar(digits[:, 0], key[:], 6, None, ALU.logical_shift_right)
                nc.vector.tensor_scalar(digits[:, 1], key[:], LO - 1, None, ALU.bitwise_and)
                v.drain()
                for q in range(2):
                    nc.vector.tensor_copy(dig[:, :, q, 0:T], digits[:, q])
                v.drain()
                v.sem_inc(used, U)
                with v.Fori(0, NBLK // U) as i:
                    for u in range(U):
                        v.wait_ge(used, i * U + u + 1)
                        one_hots((i * U + u) * B, u, 0)
                        one_hots((i * U + u) * B, u, 1).then_inc(made, 1)
                nc.vector.tensor_tensor(down[:, 1:T], key[:, 0, 1:T], key[:, 0, 0:T - 1], ALU.is_lt)
                nc.vector.tensor_tensor(down[:, 0:1], nxt[:], key[:, 0, T - 1:T], ALU.is_lt)
                v.drain()
                nc.vector.tensor_reduce(viol[:, 0:1], down[:], AX.X, ALU.add)
                v.wait_ge(ids, 1)
                nc.vector.tensor_copy(rec[:, :, 0:2], key[:].rearrange("p k t -> p t k")).then_inc(rd, 1)
                v.drain()
                nc.vector.tensor_copy(viol[:, 1:2], viol[:, 0:1]).then_inc(vs, 1)
                v.wait_ge(hd, 1)
                for k in range(2):
                    nc.vector.tensor_copy(hist[:, k, :], psH[k][:, 0:LO])
                nc.vector.tensor_copy(c.flag[:], psV[:, 0:1])
                v.drain()
                for k in range(2):
                    nc.vector.tensor_reduce(tot[:, k:k + 1], hist[:, k, :], AX.X, ALU.add)
                v.drain()
                nc.vector.tensor_copy(junk[:, 0:2], tot[:]).then_inc(hc, 1)
                v.wait_ge(off, 1)
                nc.vector.tensor_copy(offs[:], psR[:, 0:2])
                nc.vector.memset(tmp[:], 0.0)
                v.drain()
                for k in range(2):
                    nc.vector.tensor_tensor_scan(base[:, k, :], hist[:, k, :], tmp[:], offs[:, k:k + 1], ALU.add, ALU.add)
                v.drain()
                for k in range(2):
                    nc.vector.tensor_scalar(tmp[:], hist[:, k, :], 0.5, None, ALU.is_ge)
                    nc.vector.tensor_scalar(junk[:, 0:LO], base[:, k, :], -1.0 - EP, None, ALU.add)
                    v.drain()
                    nc.vector.tensor_tensor(base[:, k, :], base[:, k, :], hist[:, k, :], ALU.subtract)
                    nc.vector.tensor_tensor(junk[:, 0:LO], junk[:, 0:LO], tmp[:], ALU.mult)
                    v.drain()
                    nc.vector.tensor_tensor(junk[:, LO:2 * LO], base[:, k, :], nid[:], ALU.subtract)
                    nc.vector.tensor_scalar(ends[:, k, 1, :], junk[:, 0:LO], float(EP), None, ALU.add)
                    v.drain()
                    nc.vector.tensor_tensor(junk[:, LO:2 * LO], junk[:, LO:2 * LO], tmp[:], ALU.mult)
                    v.drain()
                    nc.vector.tensor_tensor(ends[:, k, 0, :], junk[:, LO:2 * LO], nid[:], ALU.add)
                    v.drain()
                nc.vector.tensor_copy(tmp[:], base[:, 0, :]).then_inc(bd, 1)

            @block.tensor
            def _(pe):
                for k in range(2):
                    nc.tensor.matmul(psH[k][:, 0:LO], c.zrow[:, 0:P], c.zrow[:, 0:LO], start=True, stop=False)
                with pe.Fori(0, NBLK // U) as i:
                    for u in range(U):
                        pe.wait_ge(made, i * U + u + 1)
                        for k in range(2):
                            for j in range(B):
                                last = nc.tensor.matmul(psH[k][:, 0:LO], oh[:, u, k, :, j], ol[:, u, k, :, j],
                                                        start=False, stop=False)
                        last.then_inc(used, 1)
                pe.wait_ge(vs, 1)
                nc.tensor.matmul(psV[:, 0:1], c.one[:, 0:1].to_broadcast([P, P]), viol[:, 1:2], start=True, stop=True)
                for k in range(2):
                    last = nc.tensor.matmul(psH[k][:, 0:LO], c.zrow[:, 0:P], c.zrow[:, 0:LO], start=False, stop=True)
                last.then_inc(hd, 1)
                pe.wait_ge(hc, 1)
                nc.tensor.matmul(psR[:, 0:2], c.triT[:], tot[:], start=True, stop=True).then_inc(off, 1)

            @block.gpsimd
            def _(pool):
                nc.gpsimd.iota(rec[:, :, 2], [[1, T]], base=0, channel_multiplier=T)
                nc.gpsimd.iota(nid[:], [[1, LO]], base=EP, channel_multiplier=LO, allow_small_or_imprecise_dtypes=True)
                nc.gpsimd.memset(rec[:, :, 3], 0)
                pool.drain()
                nc.gpsimd.tensor_scalar(rec[:, :, 2], rec[:, :, 2], E - 1, None, ALU.min).then_inc(ids, 1)

        def rank_pass(k, rec_out, only_if_unsorted):
            with ExitStack() as s2:
                sb2 = lambda n, shape, dt=FP32: s2.enter_context(nc.sbuf_tensor(f"s{k}_{n}", shape, dt))
                sem = c.semaphores(s2, f"s{k}_")
                pb = lambda n, shape=(P, 512), dt=FP32: s2.enter_context(nc.psum_tensor(f"s{k}_{n}", list(shape), dt))
                keyf = sb2("kf", [P, U, B])
                parts = sb2("kp", [P, U, 2, B], BF16)
                oht = sb2("oht", [P, U, B, P])
                tab = sb2("tab", [P, B // 2, LO])
                junk = sb2("junk", [P, B + B // 2, P], BF16)
                hit = sb2("hit", [P, B, LO])
                rank = sb2("rank", [P, 3, B])
                pos = sb2("pos", [P, U, B], I32)
                row = sb2("row", [P, U, B, 4], I32)
                psT = [pb(f"psT{u}", (P, 1024), BF16) for u in range(U)]
                psK = [pb(f"psK{q}") for q in range(2)]
                psR = [pb(f"psR{u}") for u in range(U)]
                psH = pb("psH")
                made, tp, tpc, kr, eqd, tbc, lk, lkd, hu, pd, sct0, sct1, rows_free = (sem(n) for n in (
                    "made", "tp", "tpc", "kr", "eqd", "tbc", "lk", "lkd", "hu", "pd", "sct0", "sct1", "rows_free"))
                sct = [sct0, sct1]
                block = s2.enter_context(nc.Block())

                def when(eng):
                    if not only_if_unsorted:
                        return ExitStack()
                    return eng.If(c.flag_on(eng) > 0)

                @block.sync
                def _(sp):
                    with when(sp):
                        sp.sem_inc(rows_free, U)
                        with sp.Fori(0, NBLK // U) as i:
                            for u in range(U):
                                sp.wait_ge(sct[u], (i + 1) * (16 * B))
                                sp.sem_inc(rows_free, 1)

                @block.vector
                def _(v):
                    with when(v):
                        nc.vector.memset(rank[:], 0.0)
                        nc.vector.tensor_copy(keyf[:, 0, :], key[:, k, 0:B])
                        nc.vector.tensor_scalar(parts[:, 0, 0, :], dig[:, k, 0, 0:B], float(LO), None, ALU.mult)
                        nc.vector.tensor_copy(parts[:, 0, 1, :], dig[:, k, 1, 0:B])
                        one_hots(0, 0, k).then_inc(made, 1)
                        with v.Fori(0, NBLK // U) as i:
                            for u in range(U):
                                blk = i * U + u
                                v.wait_ge(hu, (blk + U) * (B // 2))
                                nc.vector.tensor_copy(keyf[:, 1 - u, :], dig[:, k, 0, bass.ds((blk + 1) * B, B)])
                                nc.vector.tensor_copy(parts[:, 1 - u, 1, :], dig[:, k, 1, bass.ds((blk + 1) * B, B)])
                                v.drain()
                                nc.vector.tensor_scalar(parts[:, 1 - u, 0, :], keyf[:, 1 - u, :], float(LO), None, ALU.mult)
                                v.drain()
                                nc.vector.scalar_tensor_tensor(out=keyf[:, 1 - u, :], in0=keyf[:, 1 - u, :], scalar=float(LO),
                                                               in1=dig[:, k, 1, bass.ds((blk + 1) * B, B)],
                                                               op0=ALU.mult, op1=ALU.add)
                                one_hots((blk + 1) * B, 1 - u, k).then_inc(made, 1)
                                for j in range(B):
                                    if j % 4 == 0:
                                        v.wait_ge(kr, blk * 2 + j // 4 + 1)
                                    last = nc.vector.scalar_tensor_tensor(
                                        out=junk[:, j, :], in0=psK[j // 4][:, (j % 4) * P:(j % 4 + 1) * P],
                                        scalar=keyf[:, u, j:j + 1], in1=c.tri[:], op0=ALU.is_equal, op1=ALU.mult,
                                        accum_out=rank[:, 0, j:j + 1])
                                    if j % 2:
                                        last = nc.vector.scalar_tensor_tensor(
                                            out=junk[:, B + j // 2, :], in0=psK[j // 4][:, (j % 4 - 1) * P:(j % 4) * P],
                                            scalar=keyf[:, u, j:j + 1], in1=c.one[:].to_broadcast([P, P]), op0=ALU.is_equal,
                                            op1=ALU.mult, accum_out=rank[:, 2, j:j + 1])
                                    if j % 4 == 3:
                                        last.then_inc(eqd, 1)
                                v.wait_ge(lk, blk + 1)
                                nc.vector.tensor_tensor(hit[:], psR[u][:, :].rearrange("p (j l) -> p j l", l=LO),
                                                        ol[:, u, k, :, :].rearrange("p l j -> p j l"), ALU.mult).then_inc(lkd, 1)
                                v.drain()
                                nc.vector.tensor_reduce(rank[:, 1, :], hit[:], AX.X, ALU.add)
                                nc.vector.tensor_tensor(rank[:, 0, :], rank[:, 0, :], rank[:, 2, :], ALU.add)
                                v.drain()
                                v.wait_ge(rows_free, blk + 1)
                                nc.vector.tensor_tensor(pos[:, u, :], rank[:, 0, :], rank[:, 1, :], ALU.add)
                                nc.vector.tensor_copy(row[:, u, :, :], rec[:, bass.ds(blk * B, B), :]).then_inc(pd, 1)

                @block.scalar
                def _(act):
                    with when(act):
                        with act.Fori(0, NBLK // U) as i:
                            for u in range(U):
                                blk = i * U + u
                                act.wait_ge(tp, blk + 1)
                                nc.scalar.activation(oht[:, u, :, :].rearrange("p j n -> p (j n)"), psT[u][:, :],
                                                     ACT.Copy).then_inc(tpc, 1)
                                for j in range(B // 2):
                                    act.wait_ge(hu, (blk + U) * (B // 2) + j)
                                    nc.scalar.activation(tab[:, j, :], psH[:, 0:LO], ACT.Copy).then_inc(tbc, 1)

                @block.tensor
                def _(pe):
                    with when(pe):
                        nc.tensor.matmul(psH[:, 0:LO], c.ident[:], base[:, k, :], start=True, stop=True).then_inc(hu, U * (B // 2))
                        pe.sem_inc(eqd, 2)
                        pe.sem_inc(lkd, U)
                        with pe.Fori(0, NBLK // U) as i:
                            for u in range(U):
                                blk = i * U + u
                                pe.wait_ge(made, blk + 1)
                                for j in range(B):
                                    last = nc.tensor.transpose(psT[u][:, j * P:(j + 1) * P], oh[:, u, k, :, j], c.identb[:])
                                last.then_inc(tp, 1)
                                for q in range(2):
                                    pe.wait_ge(eqd, blk * 2 + q + 1)
                                    for j in range(4 * q, 4 * q + 4):
                                        for n in range(2):
                                            last = nc.tensor.matmul(psK[q][:, (j % 4) * P:(j % 4 + 1) * P],
                                                                    parts[:, u, n, j:j + 1].to_broadcast([P, P]),
                                                                    c.identb[:], start=(n == 0), stop=(n == 1))
                                    last.then_inc(kr, 1)
                                pe.wait_ge(lkd, blk + 1)
                                for m in range(B // 2):
                                    pe.wait_ge(tbc, blk * (B // 2) + m + 1)
                                    for j in (2 * m, 2 * m + 1):
                                        last = nc.tensor.matmul(psH[:, 0:LO], oh[:, u, k, :, j], ol[:, u, k, :, j],
                                                                start=False, stop=True, skip_group_check=True)
                                    last.then_inc(hu, 1)
                                    for j in (2 * m, 2 * m + 1):
                                        last = nc.tensor.matmul(psR[u][:, j * LO:(j + 1) * LO], oht[:, u, j, :], tab[:, m, :],
                                                                start=True, stop=True)
                                last.then_inc(lk, 1)

                @block.gpsimd
                def _(pool):
                    with when(pool):
                        with pool.Fori(0, NBLK // U) as i:
                            for u in range(U):
                                pool.wait_ge(pd, i * U + u + 1)
                                c.alone(pool)
                                for j in range(B):
                                    pool.indirect_dma_start(rec_out, bass.IndirectOffsetOnAxis(ap=pos[:, u, j:j + 1], axis=0),
                                                            row[:, u, j, :], None).then_inc(sct[u], 16)
                        for u in range(U):
                            pool.wait_ge(sct[u], 16 * B * (NBLK // U))

        rank_pass(1, c.rec_s, False)
        rank_pass(0, c.rec_d, True)


def targets_logits(c):
    nc = c.nc
    with ExitStack() as s:
        sb = lambda n, shape, dt=FP32: s.enter_context(nc.sbuf_tensor(n, shape, dt))
        sem = c.semaphores(s, "a_")
        startn = sb("a_start", [P, 2, NI], I32)
        logit = sb("a_logit", [P, 2, NI, 4])
        idx = sb("a_idx", [P, 2, 2, GT], I32)
        rows = sb("a_rows", [P, 2, 2, GT, 4])
        val = sb("a_val", [P, 2, T, 4])
        first = sb("a_first", [P, 2, TW])
        ld, rl, sc0, sc1, fg, vl, staged, free = (sem(n) for n in ("ld", "rl", "sc0", "sc1", "fg", "vl", "staged", "free"))
        sc = [sc0, sc1]
        landed = 2 * GT * 16
        block = s.enter_context(nc.Block())

        @block.sync
        def _(sp):
            for d, tab in enumerate((c.t1, c.t2)):
                sp.dma_start(startn[:, d, :], c.ends[d][0][0:NI * P].rearrange("(p i) -> p i", i=NI)).then_inc(ld, 16)
                sp.dma_start(logit[:, d, :, :], tab.rearrange("(p i) w -> p i w", i=NI)[:, :, 132:136]).then_inc(ld, 16)
            for d, rec in enumerate((c.rec_d, c.rec_s)):
                sp.dma_start(c.rec[:, d, :, :], rec.rearrange("(p t) w -> p t w", p=P)).then_inc(rl, 16)
            sp.sem_inc(free, 2)

            def step(g, par, ahead):
                sp.wait_ge(sc[par], turns(g, par, landed))
                sp.sem_inc(free, 1)

            over_groups(sp, lambda g, par: None, step)
            for d, st in enumerate((c.st_f, c.st_b)):
                sp.dma_start(val[:, d, :, :], st[0:EP, :].rearrange("(p t) w -> p t w", p=P)).then_inc(vl, 16)
            sp.wait_ge(vl, 32)

        @block.gpsimd
        def _(pool):
            pool.wait_ge(ld, 64)
            def step(g, par, ahead):
                pool.wait_ge(free, g + 1)
                c.alone(pool)
                nc.gpsimd.tensor_copy(idx[:, par], startn[:, :, bass.ds(g * GT, GT)])
                nc.gpsimd.tensor_copy(rows[:, par], logit[:, :, bass.ds(g * GT, GT), :]).then_inc(staged, 1)
                pool.wait_ge(staged, g + 1)
                c.alone(pool)
                for j in range(GT):
                    for d, st in enumerate((c.st_f, c.st_b)):
                        pool.indirect_dma_start(st, bass.IndirectOffsetOnAxis(ap=idx[:, par, d, j:j + 1], axis=0),
                                                rows[:, par, d, j, :], None).then_inc(sc[par], 16)

            over_groups(pool, lambda g, par: None, step)
            pool.wait_ge(rl, 32)
            for d, (tab, col) in enumerate(((c.t1, 0), (c.t2, 1))):
                pool.indirect_dma_start(first[:, d, :], None, tab,
                                        bass.IndirectOffsetOnAxis(ap=c.rec[:, d, 0, col:col + 1], axis=0)).then_inc(fg, 16)
            pool.wait_ge(fg, 32)

        @block.vector
        def _(v):
            v.wait_ge(rl, 32)
            for d in range(2):
                k = c.rec[:, d, :, d]
                nc.vector.memset(c.sep[:, d, 0:1], 0.0)
                nc.vector.tensor_tensor(c.sep[:, d, 1:T], k[:, 1:T], k[:, 0:T - 1], ALU.is_equal)
            v.wait_ge(fg, 32)
            v.wait_ge(vl, 32)
            nc.vector.tensor_copy(val[:, :, 0, :], first[:, :, 132:136])
            v.drain()
            for d in range(2):
                for h in range(4):
                    nc.vector.tensor_tensor_scan(c.ar[:, :, 4 * d + h], c.sep[:, d, :], val[:, d, :, h], 0.0,
                                                 ALU.mult, ALU.add)
            v.drain()
            nc.vector.tensor_scalar(c.sep[:], c.sep[:], 1.0, BIG, ALU.subtract, ALU.mult)
            v.drain()


def order_attributes(c):
    nc, A = c.nc, c.A
    U = 2
    with ExitStack() as s:
        sb = lambda n, shape, dt=FP32: s.enter_context(nc.sbuf_tensor("o_" + n, shape, dt))
        sem = c.semaphores(s, "o_")
        idx, rows = sb("idx", [P, U, B, 4], I32), sb("rows", [P, U, B, D])
        staged, so0, so1, g0, g1, free = (sem(n) for n in ("staged", "so0", "so1", "g0", "g1", "free"))
        so, got = [so0, so1], [g0, g1]
        block = s.enter_context(nc.Block())

        @block.gpsimd
        def _(pool):
            with pool.If(c.flag_on(pool) > 0):
                with pool.Fori(0, NBLK // U) as i:
                    for u in range(U):
                        pool.wait_ge(free, i * U + u + 1)
                        c.alone(pool)
                        nc.gpsimd.tensor_copy(idx[:, u], c.rec[:, 0, bass.ds((i * U + u) * B, B), :]).then_inc(staged, 1)
                        pool.wait_ge(staged, i * U + u + 1)
                        c.alone(pool)
                        for j in range(B):
                            pool.indirect_dma_start(rows[:, u, j, :], None, A["edge_attr_256"],
                                                    bass.IndirectOffsetOnAxis(ap=idx[:, u, j, 2:3], axis=0)).then_inc(got[u], 16)

        @block.sync
        def _(sp):
            with sp.If(c.flag_on(sp) > 0):
                sp.sem_inc(free, U)
                with sp.Fori(0, NBLK // U) as i:
                    for u in range(U):
                        sp.wait_ge(got[u], (i + 1) * (16 * B))
                        sp.dma_start(c.ea_sorted.rearrange("(p t) w -> p (t w)", p=P)[:, bass.ds((i * U + u) * (B * D), B * D)],
                                     rows[:, u, :, :]).then_inc(so[u], 16)
                        sp.wait_ge(so[u], (i + 1) * 16)
                        sp.sem_inc(free, 1)


def edge_pass(c, layer):
    nc, A = c.nc, c.A
    U = 2
    B1 = B + 1
    state = c.state[layer]
    with ExitStack() as s:
        sb = lambda n, shape, dt=FP32: s.enter_context(nc.sbuf_tensor(f"e{layer}_{n}", shape, dt))
        sem = c.semaphores(s, f"e{layer}_")
        pb = lambda n: s.enter_context(nc.psum_tensor(f"e{layer}_{n}", [P, 512], FP32))
        idx = sb("idx", [P, U, 2, B, 4], I32)
        if layer == 0:
            g1, g2 = sb("g1", [P, U, B, TW]), sb("g2", [P, U, B, TW])
        else:
            kv, q, ea = sb("kv", [P, U, B, 512]), sb("q", [P, U, B, D]), sb("ea", [P, U, B, D])
            eaT = sb("eaT", [P, 4, 2, 2, P])
            we = sb("we", [P, 2, D])
            psT = [pb(f"psT{n}") for n in range(4)]
            psE = [pb(f"psE{n}") for n in range(4)]
        sepb = sb("sepb", [P, H, B1])
        at = sb("at", [P, H, B1])
        mt = sb("mt", [P, H, B1])
        ex = sb("ex", [P, 2, H, B])
        cw = sb("cw", [P, 2, H, B1])
        den = sb("den", [P, H, B1])
        fx = sb("fx", [P, D, B1])
        wv = sb("wv", [P, D, B1])
        st = sb("st", [P, U, B, SW])
        ld, gat0, gat1, eg0, eg1, used, exd, cwd, dnd, std, act_st, so0, so1, free, dump, tp, tcp, ep, ed = (
            sem(n) for n in ("ld", "gat0", "gat1", "eg0", "eg1", "used", "exd", "cwd", "dnd", "std", "acts", "so0",
                             "so1", "free", "dump", "tp", "tcp", "ep", "ed"))
        gat, eg, so = [gat0, gat1], [eg0, eg1], [so0, so1]
        q_used = sem("q_used")
        staged, fxd, act_mt = sem("staged"), sem("fxd"), sem("act_mt")
        block = s.enter_context(nc.Block())
        ngat = 2 * B * 16

        @block.sync
        def _(sp):
            if layer == 1:
                sp.dma_start(we[:], A["L1_gnn_We"].rearrange("(k p) n -> p k n", p=P)).then_inc(ld, 16)
            sp.wait_ge(dump, 1)
            sp.dma_start(state[EP:EP + 1, :], st[0:1, 1, B - 1, :]).then_inc(so[1], 16)
            sp.wait_ge(so[1], 16)
            sp.sem_inc(free, 1)
            unsorted = c.flag_on(sp) if layer == 1 else None

            def load_attributes(b, u):
                at_ = bass.ds(b * (B * D), B * D)
                rows = lambda a: a.rearrange("(p t) w -> p (t w)", t=T)[:, at_]
                with sp.If(unsorted > 0):
                    sp.dma_start(ea[0:112, u, :, :], rows(c.ea_sorted[0:112 * T, :])).then_inc(eg[u], 16)
                    sp.dma_start(ea[112:P, u, :, :], rows(c.ea_sorted[112 * T:EP, :])).then_inc(eg[u], 16)
                with sp.Else():
                    sp.dma_start(ea[0:112, u, :, :], rows(A["edge_attr_256"][0:112 * T, :])).then_inc(eg[u], 16)
                    sp.dma_start(ea[112:P, u, :, :], rows(c.ea_tail)).then_inc(eg[u], 16)

            def store(i, u):
                blk = i * U + u
                sp.wait_ge(act_st, blk + 2)
                sp.dma_start(state[0:EP, :].rearrange("(p t) w -> p (t w)", p=P)[:, bass.ds(blk * (B * SW), B * SW)],
                             st[:, u, :, :]).then_inc(so[u], 16)
                sp.wait_ge(so[1 - u], (i + 1) * 16)
                sp.sem_inc(free, 1)

            if layer == 1:
                load_attributes(0, 0)
                load_attributes(1, 1)
            with sp.Fori(0, NBLK // U - 1) as i:
                for u in range(U):
                    if layer == 1:
                        sp.wait_ge(tp, (i * U + u + 1) * 4)
                        c.alone(sp)
                        load_attributes(i * U + u + U, u)
                    store(i, u)
            store(NBLK // U - 1, 0)
            store(NBLK // U - 1, 1)
            sp.wait_ge(so[1], (NBLK // U + 1) * 16)

        @block.gpsimd
        def _(pool):
            pool.sem_inc(used, U)
            pool.sem_inc(q_used, U)
            with pool.Fori(0, NBLK // U) as i:
                for u in range(U):
                    blk = i * U + u
                    first_free = used if layer == 0 else q_used
                    pool.wait_ge(first_free, blk + 1)
                    c.alone(pool)
                    nd = 2 if layer == 0 else 1
                    for d in range(nd):
                        last = nc.gpsimd.tensor_copy(idx[:, u, d, :, :], c.rec[:, d, bass.ds(blk * B, B), :])
                    last.then_inc(staged, 1)
                    pool.wait_ge(staged, blk + 1)
                    c.alone(pool)
                    at_ = lambda d, j, w: bass.IndirectOffsetOnAxis(ap=idx[:, u, d, j, w:w + 1], axis=0)
                    for j in range(B):
                        if layer == 0:
                            pool.indirect_dma_start(g1[:, u, j, :], None, c.t1, at_(0, j, 1)).then_inc(gat[u], 16)
                            pool.indirect_dma_start(g2[:, u, j, :], None, c.t2, at_(1, j, 0)).then_inc(gat[u], 16)
                        else:
                            pool.indirect_dma_start(q[:, u, j, :], None, c.q, at_(0, j, 0)).then_inc(gat[u], 16)
                    if layer == 1:
                        pool.wait_ge(used, blk + 1)
                        c.alone(pool)
                        for j in range(B):
                            pool.indirect_dma_start(kv[:, u, j, :], None, c.kv, at_(0, j, 1)).then_inc(gat[u], 16)

        @block.vector
        def _(v):
            tt, copy = nc.vector.tensor_tensor, nc.vector.tensor_copy
            nc.vector.memset(st[:, :, :, 0:MX], 0.0)
            nc.vector.memset(st[:, :, :, MX:SW], -BIG)
            nc.vector.memset(sepb[:], -BIG)
            nc.vector.memset(at[:], -BIG)
            nc.vector.memset(cw[:], 0.0)
            nc.vector.memset(wv[:], 0.0)
            v.drain()
            nc.vector.memset(den[:], 0.0).then_inc(dump, 1)
            if layer == 1:
                v.sem_inc(ed, 4)
            with v.Fori(0, NBLK // U) as i:
                for u in range(U):
                    blk = i * U + u
                    for d in range(2):
                        k = d if layer == 0 else 0
                        copy(sepb[:, 4 * d:4 * d + 4, 1:B1],
                             c.sep[:, k, bass.ds(blk * B, B)].unsqueeze(1).to_broadcast([P, 4, B]))
                    if layer == 0:
                        v.wait_ge(gat[u], (i + 1) * ngat)
                        for d, g in enumerate((g1, g2)):
                            tt(at[:, 4 * d:4 * d + 4, 1:B1].rearrange("p h b -> p b h"), g[:, u, :, P:P + 4],
                               c.ar[:, bass.ds(blk * B, B), 4 * d:4 * d + 4], ALU.add)
                        v.drain()
                        nc.vector.scalar_tensor_tensor(out=at[:, :, 1:B1], in0=at[:, :, 1:B1], scalar=0.2,
                                                       in1=at[:, :, 1:B1], op0=ALU.mult, op1=ALU.max)
                    else:
                        v.wait_ge(gat[u], (i + 1) * ngat)
                        for m in range(4):
                            pair = psE[m][:, :].rearrange("p (j n) -> p j n", j=2)
                            v.wait_ge(ep, blk * 4 + m + 1)
                            tt(kv[:, u, 2 * m:2 * m + 2, 0:D], kv[:, u, 2 * m:2 * m + 2, 0:D], pair, ALU.add)
                            tt(kv[:, u, 2 * m:2 * m + 2, D:2 * D], kv[:, u, 2 * m:2 * m + 2, D:2 * D], pair,
                               ALU.add).then_inc(ed, 1)
                        v.drain()
                        tt(q[:, u, :, :], kv[:, u, :, 0:D], q[:, u, :, :], ALU.mult)
                        v.drain()
                        nc.vector.tensor_reduce(at[:, :, 1:B1].rearrange("p h b -> p b h"),
                                                q[:, u, :, :].rearrange("p b (h k) -> p b h k", k=C), AX.X,
                                                ALU.add).then_inc(q_used, 1)
                    v.drain()
                    flat = lambda a: a.rearrange("p h b -> p (h b)")
                    nc.vector.tensor_tensor_scan(flat(mt[:]), flat(sepb[:]), flat(at[:]), 0.0, ALU.add, ALU.max)
                    v.drain()
                    tt(ex[:, 0, :, :], mt[:, :, 0:B], sepb[:, :, 1:B1], ALU.add)
                    tt(ex[:, 1, :, :], at[:, :, 1:B1], mt[:, :, 1:B1], ALU.subtract)
                    v.drain()
                    copy(at[:, :, 0], mt[:, :, B])
                    tt(ex[:, 0, :, :], ex[:, 0, :, :], mt[:, :, 1:B1], ALU.subtract).then_inc(exd, 1)
                    v.wait_ge(cwd, blk + 1)
                    nc.vector.tensor_tensor_scan(flat(den[:]), flat(cw[:, 0, :, :]), flat(cw[:, 1, :, :]), 0.0,
                                                 ALU.mult, ALU.add).then_inc(dnd, 1)
                    wt = lambda h0, n: cw[:, 1, h0:h0 + n, 1:B1].rearrange("p h b -> p b h").unsqueeze(3).to_broadcast([P, B, n, C])
                    msg = lambda a: a.rearrange("p b (h k) -> p b h k", k=C)
                    by_edge = wv[:, :, 1:B1].rearrange("p n b -> p b n")
                    v.wait_ge(act_st, blk + 1)
                    if layer == 0:
                        for d, g in enumerate((g1, g2)):
                            last = tt(msg(by_edge[:, :, P * d:P * d + P]), msg(g[:, u, :, 0:P]), wt(4 * d, 4), ALU.mult)
                    else:
                        last = tt(msg(by_edge), msg(kv[:, u, :, D:2 * D]), wt(0, H), ALU.mult)
                    last.then_inc(used, 1)
                    v.drain()
                    copy(cw[:, 1, :, 0], den[:, :, B])
                    v.wait_ge(fxd, blk + 1)
                    nc.vector.tensor_tensor_scan(wv[:].rearrange("p n b -> p (n b)"), fx[:].rearrange("p n b -> p (n b)"),
                                                 wv[:].rearrange("p n b -> p (n b)"), 0.0, ALU.mult, ALU.add).then_inc(std, 1)
                    v.wait_ge(act_mt, blk + 1)
            c.alone(v)
            v.drain()
            v.wait_ge(act_st, NBLK + 1)
            copy(c.tail[:], st[:, 1, B - 1, :])

        @block.scalar
        def _(act):
            act.sem_inc(act_st, 1)

            def transposed_attributes(blk):
                if layer == 1:
                    for m in range(4):
                        act.wait_ge(tp, blk * 4 + m + 1)
                        nc.scalar.activation(eaT[:, m, :, :, :].rearrange("p a b c -> p (a b c)"), psT[m][:, :],
                                             ACT.Copy).then_inc(tcp, 1)

            def one_block(blk, u, ahead):
                if ahead:
                    transposed_attributes(blk + 1)
                act.wait_ge(exd, blk + 1)
                nc.scalar.activation(cw[:, :, :, 1:B1].rearrange("p x h b -> p (x h) b"),
                                     ex[:].rearrange("p x h b -> p (x h) b"), ACT.Exp).then_inc(cwd, 1)
                act.wait_ge(cwd, blk + 1)
                nc.scalar.activation(fx[:].rearrange("p (h k) b -> p h k b", k=C),
                                     cw[:, 0, :, :].unsqueeze(2).to_broadcast([P, H, C, B1]), ACT.Copy).then_inc(fxd, 1)
                act.wait_ge(dnd, blk + 1)
                act.wait_ge(free, blk + 1)
                nc.scalar.activation(st[:, u, :, MX:SW].rearrange("p b h -> p h b"), mt[:, :, 1:B1], ACT.Copy)
                nc.scalar.activation(st[:, u, :, DEN:MX].rearrange("p b h -> p h b"), den[:, :, 1:B1],
                                     ACT.Copy).then_inc(act_mt, 1)
                act.wait_ge(std, blk + 1)
                nc.scalar.activation(wv[:, :, 0], wv[:, :, B], ACT.Copy)
                nc.scalar.activation(st[:, u, :, 0:D], wv[:, :, 1:B1].rearrange("p n b -> p b n"),
                                     ACT.Copy).then_inc(act_st, 1)

            transposed_attributes(0)
            with act.Fori(0, NBLK // U - 1) as i:
                for u in range(U):
                    one_block(i * U + u, u, True)
            one_block(NBLK - 2, 0, True)
            one_block(NBLK - 1, 1, False)

        if layer == 1:
            @block.tensor
            def _(pe):
                pe.wait_ge(ld, 16)
                with pe.Fori(0, NBLK // U) as i:
                    for u in range(U):
                        blk = i * U + u
                        pe.wait_ge(eg[u], (i + 1) * 32)

                        def turn(m):
                            for j in range(2):
                                for k in range(2):
                                    o = (2 * j + k) * P
                                    last = nc.tensor.transpose(psT[m][:, o:o + P], ea[:, u, 2 * m + j, k * P:(k + 1) * P],
                                                               c.ident[:])
                            last.then_inc(tp, 1)

                        def product(m):
                            pe.wait_ge(tcp, blk * 4 + m + 1)
                            pe.wait_ge(ed, blk * 4 + m + 1)
                            for j in range(2):
                                for k in range(2):
                                    last = nc.tensor.matmul(psE[m][:, j * D:(j + 1) * D], eaT[:, m, j, k, :], we[:, k, :],
                                                            start=(k == 0), stop=(k == 1))
                            last.then_inc(ep, 1)

                        for m in range(4):
                            turn(m)
                        for m in range(4):
                            product(m)


def join_tails(c, layer):
    nc = c.nc
    nd = 2 if layer == 0 else 1
    hd = H // nd
    wd = hd * C
    with ExitStack() as s:
        sb = lambda n, shape, dt=FP32: s.enter_context(nc.sbuf_tensor(f"j{layer}_{n}", shape, dt))
        sem = c.semaphores(s, f"j{layer}_")
        pb = lambda n: s.enter_context(nc.psum_tensor(f"j{layer}_{n}", [P, 512], FP32))
        nxt = sb("nxt", [P, nd], I32)
        last, opened, key, first, before = (sb(n, [P, nd]) for n in ("last", "open", "key", "first", "before"))
        same, pen = sb("same", [P, nd, P]), sb("pen", [P, nd, P])
        junk = sb("junk", [P, nd, P])
        mrow = sb("mrow", [P, H, P])
        top, fac = sb("top", [P, H]), sb("fac", [P, H])
        scaled = sb("scaled", [P, nd, wd + hd])
        psK = [pb("psK0"), pb("psK1")]
        psM = [pb("psM0"), pb("psM1")]
        psG = [pb("psG0"), pb("psG1")]
        nz, nl, kd, kr, mr, xd, fd, sd, gd = (sem(n) for n in ("nz", "nl", "kd", "kr", "mr", "xd", "fd", "sd", "gd"))
        block = s.enter_context(nc.Block())

        @block.sync
        def _(sp):
            sp.wait_ge(nz, 1)
            for d, rec in enumerate((c.rec_d, c.rec_s)[0:nd]):
                with nc.allow_non_contiguous_dma("one word of each partition's first record"):
                    sp.dma_start(nxt[0:P - 1, d:d + 1],
                                 rec.rearrange("(p t) w -> p t w", t=T)[1:P, 0, d:d + 1]).then_inc(nl, 16)
            sp.wait_ge(nl, 16 * nd)

        @block.vector
        def _(v):
            tt, ts, copy = nc.vector.tensor_tensor, nc.vector.tensor_scalar, nc.vector.tensor_copy
            nc.vector.memset(nxt[:], -1).then_inc(nz, 1)
            for d in range(nd):
                copy(last[:, d:d + 1], c.rec[:, d, T - 1, d:d + 1])
            v.wait_ge(nl, 16 * nd)
            v.drain()
            tt(opened[:], last[:], nxt[:], ALU.is_equal)
            ts(last[:], last[:], 1.0, None, ALU.add)
            v.drain()
            tt(key[:], last[:], opened[:], ALU.mult)
            v.drain()
            ts(key[:], key[:], 1.0, None, ALU.subtract)
            v.drain()
            copy(junk[:, 0, 0:nd], key[:]).then_inc(kd, 1)
            v.wait_ge(kr, 1)
            for d in range(nd):
                ts(same[:, d, :], psK[d][:, 0:P], key[:, d:d + 1], None, ALU.is_equal)
            v.drain()
            for d in range(nd):
                nc.vector.scalar_tensor_tensor(out=junk[:, d, :], in0=same[:, d, :], scalar=1.0, in1=c.tri[:],
                                               op0=ALU.mult, op1=ALU.mult, accum_out=before[:, d:d + 1])
            ts(pen[:], same[:], 1.0, BIG, ALU.subtract, ALU.mult)
            v.drain()
            ts(first[:], before[:], 0.5, None, ALU.is_lt)
            v.wait_ge(mr, 1)
            for h in range(H):
                tt(mrow[:, h, :], psM[h // 4][:, (h % 4) * P:(h % 4 + 1) * P], pen[:, h // hd, :], ALU.add)
            v.drain()
            tt(first[:], first[:], opened[:], ALU.mult)
            nc.vector.tensor_reduce(top[:], mrow[:], AX.X, ALU.max)
            v.drain()
            tt(first[:], first[:], last[:], ALU.mult)
            tt(fac[:], c.tail[:, MX:SW], top[:], ALU.subtract).then_inc(xd, 1)
            v.drain()
            ts(c.fkey[:, 0:nd], first[:], 1.0, None, ALU.subtract)
            v.wait_ge(fd, 1)
            for d in range(nd):
                tt(scaled[:, d, 0:wd].rearrange("p (h k) -> p h k", k=C),
                   c.tail[:, d * wd:(d + 1) * wd].rearrange("p (h k) -> p h k", k=C),
                   fac[:, d * hd:(d + 1) * hd].unsqueeze(2).to_broadcast([P, hd, C]), ALU.mult)
                op = tt(scaled[:, d, wd:wd + hd], c.tail[:, DEN + d * hd:DEN + (d + 1) * hd],
                        fac[:, d * hd:(d + 1) * hd], ALU.mult)
            op.then_inc(sd, 1)
            v.wait_ge(gd, 1)
            g = c.carry[:, 0:nd * (wd + 2 * hd + 1)].rearrange("p (d w) -> p d w", d=nd)
            for d in range(nd):
                copy(g[:, d, 0:wd + hd], psG[d][:, 0:wd + hd])
                copy(g[:, d, wd + hd:wd + 2 * hd], top[:, d * hd:(d + 1) * hd])
            nc.vector.memset(g[:, :, wd + 2 * hd:wd + 2 * hd + 1], 1.0)
            v.drain()

        @block.scalar
        def _(act):
            act.wait_ge(xd, 1)
            nc.scalar.activation(fac[:], fac[:], ACT.Exp).then_inc(fd, 1)

        @block.tensor
        def _(pe):
            for h in range(H):
                op = nc.tensor.matmul(psM[h // 4][:, (h % 4) * P:(h % 4 + 1) * P],
                                      c.tail[:, MX + h:MX + h + 1].to_broadcast([P, P]), c.ident[:], start=True, stop=True)
            op.then_inc(mr, 1)
            pe.wait_ge(kd, 1)
            for d in range(nd):
                op = nc.tensor.matmul(psK[d][:, 0:P], key[:, d:d + 1].to_broadcast([P, P]), c.ident[:], start=True, stop=True)
            op.then_inc(kr, 1)
            pe.wait_ge(sd, 1)
            for d in range(nd):
                op = nc.tensor.matmul(psG[d][:, 0:wd + hd], same[:, d, :], scaled[:, d, :], start=True, stop=True)
            op.then_inc(gd, 1)


def combine(c, layer):
    nc, A = c.nc, c.A
    nd = 2 if layer == 0 else 1
    hd = H // nd
    wd = hd * C
    wc = wd + 2 * hd + 1
    parts = 3 if layer == 0 else 2
    with ExitStack() as s:
        sb = lambda n, shape, dt=FP32: s.enter_context(nc.sbuf_tensor(f"c{layer}_{n}", shape, dt))
        sem = c.semaphores(s, f"c{layer}_")
        pb = lambda n: s.enter_context(nc.psum_tensor(f"c{layer}_{n}", [P, 512], FP32))
        endn = sb("endn", [P, nd, NI], I32)
        idx = sb("idx", [P, 2, nd, GT], I32)
        r2 = sb("r", [P, 2, nd, GT, SW])
        nrow = sb("nrow", [P, P])
        oh = sb("oh", [P, nd, GT, P])
        cc2 = sb("cc", [P, 2, nd, GT, wc])
        own2 = sb("own", [P, 2, 2, GT, TW]) if layer == 0 else None
        top = sb("top", [P, nd, GT, hd])
        mc = sb("mc", [P, nd, GT, hd])
        eself = sb("eself", [P, nd, GT, hd])
        xa = sb("xa", [P, nd, parts, GT, hd])
        dsum, dtmp = sb("dsum", [P, nd, GT, hd]), sb("dtmp", [P, nd, parts, GT, hd])
        pres = sb("pres", [P, nd, GT])
        num, tmp = sb("num", [P, GT, D]), sb("tmp", [P, GT, D])
        psC = [pb("psC0"), pb("psC1")]
        ld, gat, tl, ohd, cm, ccd, xd, fd, used, tr, tc, mm, fs = (sem(n) for n in (
            "ld", "gat", "tl", "ohd", "cm", "ccd", "xd", "fd", "used", "tr", "tc", "mm", "fs"))
        catd, staged, gat1, tl1 = (sem(n) for n in ("catd", "staged", "gat1", "tl1"))
        gat, tl = [gat, gat1], [tl, tl1]
        if layer == 0:
            cT = sb("cT", [P, 2, GT * P])
            wf = sb("wf", [P, 2, D])
            vec = sb("vec", [P, 6, D])
            psT, psF = [pb("psT0"), pb("psT1")], [pb("psF0"), pb("psF1")]
        nld = 16 * (nd + (8 if layer == 0 else 0))
        block = s.enter_context(nc.Block())

        @block.sync
        def _(sp):
            for d in range(nd):
                sp.dma_start(endn[:, d, :], c.ends[d][1][0:NI * P].rearrange("(p i) -> p i", i=NI)).then_inc(ld, 16)
            if layer == 0:
                sp.dma_start(wf[:], A["L0_gnn_W_fuse"].rearrange("(k p) n -> p k n", p=P)).then_inc(ld, 16)
                sp.dma_start(vec[:, 0, 0:P], row_bcast(A["L0_gnn_b_f"], 0, P)).then_inc(ld, 16)
                sp.dma_start(vec[:, 0, P:D], row_bcast(A["L0_gnn_b_b"], 0, P)).then_inc(ld, 16)
                for n, name in enumerate(("b_fuse", "run_mean", "run_var", "gamma", "beta")):
                    sp.dma_start(vec[:, 1 + n, :], row_bcast(A["L0_gnn_" + name], 0, D)).then_inc(ld, 16)

                def step(g, par, ahead):
                    sp.wait_ge(used, g + 1)
                    for d, tab in enumerate((c.t1, c.t2)):
                        sp.dma_start(own2[:, par, d, :, :],
                                     tab.rearrange("(p i) w -> p (i w)", i=NI)[:, bass.ds(g * (GT * TW), GT * TW)]).then_inc(tl[par], 16)

                over_groups(sp, lambda g, par: None, step)

        @block.gpsimd
        def _(pool):
            pool.wait_ge(ld, nld)

            def step(g, par, ahead):
                pool.wait_ge(used, g + 1)
                c.alone(pool)
                nc.gpsimd.tensor_copy(idx[:, par], endn[:, :, bass.ds(g * GT, GT)]).then_inc(staged, 1)
                pool.wait_ge(staged, g + 1)
                c.alone(pool)
                for d in range(nd):
                    for j in range(GT):
                        pool.indirect_dma_start(r2[:, par, d, j, :], None, c.state[layer],
                                                bass.IndirectOffsetOnAxis(ap=idx[:, par, d, j:j + 1], axis=0)).then_inc(gat[par], 16)

            over_groups(pool, lambda g, par: None, step)

        @block.vector
        def _(v):
            tt, ts = nc.vector.tensor_tensor, nc.vector.tensor_scalar
            v.sem_inc(used, 2)
            v.wait_ge(ld, nld)
            ts(nrow[:], c.cols[:], float(NI), None, ALU.mult)
            if layer == 0:
                ts(vec[:, 3, :], vec[:, 3, :], BN_EPS, None, ALU.add).then_inc(xd, 1)
                v.wait_ge(fd, 1)
                nc.vector.reciprocal(vec[:, 3, :], vec[:, 3, :])
                tt(vec[:, 1, :], vec[:, 1, :], vec[:, 2, :], ALU.subtract)
                v.drain()
                tt(vec[:, 4, :], vec[:, 4, :], vec[:, 3, :], ALU.mult)
                v.drain()
                tt(vec[:, 1, :], vec[:, 1, :], vec[:, 4, :], ALU.mult)
                v.drain()
                tt(vec[:, 5, :], vec[:, 5, :], vec[:, 1, :], ALU.add)
            x0 = 1 if layer == 0 else 0
            v.drain()

            def prepare(g, par):
                for d in range(nd):
                    for j in range(GT):
                        last = ts(oh[:, d, j, :], nrow[:], float(j), c.fkey[:, d:d + 1], ALU.add, ALU.is_equal)
                last.then_inc(ohd, 1)
                v.drain()
                ts(nrow[:], nrow[:], float(GT), None, ALU.add)
                v.drain()

            def step(g, par, ahead):
                r, cc, own = r2[:, par], cc2[:, par], own2[:, par] if layer == 0 else None
                v.wait_ge(ccd, (g + 1) * (nd * GT))
                if ahead:
                    prepare(g + 1, 1 - par)
                v.wait_ge(gat[par], turns(g, par, nd * GT * 16))
                if layer == 0:
                    v.wait_ge(tl[par], turns(g, par, 32))
                ts(pres[:], cc[:, :, :, wc - 1], 1.0, BIG, ALU.subtract, ALU.mult)
                if layer == 0:
                    tt(eself[:], own[:, :, :, 128:132], own[:, :, :, 132:136], ALU.add)
                v.drain()
                for d in range(nd):
                    tt(mc[:, d], cc[:, d, :, wd + hd:wd + 2 * hd], pres[:, d, :].unsqueeze(2).to_broadcast([P, GT, hd]), ALU.add)
                    if layer == 0:
                        nc.vector.scalar_tensor_tensor(out=eself[:, d], in0=eself[:, d], scalar=0.2, in1=eself[:, d],
                                                       op0=ALU.mult, op1=ALU.max)
                v.drain()
                for d in range(nd):
                    tt(top[:, d], mc[:, d], r[:, d, :, MX + d * hd:MX + (d + 1) * hd], ALU.max)
                v.drain()
                if layer == 0:
                    tt(top[:], top[:], eself[:], ALU.max)
                    v.drain()
                for d in range(nd):
                    tt(xa[:, d, 0], r[:, d, :, MX + d * hd:MX + (d + 1) * hd], top[:, d], ALU.subtract)
                    last = tt(xa[:, d, 1], mc[:, d], top[:, d], ALU.subtract)
                    if layer == 0:
                        last = tt(xa[:, d, 2], eself[:, d], top[:, d], ALU.subtract)
                last.then_inc(xd, 1)
                v.wait_ge(fd, g + 1 + x0)
                for d in range(nd):
                    tt(dtmp[:, d, 0], r[:, d, :, DEN + d * hd:DEN + (d + 1) * hd], xa[:, d, 0], ALU.mult)
                    tt(dtmp[:, d, 1], cc[:, d, :, wd:wd + hd], xa[:, d, 1], ALU.mult)
                v.drain()
                tt(dsum[:], dtmp[:, :, 0], dtmp[:, :, 1], ALU.add)
                v.drain()
                if layer == 0:
                    tt(dsum[:], dsum[:], xa[:, :, 2], ALU.add)
                    v.drain()
                    ts(dsum[:], dsum[:], 1e-16, None, ALU.add)
                else:
                    ts(dsum[:], dsum[:], 1e-30, None, ALU.max)
                v.drain()
                nc.vector.reciprocal(dsum[:], dsum[:])
                v.drain()
                for d in range(nd):
                    for n in range(parts):
                        tt(xa[:, d, n], xa[:, d, n], dsum[:, d], ALU.mult)
                v.drain()
                hk = lambda a: a.rearrange("p i (h k) -> p i h k", k=C)
                for n in range(parts):
                    for d in range(nd):
                        src = (r[:, d, :, d * wd:(d + 1) * wd], cc[:, d, :, 0:wd], own[:, d, :, 0:wd] if layer == 0 else None)[n]
                        dst = num if n == 0 else tmp
                        tt(hk(dst[:, :, d * wd:(d + 1) * wd]), hk(src),
                           xa[:, d, n].unsqueeze(3).to_broadcast([P, GT, hd, C]), ALU.mult)
                    v.drain()
                    if n:
                        tt(num[:], num[:], tmp[:], ALU.add)
                        v.drain()
                xg = c.x[:, bass.ds(g * (GT * D), GT * D)]
                flat = lambda a: a.rearrange("p i d -> p (i d)")
                if layer == 0:
                    tt(num[:], num[:], vec[:, 0, :].unsqueeze(1).to_broadcast([P, GT, D]), ALU.add).then_inc(catd, 1)
                    v.sem_inc(used, 1)
                    for j in range(GT):
                        v.wait_ge(mm, g * GT + j + 1)
                        tt(tmp[:, j, :], psF[j % 2][:, 0:D], vec[:, 4, :], ALU.mult).then_inc(fs, 1)
                    v.drain()
                    tt(tmp[:], tmp[:], vec[:, 5, :].unsqueeze(1).to_broadcast([P, GT, D]), ALU.add)
                    v.drain()
                    nc.vector.scalar_tensor_tensor(out=xg, in0=flat(tmp[:]), scalar=0.0, in1=xg, op0=ALU.max, op1=ALU.add)
                else:
                    tt(xg, xg, flat(num[:]), ALU.add).then_inc(used, 1)
                v.drain()

            over_groups(v, prepare, step)

        @block.scalar
        def _(act):
            if layer == 0:
                act.wait_ge(xd, 1)
                nc.scalar.activation(vec[:, 3, :], vec[:, 3, :], ACT.Sqrt).then_inc(fd, 1)
            x0 = 1 if layer == 0 else 0

            def prepare(g, par):
                for n in range(nd * GT):
                    act.wait_ge(cm, g * (nd * GT) + n + 1)
                    nc.scalar.activation(cc2[:, par, n // GT, n % GT, :], psC[n % 2][:, 0:wc], ACT.Copy).then_inc(ccd, 1)

            def step(g, par, ahead):
                act.wait_ge(xd, g + 1 + x0)
                nc.scalar.activation(xa[:].rearrange("p a b i h -> p (a b i h)"),
                                     xa[:].rearrange("p a b i h -> p (a b i h)"), ACT.Exp).then_inc(fd, 1)
                if ahead:
                    prepare(g + 1, 1 - par)
                if layer == 0:
                    for j in range(GT):
                        act.wait_ge(tr, g * GT + j + 1)
                        nc.scalar.activation(cT[:, :, j * P:(j + 1) * P],
                                             psT[j % 2][:, 0:2 * P].rearrange("p (k n) -> p k n", k=2), ACT.Copy).then_inc(tc, 1)

            over_groups(act, prepare, step)

        @block.tensor
        def _(pe):
            pe.wait_ge(ld, nld)

            def prepare(g, par):
                pe.wait_ge(ohd, g + 1)
                for n in range(nd * GT):
                    if n >= 2:
                        pe.wait_ge(ccd, g * (nd * GT) + n - 1)
                    nc.tensor.matmul(psC[n % 2][:, 0:wc], oh[:, n // GT, n % GT, :],
                                     c.carry[:, (n // GT) * wc:(n // GT + 1) * wc], start=True, stop=True).then_inc(cm, 1)

            def step(g, par, ahead):
                pe.wait_ge(ccd, (g + 1) * (nd * GT))
                if ahead:
                    prepare(g + 1, 1 - par)
                if layer == 0:
                    pe.wait_ge(catd, g + 1)
                    for j in range(GT):
                        if j >= 2:
                            pe.wait_ge(tc, g * GT + j - 1)
                        for k in range(2):
                            last = nc.tensor.transpose(psT[j % 2][:, k * P:(k + 1) * P], num[:, j, k * P:(k + 1) * P], c.ident[:])
                        last.then_inc(tr, 1)
                    for j in range(GT):
                        pe.wait_ge(tc, g * GT + j + 1)
                        if j >= 2:
                            pe.wait_ge(fs, g * GT + j - 1)
                        for k in range(2):
                            last = nc.tensor.matmul(psF[j % 2][:, 0:D], cT[:, k, j * P:(j + 1) * P], wf[:, k, :],
                                                    start=(k == 0), stop=(k == 1))
                        last.then_inc(mm, 1)

            over_groups(pe, prepare, step)


def normalize_group(c, v, w, xln, g, vin, root, xr):
    layernorm_stats(c, v, w, lambda j: c.x[:, bass.ds((g * GT + j) * D, D)], GT, vin, root, g + 1)
    for j in range(GT):
        c.nc.vector.tensor_scalar(xln[:, j, 0:D], c.x[:, bass.ds((g * GT + j) * D, D)], w["mv"][:, j, 0:1],
                                  w["rstd"][:, j:j + 1], ALU.subtract, ALU.mult).then_inc(xr, 1)


def root_and_copies(c, act, w, g, vin, root, tr, tc, psT, xT):
    act.wait_ge(vin, g + 1)
    c.nc.scalar.activation(w["rstd"][:], w["rstd"][:], ACT.Sqrt).then_inc(root, 1)
    for j in range(GT):
        act.wait_ge(tr, g * GT + j + 1)
        c.nc.scalar.activation(xT[:, :, j * P:(j + 1) * P], psT[j % 2][:, 0:2 * P].rearrange("p (k n) -> p k n", k=2),
                               ACT.Copy).then_inc(tc, 1)


def transposes(c, pe, xln, g, xr, tr, tc, psT):
    for j in range(GT):
        pe.wait_ge(xr, g * GT + j + 1)
        if j >= 2:
            pe.wait_ge(tc, g * GT + j - 1)
        for k in range(2):
            last = c.nc.tensor.transpose(psT[j % 2][:, k * P:(k + 1) * P], xln[:, j, k * P:(k + 1) * P], c.ident[:])
        last.then_inc(tr, 1)


def experts(c):
    nc, A = c.nc, c.A
    HC = HID // P
    halves = ((0, 4), (4, 3))
    UNITS = 2 * EXP
    pairs = ((0, 1), (2, 3), (4, 5), (6,))
    STATS, SCALE, TURN, GATE, MASK, BIAS = 1, 3, 5, 9, 10, 11
    with ExitStack() as s:
        sb = lambda n, shape, dt=FP32: s.enter_context(nc.sbuf_tensor("m_" + n, shape, dt))
        sem = c.semaphores(s, "m_")
        pb = lambda n: s.enter_context(nc.psum_tensor("m_" + n, [P, 512], FP32))
        w1, w2 = sb("w1", [P, EXP, 2, HID]), sb("w2", [P, EXP, HC, D])
        wg, bg = sb("wg", [P, 2, EXP]), sb("bg", [P, EXP])
        b1, b2 = sb("b1", [P, EXP, HC]), sb("b2", [EXP, D])
        w = {"stats": sb("st", [P, GT, 6]), "mv": sb("mv", [P, GT, 2]), "rstd": sb("rs", [P, GT])}
        xln, xT = sb("xln", [P, GT, D]), sb("xT", [P, 2, 2, GT * P])
        hT = sb("hT", [P, 2, HC, 512])
        gate, rank, mask = sb("gate", [P, GT, EXP]), sb("rank", [P, GT, EXP]), sb("mask", [P, 2, GT, EXP])
        gt, eq = sb("gt", [P, GT, EXP, EXP]), sb("eq", [P, GT, EXP, EXP])
        lower = sb("lower", [P, EXP, EXP])
        maskT = sb("maskT", [EXP, GT * P])
        psM = [pb("psM0"), pb("psM1")]
        psH = [pb(f"psH{n}") for n in range(HC)]
        psY = [pb("psY0"), pb("psY1")]
        ld, lw, vin, root, xr, tr, tc, gd, md, mt_, mc, bt, ba, hp, gelud, yd, ya = (sem(n) for n in (
            "ld", "lw", "vin", "root", "xr", "tr", "tc", "gd", "md", "mt", "mc", "bt", "ba", "hp", "gelud", "yd", "ya"))
        ldw = sem("ldw")
        block = s.enter_context(nc.Block())

        def all_groups(eng, unit, step):
            def group(g, par, ahead):
                for u in range(UNITS):
                    unit(g, par, u)
                    if ahead and u:
                        step(g + 1, 1 - par, u)

            for n in range(1, UNITS):
                step(0, 0, n)
            with eng.Fori(0, NG // 2) as i:
                group(i * 2, 0, True)
                group(i * 2 + 1, 1, True)
            group(NG - 1, 0, False)

        @block.sync
        def _(sp):
            sp.dma_start(wg[:], A["L0_ffn_Wg"].rearrange("(k p) n -> p k n", p=P)).then_inc(ld, 16)
            sp.dma_start(bg[:], row_bcast(A["L0_ffn_bg"], 0, EXP)).then_inc(ld, 16)
            sp.dma_start(b2[:], A["L0_ffn_b2"]).then_inc(ld, 16)
            with nc.allow_non_contiguous_dma("biases one word per partition"):
                for e in range(EXP):
                    sp.dma_start(b1[:, e, :], A["L0_ffn_b1"][e, :].rearrange("(k p) -> p k", p=P)).then_inc(ld, 16)
            for e in range(EXP):
                sp.dma_start(w1[:, e, :, :], A["L0_ffn_W1"][e].rearrange("(k p) n -> p k n", p=P)).then_inc(ldw, 16)
                sp.dma_start(w2[:, e, :, :], A["L0_ffn_W2"][e].rearrange("(k p) n -> p k n", p=P)).then_inc(ldw, 16)
            sp.wait_ge(ld, 16 * (3 + EXP))
            sp.wait_ge(ldw, 32 * EXP)

        @block.gpsimd
        def _(pool):
            nc.gpsimd.memset(lower[:], 1.0)
            pool.drain()
            nc.gpsimd.affine_select(out=lower[:], in_=lower[:], compare_op=ALU.is_gt, fill=0.0, base=0,
                                    pattern=[[1, EXP], [-1, EXP]], channel_multiplier=0).then_inc(lw, 1)

        @block.vector
        def _(v):
            tt, ts = nc.vector.tensor_tensor, nc.vector.tensor_scalar
            v.wait_ge(lw, 1)
            v.wait_ge(ld, 16 * (3 + EXP))
            v.sem_inc(ya, 2)

            def step(g, par, n):
                if n == STATS:
                    for j in range(GT):
                        nc.vector.bn_stats(w["stats"][:, j, :], c.x[:, bass.ds((g * GT + j) * D, D)])
                    v.drain()
                    for j in range(GT):
                        nc.vector.bn_aggr(w["mv"][:, j, :], w["stats"][:, j, :])
                    v.drain()
                    ts(w["rstd"][:], w["mv"][:, :, 1], LN_EPS, None, ALU.add).then_inc(vin, 1)
                elif n == SCALE:
                    v.wait_ge(root, g + 1)
                    nc.vector.reciprocal(w["rstd"][:], w["rstd"][:])
                    v.drain()
                    for j in range(GT):
                        ts(xln[:, j, :], c.x[:, bass.ds((g * GT + j) * D, D)], w["mv"][:, j, 0:1],
                           w["rstd"][:, j:j + 1], ALU.subtract, ALU.mult).then_inc(xr, 1)
                elif n == GATE:
                    v.wait_ge(gd, g + 1)
                    tt(gate[:], psM[0][:, 0:GT * EXP].rearrange("p (i e) -> p i e", e=EXP),
                       bg[:].unsqueeze(1).to_broadcast([P, GT, EXP]), ALU.add)
                    v.drain()
                    gj = gate[:].unsqueeze(2).to_broadcast([P, GT, EXP, EXP])
                    gi = gate[:].unsqueeze(3).to_broadcast([P, GT, EXP, EXP])
                    tt(gt[:], gj, gi, ALU.is_gt)
                    tt(eq[:], gj, gi, ALU.is_equal)
                    v.drain()
                    tt(eq[:], eq[:], lower[:].unsqueeze(1).to_broadcast([P, GT, EXP, EXP]), ALU.mult)
                    v.drain()
                    tt(gt[:], gt[:], eq[:], ALU.add)
                    v.drain()
                    nc.vector.tensor_reduce(rank[:], gt[:], AX.X, ALU.add)
                    v.drain()
                    ts(mask[:, par], rank[:], 1.5, None, ALU.is_lt).then_inc(md, 1)
                elif BIAS <= n < BIAS + 4:
                    for j in pairs[n - BIAS]:
                        v.wait_ge(bt, g * GT + j + 1)
                        xj = c.x[:, bass.ds((g * GT + j) * D, D)]
                        tt(xj, psM[j % 2][:, 0:D], xj, ALU.add).then_inc(ba, 1)
                    v.drain()

            def unit(g, par, u):
                for u in {0: (), UNITS - 1: (u - 1, u)}.get(u, (u - 1,)):
                    t0, n = halves[u % 2]
                    for t in range(t0, t0 + n):
                        y = (u // 2) * GT + t
                        v.wait_ge(yd, g * (EXP * GT) + y + 1)
                        xj = c.x[:, bass.ds((g * GT + t) * D, D)]
                        nc.vector.scalar_tensor_tensor(out=xj, in0=psY[y % 2][:, 0:D], scalar=mask[:, par, t, u // 2:u // 2 + 1],
                                                       in1=xj, op0=ALU.mult, op1=ALU.add).then_inc(ya, 1)
                    v.drain()

            all_groups(v, unit, step)

        @block.scalar
        def _(act):
            act.wait_ge(ld, 16 * (3 + EXP))

            def step(g, par, n):
                if n == STATS + 1:
                    act.wait_ge(vin, g + 1)
                    nc.scalar.activation(w["rstd"][:], w["rstd"][:], ACT.Sqrt).then_inc(root, 1)
                elif TURN <= n < TURN + 4:
                    for j in pairs[n - TURN]:
                        act.wait_ge(tr, g * GT + j + 1)
                        nc.scalar.activation(xT[:, par, :, j * P:(j + 1) * P],
                                             psM[j % 2][:, 0:2 * P].rearrange("p (k n) -> p k n", k=2), ACT.Copy).then_inc(tc, 1)
                elif n == MASK:
                    for q, (t0, m) in enumerate(halves):
                        act.wait_ge(mt_, g * 2 + q + 1)
                        nc.scalar.activation(maskT[:, t0 * P:(t0 + m) * P], psM[q][0:EXP, 0:m * P], ACT.Copy).then_inc(mc, 1)

            def unit(g, par, u):
                n = halves[u % 2][1] * P
                for k in range(HC):
                    act.wait_ge(hp, (g * UNITS + u) * HC + k + 1)
                    nc.scalar.activation(hT[:, u % 2, k, 0:n], psH[k][:, 0:n], ACT.Gelu,
                                         bias=b1[:, u // 2, k:k + 1]).then_inc(gelud, 1)

            all_groups(act, unit, step)

        @block.tensor
        def _(pe):
            mm = nc.tensor.matmul
            pe.wait_ge(ld, 16 * (3 + EXP))
            pe.sem_inc(gelud, HC)

            def step(g, par, n):
                if TURN <= n < TURN + 4:
                    if n == TURN and not isinstance(g, int):
                        pe.wait_ge(ba, g * GT)
                    for j in pairs[n - TURN]:
                        pe.wait_ge(xr, g * GT + j + 1)
                        if j >= 2:
                            pe.wait_ge(tc, g * GT + j - 1)
                        for k in range(2):
                            last = nc.tensor.transpose(psM[j % 2][:, k * P:(k + 1) * P], xln[:, j, k * P:(k + 1) * P], c.ident[:])
                        last.then_inc(tr, 1)
                elif n == GATE:
                    pe.wait_ge(tc, (g + 1) * GT)
                    for j in range(GT):
                        for k in range(2):
                            last = mm(psM[0][:, j * EXP:(j + 1) * EXP], xT[:, par, k, j * P:(j + 1) * P], wg[:, k, :],
                                      start=(k == 0), stop=(k == 1))
                    last.then_inc(gd, 1)
                elif n == MASK:
                    pe.wait_ge(md, g + 1)
                    for q, (t0, m) in enumerate(halves):
                        for j in range(m):
                            last = nc.tensor.transpose(psM[q][0:EXP, j * P:(j + 1) * P], mask[:, par, t0 + j, :], c.ident[:])
                        last.then_inc(mt_, 1)
                elif BIAS <= n < BIAS + 4:
                    if isinstance(g, int):
                        pe.wait_ge(ldw, 32 * EXP)
                    pe.wait_ge(mc, g * 2 + 2)
                    for j in pairs[n - BIAS]:
                        if j >= 2:
                            pe.wait_ge(ba, g * GT + j - 1)
                        mm(psM[j % 2][:, 0:D], maskT[:, j * P:(j + 1) * P], b2[:], start=True, stop=True).then_inc(bt, 1)

            def hidden(g, par, u):
                t0, n = halves[u % 2]
                for k in range(HC):
                    pe.wait_ge(gelud, (g * UNITS + u) * HC + k + 1)
                    for q in range(2):
                        last = mm(psH[k][:, 0:n * P], w1[:, u // 2, q, k * P:(k + 1) * P],
                                  xT[:, par, q, t0 * P:(t0 + n) * P], start=(q == 0), stop=(q == 1))
                    last.then_inc(hp, 1)

            def output(g, u):
                t0, n = halves[u % 2]
                pe.wait_ge(gelud, (g * UNITS + u) * HC + 2 * HC)
                for t in range(t0, t0 + n):
                    y = (u // 2) * GT + t
                    pe.wait_ge(ya, g * (EXP * GT) + y + 1)
                    for k in range(HC):
                        last = mm(psY[y % 2][:, 0:D], hT[:, u % 2, k, (t - t0) * P:(t - t0 + 1) * P], w2[:, u // 2, k, :],
                                  start=(k == 0), stop=(k == HC - 1))
                    last.then_inc(yd, 1)

            def unit(g, par, u):
                hidden(g, par, u)
                if u:
                    output(g, u - 1)
                if u == UNITS - 1:
                    output(g, u)

            all_groups(pe, unit, step)


def layer1_tables(c):
    nc, A = c.nc, c.A
    with ExitStack() as s:
        sb = lambda n, shape, dt=FP32: s.enter_context(nc.sbuf_tensor("q_" + n, shape, dt))
        sem = c.semaphores(s, "q_")
        pb = lambda n: s.enter_context(nc.psum_tensor("q_" + n, [P, 512], FP32))
        wall, ball = sb("w", [P, 2, 4 * D]), sb("b", [P, 4 * D])
        w = {"stats": sb("st", [P, GT, 6]), "mv": sb("mv", [P, GT, 2]), "rstd": sb("rs", [P, GT])}
        xln, xT = sb("xln", [P, GT, D]), sb("xT", [P, 2, 2, GT * P])
        qrow, kvrow, srow = sb("qrow", [P, 2, GT, D]), sb("kvrow", [P, 2, GT, 2 * D]), sb("srow", [P, GT, D])
        psT = [pb("psT0"), pb("psT1")]
        psO = [[pb(f"psO{r}{n}") for n in range(2)] for r in range(2)]
        ld, vin, root, xr, tr, tc, mm, od, rows, st0, st1 = (sem(n) for n in (
            "ld", "vin", "root", "xr", "tr", "tc", "mm", "od", "rows", "st0", "st1"))
        st = [st0, st1]
        block = s.enter_context(nc.Block())

        @block.sync
        def _(sp):
            for n, (wn, bn) in enumerate((("Wq", "bq"), ("Wk", "bk"), ("Wv", "bv"), ("Ws", "bs"))):
                sp.dma_start(wall[:, :, n * D:(n + 1) * D], A["L1_gnn_" + wn].rearrange("(k p) n -> p k n", p=P)).then_inc(ld, 16)
                sp.dma_start(ball[:, n * D:(n + 1) * D], row_bcast(A["L1_gnn_" + bn], 0, D)).then_inc(ld, 16)
            sp.sem_inc(st0, 32)
            sp.sem_inc(st1, 32)

            def step(g, par, ahead):
                sp.wait_ge(rows, g + 1)
                sp.dma_start(c.q.rearrange("(p i) w -> p (i w)", i=NI)[:, bass.ds(g * (GT * D), GT * D)],
                             qrow[:, par]).then_inc(st[par], 16)
                sp.dma_start(c.kv.rearrange("(p i) w -> p (i w)", i=NI)[:, bass.ds(g * (2 * GT * D), 2 * GT * D)],
                             kvrow[:, par]).then_inc(st[par], 16)

            over_groups(sp, lambda g, par: None, step)
            sp.wait_ge(st0, 32 * (NG // 2 + 2))
            sp.wait_ge(st1, 32 * (NG // 2 + 1))

        @block.vector
        def _(v):
            tt = nc.vector.tensor_tensor
            v.wait_ge(ld, 128)

            def prepare(g, par):
                normalize_group(c, v, w, xln, g, vin, root, xr)

            def step(g, par, ahead):
                if ahead:
                    v.wait_ge(tr, (g + 1) * GT)
                    prepare(g + 1, 1 - par)
                v.wait_ge(st[par], turns(g, par, 32))
                for j in range(GT):
                    v.wait_ge(mm, g * GT + j + 1)
                    o = psO[j % 2]
                    tt(qrow[:, par, j, :], o[0][:, 0:D], ball[:, 0:D], ALU.add)
                    tt(kvrow[:, par, j, 0:D], o[0][:, D:2 * D], ball[:, D:2 * D], ALU.add)
                    tt(kvrow[:, par, j, D:2 * D], o[1][:, 0:D], ball[:, 2 * D:3 * D], ALU.add)
                    tt(srow[:, j, :], o[1][:, D:2 * D], ball[:, 3 * D:4 * D], ALU.add).then_inc(od, 1)
                v.drain()
                nc.vector.tensor_scalar(qrow[:, par], qrow[:, par], float(C) ** -0.5, None, ALU.mult).then_inc(rows, 1)
                xg = c.x[:, bass.ds(g * (GT * D), GT * D)]
                tt(xg, xg, srow[:].rearrange("p i d -> p (i d)"), ALU.add)
                v.drain()

            over_groups(v, prepare, step)

        @block.scalar
        def _(act):
            def root_of(g, par):
                act.wait_ge(vin, g + 1)
                nc.scalar.activation(w["rstd"][:], w["rstd"][:], ACT.Sqrt).then_inc(root, 1)
                for j in range(GT):
                    act.wait_ge(tr, g * GT + j + 1)
                    nc.scalar.activation(xT[:, par, :, j * P:(j + 1) * P],
                                         psT[j % 2][:, 0:2 * P].rearrange("p (k n) -> p k n", k=2), ACT.Copy).then_inc(tc, 1)

            over_groups(act, root_of, lambda g, par, ahead: root_of(g + 1, 1 - par) if ahead else None)

        @block.tensor
        def _(pe):
            pe.wait_ge(ld, 128)

            def turn(g, j):
                pe.wait_ge(xr, g * GT + j + 1)
                if j >= 2:
                    pe.wait_ge(tc, g * GT + j - 1)
                for k in range(2):
                    last = nc.tensor.transpose(psT[j % 2][:, k * P:(k + 1) * P], xln[:, j, k * P:(k + 1) * P], c.ident[:])
                last.then_inc(tr, 1)

            def prepare(g, par):
                for j in range(GT):
                    turn(g, j)

            def step(g, par, ahead):
                pe.wait_ge(tc, (g + 1) * GT)
                for j in range(GT):
                    pe.wait_ge(od, g * GT + j + (1 if j else 2))
                    for n in range(2):
                        for k in range(2):
                            last = nc.tensor.matmul(psO[j % 2][n][:, :], xT[:, par, k, j * P:(j + 1) * P],
                                                    wall[:, k, n * 512:(n + 1) * 512], start=(k == 0), stop=(k == 1))
                    last.then_inc(mm, 1)
                    if ahead and j:
                        turn(g + 1, j - 1)
                if ahead:
                    turn(g + 1, GT - 1)

            pe.sem_inc(od, 2)
            over_groups(pe, prepare, step)


def reload_edges(c):
    nc = c.nc
    with ExitStack() as s:
        rl = s.enter_context(nc.semaphore("r_ld"))
        block = s.enter_context(nc.Block())

        @block.sync
        def _(sp):
            sp.dma_start(c.rec[:, 0, :, :], c.rec_d.rearrange("(p t) w -> p t w", p=P)).then_inc(rl, 16)
            sp.wait_ge(rl, 16)

        @block.vector
        def _(v):
            v.wait_ge(rl, 16)
            k = c.rec[:, 0, :, 0]
            nc.vector.memset(c.sep[:, 0, 0:1], 0.0)
            nc.vector.tensor_tensor(c.sep[:, 0, 1:T], k[:, 1:T], k[:, 0:T - 1], ALU.is_equal)
            v.drain()
            nc.vector.tensor_scalar(c.sep[:], c.sep[:], 1.0, BIG, ALU.subtract, ALU.mult)
            v.drain()


SH, SG, SC = 8, 64, 64
SQ = SH * SG // P


def slice_attention(c):
    nc, A = c.nc, c.A
    ones = D
    XW = D + 1
    with ExitStack() as s:
        sb = lambda n, shape, dt=FP32: s.enter_context(nc.sbuf_tensor("f_" + n, shape, dt))
        sem = c.semaphores(s, "f_")
        wx, wfx = sb("wx", [P, 2, 512]), sb("wfx", [P, 2, 512])
        wsl, wqkv = sb("wsl", [SC, SG]), sb("wqkv", [SC, 3, SC])
        wout = sb("wout", [SC, SH, D])
        bx = sb("bx", [SC, SH])
        bsl, bfx, bout, temp = sb("bsl", [P, SG]), sb("bfx", [SG, 512]), sb("bout", [P, D]), sb("temp", [P, SH])
        wxT = sb("wxT", [SC, SH, 2, P])
        wc, bc = sb("wc", [P, 2, 512]), sb("bc", [P, 512])
        with ExitStack() as s1:
            psA = [s1.enter_context(nc.psum_tensor(f"f1_psA{n}", [P, 512], FP32)) for n in range(4)]
            psW = [s1.enter_context(nc.psum_tensor(f"f1_psW{n}", [P, 512], FP32)) for n in range(2)]
            psB = s1.enter_context(nc.psum_tensor("f1_psB", [P, 512], FP32))
            ld, t1, t1c, w1 = (sem(n) for n in ("ld", "t1", "t1c", "w1"))
            block = s1.enter_context(nc.Block())

            @block.sync
            def _(sp):
                f = "L1_ffn_"
                sp.dma_start(wx[:], A[f + "W_x"].rearrange("(k p) n -> p k n", p=P)).then_inc(ld, 16)
                sp.dma_start(wfx[:], A[f + "W_fx"].rearrange("(k p) n -> p k n", p=P)).then_inc(ld, 16)
                sp.dma_start(wsl[:], A[f + "W_slice"]).then_inc(ld, 16)
                for n, name in enumerate(("W_q", "W_k", "W_v")):
                    sp.dma_start(wqkv[:, n, :], A[f + name]).then_inc(ld, 16)
                sp.dma_start(wout[:], A[f + "W_out"].rearrange("(h c) n -> c h n", c=SC)).then_inc(ld, 16)
                with nc.allow_non_contiguous_dma("biases one word per partition"):
                    sp.dma_start(bx[:], A[f + "b_x"].rearrange("(h c) -> c h", c=SC)).then_inc(ld, 16)
                sp.dma_start(bsl[:], row_bcast(A[f + "b_slice"], 0, SG)).then_inc(ld, 16)
                sp.dma_start(bfx[:], A[f + "b_fx"].rearrange("(a n) -> a n", a=1).to_broadcast([SG, 512])).then_inc(ld, 16)
                sp.dma_start(bout[:], row_bcast(A[f + "b_out"], 0, D)).then_inc(ld, 16)
                sp.dma_start(temp[:], A[f + "temperature"].rearrange("a h b c -> a (h b c)").to_broadcast([P, SH])).then_inc(ld, 16)
                sp.wait_ge(ld, 192)

            @block.tensor
            def _(pe):
                pe.wait_ge(ld, 192)
                for h in range(SH):
                    for k in range(2):
                        o = ((h % 2) * 2 + k) * P
                        last = nc.tensor.transpose(psA[h // 2][0:SC, o:o + P], wx[:, k, h * SC:(h + 1) * SC], c.ident[:])
                last.then_inc(t1, 1)
                pe.wait_ge(t1c, 1)
                for h in range(SH):
                    for k in range(2):
                        nc.tensor.matmul(psW[k][:, h * SG:(h + 1) * SG], wxT[:, h, k, :], wsl[:], start=True, stop=True)
                    last = nc.tensor.matmul(psB[:, h * SG:(h + 1) * SG], bx[:, h:h + 1].to_broadcast([SC, P]), wsl[:],
                                            start=True, stop=True)
                last.then_inc(w1, 1)

            @block.scalar
            def _(act):
                act.wait_ge(t1, 1)
                for q in range(4):
                    last = nc.scalar.activation(wxT[:, 2 * q:2 * q + 2, :, :].rearrange("p a b c -> p (a b c)"),
                                                psA[q][0:SC, :], ACT.Copy)
                last.then_inc(t1c, 1)

            @block.vector
            def _(v):
                tt, ts = nc.vector.tensor_tensor, nc.vector.tensor_scalar
                v.wait_ge(ld, 192)
                ts(temp[:], temp[:], 0.1, 5.0, ALU.max, ALU.min)
                v.drain()
                nc.vector.reciprocal(temp[:], temp[:])
                v.wait_ge(w1, 1)
                v.drain()
                hg = lambda a: a.rearrange("p (h g) -> p h g", g=SG)
                it = temp[:].unsqueeze(2).to_broadcast([P, SH, SG])
                for k in range(2):
                    tt(hg(wc[:, k, :]), hg(psW[k][:, :]), it, ALU.mult)
                tt(hg(bc[:]), hg(psB[:, :]), bsl[:].unsqueeze(1).to_broadcast([P, SH, SG]), ALU.add)
                v.drain()
                tt(hg(bc[:]), hg(bc[:]), it, ALU.mult)
                v.drain()

        w = {"stats": sb("st", [P, GT, 6]), "mv": sb("mv", [P, GT, 2]), "rstd": sb("rs", [P, GT])}
        xln, xT = sb("xln", [P, 2, GT, XW]), sb("xT", [P, 2, GT * P])
        real = sb("real", [P, NI])
        sums = sb("sums", [P, SQ, XW])
        with ExitStack() as s2:
            sb2 = lambda n, shape, dt=FP32: s2.enter_context(nc.sbuf_tensor("f2_" + n, shape, dt))
            wt = sb2("wt", [P, 2, GT, 512])
            wtT = sb2("wtT", [P, 2, SQ, GT * P])
            mx, dn = sb2("mx", [P, GT, SH]), sb2("dn", [P, GT, SH])
            pb2 = lambda n: s2.enter_context(nc.psum_tensor("f2_" + n, [P, 512], FP32))
            psT = [pb2("psT0"), pb2("psT1")]
            psL = [pb2("psL0"), pb2("psL1")]
            psS = [pb2(f"psS{q}") for q in range(SQ)]
            ri, one, vin, root, xr, tr, tc, lg, lgd, ex, exd, wd, wr, wrc, acc, st, sd = (sem("2" + n) for n in (
                "ri", "one", "vin", "root", "xr", "tr", "tc", "lg", "lgd", "ex", "exd", "wd", "wr", "wrc", "acc", "st", "sd"))
            st = [st, sem("2st1")]
            block = s2.enter_context(nc.Block())
            flat = lambda a: a.rearrange("p i n -> p (i n)")

            @block.sync
            def _(sp):
                sp.sem_inc(st[0], 16)
                sp.sem_inc(st[1], 16)

                def step(g, par, ahead):
                    sp.wait_ge(wrc, (g + 1) * GT)
                    sp.dma_start(c.wT[:, bass.ds(g * (SQ * GT * P), SQ * GT * P)], wtT[:, par]).then_inc(st[par], 16)

                over_groups(sp, lambda g, par: None, step)
                sp.wait_ge(st[0], 16 * (NG // 2 + 2))
                sp.wait_ge(st[1], 16 * (NG // 2 + 1))

            @block.gpsimd
            def _(pool):
                nc.gpsimd.iota(real[:], [[1, NI]], base=0, channel_multiplier=NI,
                               allow_small_or_imprecise_dtypes=True).then_inc(ri, 1)

            @block.vector
            def _(v):
                tt, ts = nc.vector.tensor_tensor, nc.vector.tensor_scalar
                nc.vector.memset(xln[:, :, :, ones:XW], 1.0).then_inc(one, 1)
                v.wait_ge(ri, 1)
                ts(real[:], real[:], N - 0.5, None, ALU.is_lt)
                v.drain()
                hg = lambda a: a.rearrange("p i (h g) -> p (i h) g", g=SG)
                ih = lambda a: a.rearrange("p i h -> p (i h)").unsqueeze(2).to_broadcast([P, GT * SH, SG])

                def logits(g, par):
                    for j in range(GT):
                        v.wait_ge(lg, g * GT + j + 1)
                        tt(wt[:, par, j, :], psL[j % 2][:, :], bc[:], ALU.add).then_inc(lgd, 1)
                    v.drain()
                    nc.vector.tensor_reduce(mx[:], wt[:, par].rearrange("p i (h g) -> p i h g", g=SG), AX.X, ALU.max)
                    v.drain()
                    tt(hg(wt[:, par]), hg(wt[:, par]), ih(mx[:]), ALU.subtract).then_inc(ex, 1)

                def prepare(g, par):
                    normalize_group(c, v, w, xln[:, par], g, vin, root, xr)
                    logits(g, par)

                def step(g, par, ahead):
                    if ahead:
                        v.wait_ge(acc, g + 1)
                        normalize_group(c, v, w, xln[:, 1 - par], g + 1, vin, root, xr)
                    v.wait_ge(exd, g + 1)
                    nc.vector.tensor_reduce(dn[:], wt[:, par].rearrange("p i (h g) -> p i h g", g=SG), AX.X, ALU.add)
                    v.drain()
                    nc.vector.reciprocal(dn[:], dn[:])
                    v.drain()
                    tt(dn[:], dn[:], real[:, bass.ds(g * GT, GT)].unsqueeze(2).to_broadcast([P, GT, SH]), ALU.mult)
                    v.drain()
                    tt(hg(wt[:, par]), hg(wt[:, par]), ih(dn[:]), ALU.mult).then_inc(wd, 1)
                    if ahead:
                        logits(g + 1, 1 - par)

                over_groups(v, prepare, step)
                v.wait_ge(sd, 1)
                for q in range(SQ):
                    nc.vector.tensor_copy(sums[:, q, :], psS[q][:, 0:XW])
                v.drain()

            @block.scalar
            def _(act):
                def exps(g, par):
                    act.wait_ge(ex, g + 1)
                    nc.scalar.activation(flat(wt[:, par]), flat(wt[:, par]), ACT.Exp).then_inc(exd, 1)

                def prepare(g, par):
                    root_and_copies(c, act, w, g, vin, root, tr, tc, psT, xT)
                    exps(g, par)

                def step(g, par, ahead):
                    if ahead:
                        root_and_copies(c, act, w, g + 1, vin, root, tr, tc, psT, xT)
                    act.wait_ge(st[par], turns(g, par, 16))
                    for j in range(GT):
                        act.wait_ge(wr, g * GT + j + 1)
                        nc.scalar.activation(wtT[:, par, :, j * P:(j + 1) * P],
                                             psT[j % 2][:, :].rearrange("p (q n) -> p q n", q=SQ), ACT.Copy).then_inc(wrc, 1)
                    if ahead:
                        exps(g + 1, 1 - par)

                over_groups(act, prepare, step)

            @block.tensor
            def _(pe):
                mm = nc.tensor.matmul
                for q in range(SQ):
                    mm(psS[q][:, 0:XW], c.zrow[:, 0:P], c.zrow[:, 0:XW], start=True, stop=False)
                pe.wait_ge(one, 1)
                pe.sem_inc(acc, 1)
                pe.sem_inc(lgd, 2)

                def prepare(g, par):
                    transposes(c, pe, xln[:, par], g, xr, tr, tc, psT)
                    for j in range(GT):
                        pe.wait_ge(tc, g * GT + j + 1)
                        pe.wait_ge(lgd, g * GT + j + (1 if j else 2))
                        for k in range(2):
                            last = mm(psL[j % 2][:, :], xT[:, k, j * P:(j + 1) * P], wc[:, k, :], start=(k == 0), stop=(k == 1))
                        last.then_inc(lg, 1)

                def step(g, par, ahead):
                    if ahead:
                        prepare(g + 1, 1 - par)
                    pe.wait_ge(wd, g + 1)
                    for j in range(GT):
                        if j >= 2:
                            pe.wait_ge(wrc, g * GT + j - 1)
                        for q in range(SQ):
                            last = nc.tensor.transpose(psT[j % 2][:, q * P:(q + 1) * P], wt[:, par, j, q * P:(q + 1) * P], c.ident[:])
                        last.then_inc(wr, 1)
                        for q in range(SQ):
                            last = mm(psS[q][:, 0:XW], wt[:, par, j, q * P:(q + 1) * P], xln[:, par, j, :], start=False, stop=False)
                    last.then_inc(acc, 1)
                    pe.wait_ge(wrc, (g + 1) * GT)

                over_groups(pe, prepare, step)
                for q in range(SQ):
                    last = mm(psS[q][:, 0:XW], c.zrow[:, 0:P], c.zrow[:, 0:XW], start=False, stop=True)
                last.then_inc(sd, 1)

        ow = sb("ow", [P, SQ, D])
        with ExitStack() as s3:
            sb3 = lambda n, shape, dt=FP32: s3.enter_context(nc.sbuf_tensor("f3_" + n, shape, dt))
            pb3 = lambda n: s3.enter_context(nc.psum_tensor("f3_" + n, [P, 512], FP32))
            sh = sb3("sh", [SG, SH, XW])
            shT = sb3("shT", [P, 2, SH, SG])
            rn, nm = sb3("rn", [SG, SH]), sb3("nm", [SG, SH])
            tok, bt = sb3("tok", [SG, SH, SC]), sb3("bt", [SG, SH, SC])
            tokT, qT, kT = sb3("tokT", [SC, SH, SG]), sb3("qT", [SC, SH, SG]), sb3("kT", [SC, SH, SG])
            vv = sb3("vv", [SG, SH, SC])
            at, atT = sb3("at", [SG, SH, SG]), sb3("atT", [SG, SH, SG])
            mx, dn = sb3("mx", [SG, SH]), sb3("dn", [SG, SH])
            oT = sb3("oT", [SC, SH, SG])
            owh = sb3("owh", [SG, SH, D])
            ps = [pb3(f"ps{n}") for n in range(8)]
            mv, step, back, fin = (sem("3" + n) for n in ("mv", "step", "back", "fin"))
            block = s3.enter_context(nc.Block())
            f3 = lambda a: a.rearrange("p h g -> p (h g)")

            @block.sync
            def _(sp):
                for half in range(2):
                    sp.dma_start(sh[:].rearrange("g (q b) w -> g q b w", b=2)[:, :, half, :],
                                 sums[half * SG:(half + 1) * SG, :, :]).then_inc(mv, 16)
                sp.wait_ge(mv, 32)
                sp.wait_ge(back, 9)
                for half in range(2):
                    sp.dma_start(ow[half * SG:(half + 1) * SG, :, :],
                                 owh[:].rearrange("g (q b) w -> g q b w", b=2)[:, :, half, :]).then_inc(fin, 16)
                sp.wait_ge(fin, 32)

            @block.tensor
            def _(pe):
                mm, turn = nc.tensor.matmul, nc.tensor.transpose
                pe.wait_ge(mv, 32)
                for k in range(2):
                    for h in range(SH):
                        last = turn(ps[k][:, h * SG:(h + 1) * SG], sh[:, h, k * P:(k + 1) * P], c.ident[0:SG, 0:SG])
                last.then_inc(step, 1)
                pe.wait_ge(back, 1)
                for h in range(SH):
                    for k in range(2):
                        last = mm(ps[2][0:SG, h * SC:(h + 1) * SC], shT[:, k, h, :], wfx[:, k, h * SC:(h + 1) * SC],
                                  start=(k == 0), stop=(k == 1))
                last.then_inc(step, 1)
                pe.wait_ge(back, 2)
                for h in range(SH):
                    last = turn(ps[3][0:SC, h * SG:(h + 1) * SG], tok[:, h, :], c.ident[0:SG, 0:SG])
                last.then_inc(step, 1)
                pe.wait_ge(back, 3)
                mm(ps[4][0:SC, :], wqkv[:, 0, :], f3(tokT[:]), start=True, stop=True)
                mm(ps[5][0:SC, :], wqkv[:, 1, :], f3(tokT[:]), start=True, stop=True)
                for h in range(SH):
                    last = mm(ps[6][0:SG, h * SC:(h + 1) * SC], tokT[:, h, :], wqkv[:, 2, :], start=True, stop=True)
                last.then_inc(step, 1)
                pe.wait_ge(back, 4)
                for h in range(SH):
                    last = mm(ps[7][0:SG, h * SG:(h + 1) * SG], qT[:, h, :], kT[:, h, :], start=True, stop=True)
                last.then_inc(step, 1)
                pe.wait_ge(back, 6)
                for h in range(SH):
                    last = turn(ps[0][0:SG, h * SG:(h + 1) * SG], at[:, h, :], c.ident[0:SG, 0:SG])
                last.then_inc(step, 1)
                pe.wait_ge(back, 7)
                for h in range(SH):
                    last = mm(ps[1][0:SC, h * SG:(h + 1) * SG], vv[:, h, :], atT[:, h, :], start=True, stop=True)
                last.then_inc(step, 1)
                pe.wait_ge(back, 8)
                for h in range(SH):
                    last = mm(ps[2 + h // 2][0:SG, (h % 2) * D:(h % 2 + 1) * D], oT[:, h, :], wout[:, h, :], start=True, stop=True)
                last.then_inc(step, 1)

            @block.scalar
            def _(act):
                act.wait_ge(back, 5)
                nc.scalar.activation(f3(at[:]), f3(at[:]), ACT.Exp).then_inc(mv, 1)

            @block.vector
            def _(v):
                tt, ts, copy = nc.vector.tensor_tensor, nc.vector.tensor_scalar, nc.vector.tensor_copy
                hsc = lambda a: a.unsqueeze(2).to_broadcast([SG, SH, SC])
                h3 = lambda a: a.rearrange("p (h g) -> p h g", h=SH)
                v.wait_ge(step, 1)
                copy(shT[:, 0, :, :], h3(ps[0][:, :]))
                copy(shT[:, 1, :, :], h3(ps[1][:, :])).then_inc(back, 1)
                copy(nm[:], sh[:, :, ones])
                ts(rn[:], sh[:, :, ones], 1e-5, None, ALU.add)
                v.drain()
                nc.vector.reciprocal(rn[:], rn[:])
                tt(bt[:], h3(bfx[:]), hsc(nm[:]), ALU.mult)
                v.wait_ge(step, 2)
                v.drain()
                tt(tok[:], h3(ps[2][0:SG, :]), bt[:], ALU.add)
                v.drain()
                tt(tok[:], tok[:], hsc(rn[:]), ALU.mult).then_inc(back, 1)
                v.wait_ge(step, 3)
                copy(f3(tokT[:]), ps[3][0:SC, :]).then_inc(back, 1)
                v.wait_ge(step, 4)
                ts(f3(qT[:]), ps[4][0:SC, :], float(SC) ** -0.5, None, ALU.mult)
                copy(f3(kT[:]), ps[5][0:SC, :])
                copy(f3(vv[:]), ps[6][0:SG, :]).then_inc(back, 1)
                v.wait_ge(step, 5)
                nc.vector.tensor_reduce(mx[:], h3(ps[7][0:SG, :]), AX.X, ALU.max)
                v.drain()
                tt(at[:], h3(ps[7][0:SG, :]), hsc(mx[:]), ALU.subtract).then_inc(back, 1)
                v.wait_ge(mv, 33)
                nc.vector.tensor_reduce(dn[:], at[:], AX.X, ALU.add)
                v.drain()
                nc.vector.reciprocal(dn[:], dn[:])
                v.drain()
                tt(at[:], at[:], hsc(dn[:]), ALU.mult).then_inc(back, 1)
                v.wait_ge(step, 6)
                copy(f3(atT[:]), ps[0][0:SG, :]).then_inc(back, 1)
                v.wait_ge(step, 7)
                copy(f3(oT[:]), ps[1][0:SC, :]).then_inc(back, 1)
                v.wait_ge(step, 8)
                for q in range(SQ):
                    last = copy(owh[:, 2 * q:2 * q + 2, :].rearrange("p h d -> p (h d)"), ps[2 + q][0:SG, :])
                last.then_inc(back, 1)
                v.drain()

        with ExitStack() as s4:
            wtT = s4.enter_context(nc.sbuf_tensor("f4_wtT", [P, 2, SQ, GT * P], FP32))
            psO = [s4.enter_context(nc.psum_tensor(f"f4_psO{n}", [P, 512], FP32)) for n in range(GT)]
            lw0, lw1, mmd, od, so = (sem("4" + n) for n in ("lw0", "lw1", "mm", "od", "so"))
            lw = [lw0, lw1]
            block = s4.enter_context(nc.Block())

            @block.sync
            def _(sp):
                full = (P - 1) * NI
                rows = c.out[0:full, :].rearrange("(p i) d -> p (i d)", i=NI)

                def load(g):
                    if g >= 2:
                        sp.wait_ge(mmd, (g - 1) * GT)
                    sp.dma_start(wtT[:, g % 2, :, :], c.wT[:, g * SQ * GT * P:(g + 1) * SQ * GT * P]).then_inc(lw[g % 2], 16)

                load(0)
                load(1)
                stores = 0
                for g in range(NG):
                    sp.wait_ge(od, (g + 1) * GT)
                    cols = slice(g * GT * D, (g + 1) * GT * D)
                    for p0, p1 in slices_of(0, P - 1):
                        sp.dma_start(rows[p0:p1, cols], c.x[p0:p1, cols]).then_inc(so, 16)
                        stores += 1
                    n = min(GT, N - full - g * GT)
                    if n > 0:
                        sp.dma_start(c.out[full + g * GT:full + g * GT + n, :].rearrange("(p i) d -> p (i d)", p=1),
                                     c.x[P - 1:P, g * GT * D:(g * GT + n) * D]).then_inc(so, 16)
                        stores += 1
                    if g + 2 < NG:
                        load(g + 2)
                sp.wait_ge(so, 16 * stores)

            @block.tensor
            def _(pe):
                for g in range(NG):
                    pe.wait_ge(lw[g % 2], 16 * (g // 2 + 1))
                    for j in range(GT):
                        t = g * GT + j
                        if g:
                            pe.wait_ge(od, t - GT + 1)
                        for q in range(SQ):
                            last = nc.tensor.matmul(psO[j][:, 0:D], wtT[:, g % 2, q, j * P:(j + 1) * P], ow[:, q, :],
                                                    start=(q == 0), stop=(q == SQ - 1))
                        last.then_inc(mmd, 1)

            @block.vector
            def _(v):
                tt = nc.vector.tensor_tensor
                for g in range(NG):
                    xg = c.x[:, g * GT * D:(g + 1) * GT * D].rearrange("p (i d) -> p i d", d=D)
                    tt(xg, xg, bout[:].unsqueeze(1).to_broadcast([P, GT, D]), ALU.add)
                    v.drain()
                    for j in range(GT):
                        v.wait_ge(mmd, g * GT + j + 1)
                        xj = c.x[:, (g * GT + j) * D:(g * GT + j + 1) * D]
                        tt(xj, psO[j][:, 0:D], xj, ALU.add).then_inc(od, 1)


def build(nc, A, out):
    c = Chip()
    c.nc, c.A, c.out = nc, A, out
    dram = lambda n, shape, dt=FP32: nc.dram_tensor(n, shape, dt).ap()
    c.t1, c.t2 = dram("t1", (NI * P, TW)), dram("t2", (NI * P, TW))
    c.rec_d, c.rec_s = dram("rec_d", (EP, 4), I32), dram("rec_s", (EP, 4), I32)
    c.ends = [[dram(f"{w}_{k}", (KEYS,), I32) for w in ("start", "end")] for k in ("d", "s")]
    c.st_f, c.st_b = dram("st_f", (EP + KEYS, 4)), dram("st_b", (EP + KEYS, 4))
    c.state = [dram("state0", (EP + 1, SW)), dram("state1", (EP + 1, SW))]
    c.ea_sorted = dram("ea_sorted", (EP, D))
    c.ea_tail = dram("ea_tail", (16 * T, D))
    c.wT = dram("wT", (P, SQ * NI * P))
    c.kv, c.q = dram("kv", (NI * P, 512)), dram("q", (NI * P, D))
    with ExitStack() as s:
        sb = lambda n, shape, dt=FP32: s.enter_context(nc.sbuf_tensor(n, shape, dt))
        c.x = sb("x", [P, NI * D])
        c.ident, c.tri, c.triT, c.cols = (sb(n, [P, P]) for n in ("ident", "tri", "triT", "cols"))
        c.identb, c.colsb = sb("identb", [P, P], BF16), sb("colsb", [P, P], BF16)
        c.zrow, c.one = sb("zrow", [P, 2 * D]), sb("one", [P, 1])
        c.tail = sb("tail", [P, SW])
        c.carry, c.fkey = sb("carry", [P, 2 * 137]), sb("fkey", [P, 2])
        c.flag = sb("flag", [P, 1], I32)
        c.placed = s.enter_context(nc.semaphore("placed"))
        constants(c)
        layer0_tables(c)
        sort_edges(c)
        edges = s.enter_context(ExitStack())
        se = lambda n, shape, dt=FP32: edges.enter_context(nc.sbuf_tensor(n, shape, dt))
        c.rec, c.sep, c.ar = se("rec", [P, 2, T, 4], I32), se("sep", [P, 2, T]), se("ar", [P, T, 8])
        targets_logits(c)
        edge_pass(c, 0)
        join_tails(c, 0)
        edges.close()
        combine(c, 0)
        experts(c)
        layer1_tables(c)
        edges = s.enter_context(ExitStack())
        se = lambda n, shape, dt=FP32: edges.enter_context(nc.sbuf_tensor(n, shape, dt))
        c.rec, c.sep = se("rec1", [P, 1, T, 4], I32), se("sep1", [P, 1, T])
        reload_edges(c)
        order_attributes(c)
        edge_pass(c, 1)
        join_tails(c, 1)
        edges.close()
        combine(c, 1)
        slice_attention(c)


_INS = [
    'x', 'src', 'dst', 'edge_attr_256', 'L0_gnn_W_f',
    'L0_gnn_a_src_f', 'L0_gnn_a_dst_f', 'L0_gnn_b_f', 'L0_gnn_W_b', 'L0_gnn_a_src_b',
    'L0_gnn_a_dst_b', 'L0_gnn_b_b', 'L0_gnn_W_fuse', 'L0_gnn_b_fuse', 'L0_gnn_gamma',
    'L0_gnn_beta', 'L0_gnn_run_mean', 'L0_gnn_run_var', 'L0_ffn_Wg', 'L0_ffn_bg',
    'L0_ffn_W1', 'L0_ffn_b1', 'L0_ffn_W2', 'L0_ffn_b2', 'L1_gnn_Wq',
    'L1_gnn_bq', 'L1_gnn_Wk', 'L1_gnn_bk', 'L1_gnn_Wv', 'L1_gnn_bv',
    'L1_gnn_We', 'L1_gnn_Ws', 'L1_gnn_bs', 'L1_ffn_W_fx', 'L1_ffn_b_fx',
    'L1_ffn_W_x', 'L1_ffn_b_x', 'L1_ffn_W_slice', 'L1_ffn_b_slice', 'L1_ffn_W_q',
    'L1_ffn_W_k', 'L1_ffn_W_v', 'L1_ffn_W_out', 'L1_ffn_b_out', 'L1_ffn_temperature']


def kernel(**inputs):
    import numpy as _np
    import concourse.bacc as _bacc
    from concourse import mybir as _mybir
    from concourse.bass_utils import run_bass_kernel_spmd as _run

    nc = _bacc.Bacc("TRN2", target_bir_lowering=False, num_devices=1)
    arrays, args = {}, {}
    for name in _INS:
        a = _np.ascontiguousarray(inputs[name])
        arrays[f"in_{name}"] = a
        args[name] = nc.dram_tensor(f"in_{name}", a.shape, _mybir.dt.from_np(a.dtype), kind="ExternalInput").ap()
    out = nc.dram_tensor("out_x", (6250, 256), _mybir.dt.float32, kind="ExternalOutput").ap()
    build(nc, args, out)
    r = _run(nc, [arrays], core_ids=[0])
    return r.results[0]["out_x"]
```
